# Optimizing a Trainium2 kernel written in Bass

```python
import numpy as np
import jax
import jax.numpy as jnp

def _softmax(x, axis=-1):
    return jax.nn.softmax(x, axis=axis)

def _gelu(x):
    return jax.nn.gelu(x, approximate=True)

def _silu(x):
    return jax.nn.silu(x)

def _sigmoid(x):
    return jax.nn.sigmoid(x)

def _layernorm(x, axis=-1, eps=1e-05):
    m = jnp.mean(x, axis=axis, keepdims=True)
    v = jnp.var(x, axis=axis, keepdims=True)
    return (x - m) / jnp.sqrt(v + eps)

def _scatter_add(tgt, idx, src, axis=0):
    return tgt.at[idx].add(src)

def _segment_sum(src, seg, n):
    return jax.ops.segment_sum(src, seg, n)
kernel_name = 'mk_xattn_ffn_d4_seqx_r8_3d54bd'

def setup_inputs(seed: int=0):
    np.random.seed(seed)
    _w = jnp.asarray

    def _rec_inputs():
        import jax
        import jax.numpy as jnp
        _rk = jax.random.key(seed)
        x = 7.22e-05 + 1 * jax.random.normal(jax.random.fold_in(_rk, 1), (4, 256, 128), jnp.float32)
        _lenS = 256 - jax.random.randint(jax.random.fold_in(_rk, 7), (4,), 0, max(1, 256 // 4) + 1, jnp.int32)
        _lenS2 = 512 - jax.random.randint(jax.random.fold_in(_rk, 8), (4,), 0, max(1, 512 // 4) + 1, jnp.int32)
        _ctx_1024P = jax.random.normal(jax.random.fold_in(_rk, 11), (4, 16, 128), jnp.float32)
        _ctx_1024c = jax.random.dirichlet(jax.random.fold_in(_rk, 511), 0.3 * jnp.ones((16,), jnp.float32), (4, 512))
        _ctx_1024t = jnp.einsum('bsk,bkd->bsd', _ctx_1024c, _ctx_1024P)
        _ctx_1024t = _ctx_1024t * jax.lax.rsqrt(jnp.mean(jnp.square(_ctx_1024t)) + 1e-12) * 0.953939
        ctx_1024 = 4.13588e-05 + 0.999923 * (_ctx_1024t + 0.3 * jax.random.normal(jax.random.fold_in(_rk, 611), (4, 512, 128), jnp.float32))
        _validS = jnp.arange(256)[None, :] < _lenS[:, None]
        _validS2 = jnp.arange(512)[None, :] < _lenS2[:, None]
        _causal = jnp.tril(jnp.ones((256, 256), dtype=bool))
        mask_BxS2_bf0 = jnp.logical_not(jnp.ones((4, 512), dtype=bool))
        return (x, ctx_1024, mask_BxS2_bf0)
    x, ctx_1024, mask_BxS2_bf0 = _rec_inputs()

    def _L0_xattn_setup():
        import jax, jax.numpy as jnp
        import numpy as np
        B, L, D_MODEL, H, DK, DV = (4, 256, 128, 16, 64, 64)
        key = jax.random.key(seed)
        ks = jax.random.split(key, 11)
        s = 1.0 / np.sqrt(D_MODEL)
        return {'queries': jax.random.normal(ks[0], (B, L, D_MODEL), jnp.float32), 'keys': jax.random.normal(ks[1], (B, L, D_MODEL), jnp.float32), 'values': jax.random.normal(ks[2], (B, L, D_MODEL), jnp.float32), 'Wq': jax.random.normal(ks[3], (D_MODEL, H * DK), jnp.float32) * s, 'bq': jnp.zeros((H * DK,), jnp.float32), 'Wk': jax.random.normal(ks[4], (D_MODEL, H * DK), jnp.float32) * s, 'bk': jnp.zeros((H * DK,), jnp.float32), 'Wv': jax.random.normal(ks[5], (D_MODEL, H * DV), jnp.float32) * s, 'bv': jnp.zeros((H * DV,), jnp.float32), 'Wo': jax.random.normal(ks[6], (H * DV, D_MODEL), jnp.float32) * s, 'bo': jnp.zeros((D_MODEL,), jnp.float32)}
    _L0_xattn_all = _L0_xattn_setup()
    _L0_xattn_in = {k: v for k, v in _L0_xattn_all.items() if k in ('Wq', 'bq', 'Wk', 'bk', 'Wv', 'bv', 'Wo', 'bo')}
    del _L0_xattn_all

    def _L0_ffn_setup():
        import jax, jax.numpy as jnp
        import numpy as np
        DIM = 128

        def _reference_tuple_inner(x, W_r, W_k, W_v, mu_r, mu_k):
            B, T, C = x.shape
            x_prev = jnp.concatenate([jnp.zeros((B, 1, C), x.dtype), x[:, :-1, :]], axis=1)
            xr = mu_r * x + (1.0 - mu_r) * x_prev
            xk = mu_k * x + (1.0 - mu_k) * x_prev
            r = jax.nn.sigmoid(jnp.einsum('btc,dc->btd', xr, W_r))
            k = jnp.einsum('btc,dc->btd', xk, W_k)
            k_act = jnp.square(jax.nn.relu(k))
            out = r * jnp.einsum('btc,dc->btd', k_act, W_v)
            new_state = x[:, -1, :]
            return (out, new_state)
        key = jax.random.key(seed)
        ks = jax.random.split(key, 6)
        B, T, C = (8, 256, DIM)
        x = jax.random.normal(ks[0], (B, T, C), dtype=jnp.float32)
        s = 1.0 / np.sqrt(C)
        W_r = jax.random.uniform(ks[1], (C, C), jnp.float32, -s, s)
        W_k = jax.random.uniform(ks[2], (C, C), jnp.float32, -s, s)
        W_v = jax.random.uniform(ks[3], (C, C), jnp.float32, -s, s)
        mu_r = jax.random.uniform(ks[4], (C,), jnp.float32)
        mu_k = jax.random.uniform(ks[5], (C,), jnp.float32)
        return {'x': x, 'W_r': W_r, 'W_k': W_k, 'W_v': W_v, 'mu_r': mu_r, 'mu_k': mu_k}
    _L0_ffn_all = _L0_ffn_setup()
    _L0_ffn_in = {k: v for k, v in _L0_ffn_all.items() if k in ('W_r', 'W_k', 'W_v', 'mu_r', 'mu_k')}
    del _L0_ffn_all

    def _L1_xattn_setup():
        import jax, jax.numpy as jnp
        import numpy as np
        B, T, D = (2, 256, 128)
        N, H = (16, 64)
        key = jax.random.key(seed)
        ks = jax.random.split(key, 8)
        glorot = lambda k, shape, fan_in, fan_out: jax.random.uniform(k, shape, jnp.float32, -1.0, 1.0) * np.sqrt(6.0 / (fan_in + fan_out))
        return {'q': jax.random.normal(ks[0], (B, T, D), jnp.float32), 'v': jax.random.normal(ks[1], (B, T, D), jnp.float32), 'k': jax.random.normal(ks[2], (B, T, D), jnp.float32), 'w_query': glorot(ks[3], (D, N, H), D, N * H), 'b_query': jnp.zeros((N, 1, H), jnp.float32), 'w_value': glorot(ks[4], (D, N, H), D, N * H), 'b_value': jnp.zeros((N, 1, H), jnp.float32), 'w_key': glorot(ks[5], (D, N, H), D, N * H), 'b_key': jnp.zeros((N, 1, H), jnp.float32), 'w_projection': glorot(ks[6], (N, D, H), N * H, D), 'b_projection': jnp.zeros((1, D), jnp.float32)}
    _L1_xattn_all = _L1_xattn_setup()
    _L1_xattn_in = {k: v for k, v in _L1_xattn_all.items() if k in ('w_query', 'b_query', 'w_value', 'b_value', 'w_key', 'b_key', 'w_projection', 'b_projection')}
    del _L1_xattn_all

    def _L1_ffn_setup():
        import jax, jax.numpy as jnp
        import numpy as np
        B, N, C, H, REG = (1, 2309, 128, 16, 5)
        D = C // H
        key = jax.random.key(seed)
        k0, k1, k2, k3 = jax.random.split(key, 4)
        x = jax.random.normal(k0, (B, N, C), dtype=jnp.float32)
        g_info = jax.random.normal(k1, (12, 2, C), dtype=jnp.float32)
        W_qkv = jax.random.normal(k2, (C, 3 * C), dtype=jnp.float32) * 0.02
        W_proj = jax.random.normal(k3, (C, C), dtype=jnp.float32) * 0.02
        b_proj = jnp.zeros((C,), dtype=jnp.float32)
        return {'x': x, 'g_info': g_info, 'W_qkv': W_qkv, 'W_proj': W_proj, 'b_proj': b_proj}
    _L1_ffn_all = _L1_ffn_setup()
    _L1_ffn_in = {k: v for k, v in _L1_ffn_all.items() if k in ('g_info', 'W_qkv', 'W_proj', 'b_proj')}
    del _L1_ffn_all

    def _L2_xattn_setup():
        import jax, jax.numpy as jnp
        import numpy as np
        from jax import lax
        BIG = jnp.float32(1e+30)

        def _pairwise_euclidean(a, b):
            aa = jnp.sum(a * a, axis=-1)[:, None]
            bb = jnp.sum(b * b, axis=-1)[None, :]
            ab = a @ b.T
            return jnp.sqrt(jnp.maximum(aa + bb - 2.0 * ab, 0.0))

        def _dtw_cost(D):
            row0 = jnp.cumsum(D[0])

            def row_step(prev_row, d_row):
                first = d_row[0] + prev_row[0]

                def col_step(left, inp):
                    d_ij, up, diag = inp
                    r = d_ij + jnp.minimum(jnp.minimum(up, left), diag)
                    return (r, r)
                _, rest = lax.scan(col_step, first, (d_row[1:], prev_row[1:], prev_row[:-1]))
                row = jnp.concatenate([first[None], rest])
                return (row, row)
            _, rows = lax.scan(row_step, row0, D[1:])
            return jnp.concatenate([row0[None], rows], axis=0)

        def _backtrack(R, T1, T2):
            L = T1 + T2 - 1

            def step(carry, _):
                i, j, done = carry
                valid = jnp.logical_not(done)
                cd = jnp.where((i > 0) & (j > 0), R[jnp.maximum(i - 1, 0), jnp.maximum(j - 1, 0)], BIG)
                cu = jnp.where(i > 0, R[jnp.maximum(i - 1, 0), j], BIG)
                cl = jnp.where(j > 0, R[i, jnp.maximum(j - 1, 0)], BIG)
                choice = jnp.argmin(jnp.stack([cd, cu, cl]))
                ni = jnp.where(choice <= 1, i - 1, i)
                nj = jnp.where((choice == 0) | (choice == 2), j - 1, j)
                at_origin = (i == 0) & (j == 0)
                ni = jnp.where(at_origin, 0, ni)
                nj = jnp.where(at_origin, 0, nj)
                return ((ni, nj, done | at_origin), (i, j, valid))
            init = (jnp.int32(T1 - 1), jnp.int32(T2 - 1), jnp.bool_(False))
            _, (i_idx, j_idx, valid) = lax.scan(step, init, None, length=L)
            return (i_idx, j_idx, valid)

        def _align_one(small, large):
            T_small, d = small.shape
            T_large = large.shape[0]
            D = _pairwise_euclidean(small, large)
            R = _dtw_cost(D)
            i_idx, j_idx, valid = _backtrack(R, T_small, T_large)
            contrib = small[i_idx] * valid[:, None].astype(small.dtype)
            expanded = jnp.zeros((T_large, d), dtype=small.dtype).at[j_idx].add(contrib)
            return expanded
        key = jax.random.key(seed)
        k1, k2 = jax.random.split(key)
        teacher = jax.random.normal(k1, (16, 50, 128), dtype=jnp.float32)
        student = jax.random.normal(k2, (16, 75, 128), dtype=jnp.float32)
        return {'teacher_features': teacher, 'student_features': student}
    _L2_xattn_all = _L2_xattn_setup()
    _L2_xattn_in = {k: v for k, v in _L2_xattn_all.items() if k in ()}
    del _L2_xattn_all

    def _L2_ffn_setup():
        import jax, jax.numpy as jnp
        import numpy as np
        B, S, D, H, M, E, K = (4, 256, 128, 256, 64, 8, 2)

        def _layernorm(x, g, b, eps=1e-05):
            mu = x.mean(-1, keepdims=True)
            var = ((x - mu) ** 2).mean(-1, keepdims=True)
            return (x - mu) * jax.lax.rsqrt(var + eps) * g + b

        def _forward(inputs_embeds, enc_W, enc_b, s2c_W, s2c_b, rW1, rb1, rW2, rb2, We1, be1, We2, be2, c2s_W, c2s_b, dec_W, dec_b, ln_g, ln_b):
            b, s, _ = inputs_embeds.shape
            spikes_enc = jax.nn.sigmoid(inputs_embeds @ enc_W + enc_b)
            flat = spikes_enc.reshape(b * s, H)
            cont = flat @ s2c_W + s2c_b
            logits = jnp.tanh(cont @ rW1 + rb1) @ rW2 + rb2
            probs = jax.nn.softmax(logits, axis=-1)
            topw, topi = jax.lax.top_k(probs, K)
            w = topw / topw.sum(-1, keepdims=True)
            gates = (jax.nn.one_hot(topi, E, dtype=cont.dtype) * w[..., None]).sum(1)
            h = jax.nn.relu(jnp.einsum('nm,emh->enh', cont, We1) + be1[:, None, :])
            expert_out = jnp.einsum('enh,ehm->enm', h, We2) + be2[:, None, :]
            output_flat = jnp.einsum('enm,ne->nm', expert_out, gates)
            spikes_moe = jax.nn.sigmoid(output_flat @ c2s_W + c2s_b).reshape(b, s, H)
            decoded = jax.nn.sigmoid(spikes_moe @ dec_W + dec_b)
            return _layernorm(decoded, ln_g, ln_b)
        key = jax.random.key(seed)
        ks = jax.random.split(key, 10)
        r = lambda k, shape: jax.random.normal(k, shape, dtype=jnp.float32) * 0.02
        return {'inputs_embeds': jax.random.normal(ks[0], (B, S, D), dtype=jnp.float32), 'enc_W': r(ks[1], (D, H)), 'enc_b': jnp.zeros((H,), jnp.float32), 's2c_W': r(ks[2], (H, M)), 's2c_b': jnp.zeros((M,), jnp.float32), 'rW1': r(ks[3], (M, 64)), 'rb1': jnp.zeros((64,), jnp.float32), 'rW2': r(ks[4], (64, E)), 'rb2': jnp.zeros((E,), jnp.float32), 'We1': r(ks[5], (E, M, H // 2)), 'be1': jnp.zeros((E, H // 2), jnp.float32), 'We2': r(ks[6], (E, H // 2, M)), 'be2': jnp.zeros((E, M), jnp.float32), 'c2s_W': r(ks[7], (M, H)), 'c2s_b': jnp.zeros((H,), jnp.float32), 'dec_W': r(ks[8], (H, D)), 'dec_b': jnp.zeros((D,), jnp.float32), 'ln_g': jnp.ones((D,), jnp.float32), 'ln_b': jnp.zeros((D,), jnp.float32)}
    _L2_ffn_all = _L2_ffn_setup()
    _L2_ffn_in = {k: v for k, v in _L2_ffn_all.items() if k in ('enc_W', 'enc_b', 's2c_W', 's2c_b', 'rW1', 'rb1', 'rW2', 'rb2', 'We1', 'be1', 'We2', 'be2', 'c2s_W', 'c2s_b', 'dec_W', 'dec_b', 'ln_g', 'ln_b')}
    del _L2_ffn_all

    def _L3_xattn_setup():
        import jax, jax.numpy as jnp
        import numpy as np
        D_MODEL = 128
        NUM_HEADS = 16
        STRIDE = 4
        HEAD_DIM = D_MODEL // NUM_HEADS
        SCALE = HEAD_DIM ** (-0.5)
        key = jax.random.key(seed)
        ks = jax.random.split(key, 12)
        B, T, S = (2, 64, 1024)
        inp = {'query': jax.random.normal(ks[0], (B, T, D_MODEL), jnp.float32), 'key': jax.random.normal(ks[1], (B, S, D_MODEL), jnp.float32), 'value': jax.random.normal(ks[2], (B, S, D_MODEL), jnp.float32), 'key_padding_mask': jnp.zeros((B, S), dtype=bool)}
        s = 1.0 / np.sqrt(D_MODEL)
        inp['Wq'] = jax.random.normal(ks[3], (D_MODEL, D_MODEL), jnp.float32) * s
        inp['bq'] = jnp.zeros((D_MODEL,), jnp.float32)
        inp['Wk'] = jax.random.normal(ks[4], (D_MODEL, D_MODEL), jnp.float32) * s
        inp['bk'] = jnp.zeros((D_MODEL,), jnp.float32)
        inp['Wv'] = jax.random.normal(ks[5], (D_MODEL, D_MODEL), jnp.float32) * s
        inp['bv'] = jnp.zeros((D_MODEL,), jnp.float32)
        inp['Wo'] = jax.random.normal(ks[6], (D_MODEL, D_MODEL), jnp.float32) * s
        inp['bo'] = jnpp = jnp.zeros((D_MODEL,), jnp.float32)
        return inp
    _L3_xattn_all = _L3_xattn_setup()
    _L3_xattn_in = {k: v for k, v in _L3_xattn_all.items() if k in ('Wq', 'bq', 'Wk', 'bk', 'Wv', 'bv', 'Wo', 'bo')}
    del _L3_xattn_all

    def _L3_ffn_setup():
        import jax, jax.numpy as jnp
        import numpy as np
        H = 128
        I = 128
        E = 8
        key = jax.random.key(seed)
        ks = jax.random.split(key, 8)
        s = 0.02
        x = jax.random.normal(ks[0], (4, 256, H), dtype=jnp.float32)
        Wg = jax.random.normal(ks[1], (H, E), dtype=jnp.float32) * s
        bg = jnp.zeros((E,), dtype=jnp.float32)
        W1 = jax.random.normal(ks[2], (E, H, I), dtype=jnp.float32) * s
        b1 = jnp.zeros((E, I), dtype=jnp.float32)
        W2 = jax.random.normal(ks[3], (E, I, H), dtype=jnp.float32) * s
        b2 = jnp.zeros((E, H), dtype=jnp.float32)
        return {'x': x, 'Wg': Wg, 'bg': bg, 'W1': W1, 'b1': b1, 'W2': W2, 'b2': b2}
    _L3_ffn_all = _L3_ffn_setup()
    _L3_ffn_in = {k: v for k, v in _L3_ffn_all.items() if k in ('Wg', 'bg', 'W1', 'b1', 'W2', 'b2')}
    del _L3_ffn_all
    return {'x': x, 'ctx_1024': ctx_1024, 'mask_BxS2_bf0': mask_BxS2_bf0, 'L0_xattn_Wq': _L0_xattn_in['Wq'], 'L0_xattn_bq': _L0_xattn_in['bq'], 'L0_xattn_Wk': _L0_xattn_in['Wk'], 'L0_xattn_bk': _L0_xattn_in['bk'], 'L0_xattn_Wv': _L0_xattn_in['Wv'], 'L0_xattn_bv': _L0_xattn_in['bv'], 'L0_xattn_Wo': _L0_xattn_in['Wo'], 'L0_xattn_bo': _L0_xattn_in['bo'], 'L0_ffn_W_r': _L0_ffn_in['W_r'], 'L0_ffn_W_k': _L0_ffn_in['W_k'], 'L0_ffn_W_v': _L0_ffn_in['W_v'], 'L0_ffn_mu_r': _L0_ffn_in['mu_r'], 'L0_ffn_mu_k': _L0_ffn_in['mu_k'], 'L1_xattn_w_query': _L1_xattn_in['w_query'], 'L1_xattn_b_query': _L1_xattn_in['b_query'], 'L1_xattn_w_value': _L1_xattn_in['w_value'], 'L1_xattn_b_value': _L1_xattn_in['b_value'], 'L1_xattn_w_key': _L1_xattn_in['w_key'], 'L1_xattn_b_key': _L1_xattn_in['b_key'], 'L1_xattn_w_projection': _L1_xattn_in['w_projection'], 'L1_xattn_b_projection': _L1_xattn_in['b_projection'], 'L1_ffn_g_info': _L1_ffn_in['g_info'], 'L1_ffn_W_qkv': _L1_ffn_in['W_qkv'], 'L1_ffn_W_proj': _L1_ffn_in['W_proj'], 'L1_ffn_b_proj': _L1_ffn_in['b_proj'], 'L2_ffn_enc_W': _L2_ffn_in['enc_W'], 'L2_ffn_enc_b': _L2_ffn_in['enc_b'], 'L2_ffn_s2c_W': _L2_ffn_in['s2c_W'], 'L2_ffn_s2c_b': _L2_ffn_in['s2c_b'], 'L2_ffn_rW1': _L2_ffn_in['rW1'], 'L2_ffn_rb1': _L2_ffn_in['rb1'], 'L2_ffn_rW2': _L2_ffn_in['rW2'], 'L2_ffn_rb2': _L2_ffn_in['rb2'], 'L2_ffn_We1': _L2_ffn_in['We1'], 'L2_ffn_be1': _L2_ffn_in['be1'], 'L2_ffn_We2': _L2_ffn_in['We2'], 'L2_ffn_be2': _L2_ffn_in['be2'], 'L2_ffn_c2s_W': _L2_ffn_in['c2s_W'], 'L2_ffn_c2s_b': _L2_ffn_in['c2s_b'], 'L2_ffn_dec_W': _L2_ffn_in['dec_W'], 'L2_ffn_dec_b': _L2_ffn_in['dec_b'], 'L2_ffn_ln_g': _L2_ffn_in['ln_g'], 'L2_ffn_ln_b': _L2_ffn_in['ln_b'], 'L3_xattn_Wq': _L3_xattn_in['Wq'], 'L3_xattn_bq': _L3_xattn_in['bq'], 'L3_xattn_Wk': _L3_xattn_in['Wk'], 'L3_xattn_bk': _L3_xattn_in['bk'], 'L3_xattn_Wv': _L3_xattn_in['Wv'], 'L3_xattn_bv': _L3_xattn_in['bv'], 'L3_xattn_Wo': _L3_xattn_in['Wo'], 'L3_xattn_bo': _L3_xattn_in['bo'], 'L3_ffn_Wg': _L3_ffn_in['Wg'], 'L3_ffn_bg': _L3_ffn_in['bg'], 'L3_ffn_W1': _L3_ffn_in['W1'], 'L3_ffn_b1': _L3_ffn_in['b1'], 'L3_ffn_W2': _L3_ffn_in['W2'], 'L3_ffn_b2': _L3_ffn_in['b2']}

def reference(x, ctx_1024, mask_BxS2_bf0, L0_xattn_Wq, L0_xattn_bq, L0_xattn_Wk, L0_xattn_bk, L0_xattn_Wv, L0_xattn_bv, L0_xattn_Wo, L0_xattn_bo, L0_ffn_W_r, L0_ffn_W_k, L0_ffn_W_v, L0_ffn_mu_r, L0_ffn_mu_k, L1_xattn_w_query, L1_xattn_b_query, L1_xattn_w_value, L1_xattn_b_value, L1_xattn_w_key, L1_xattn_b_key, L1_xattn_w_projection, L1_xattn_b_projection, L1_ffn_g_info, L1_ffn_W_qkv, L1_ffn_W_proj, L1_ffn_b_proj, L2_ffn_enc_W, L2_ffn_enc_b, L2_ffn_s2c_W, L2_ffn_s2c_b, L2_ffn_rW1, L2_ffn_rb1, L2_ffn_rW2, L2_ffn_rb2, L2_ffn_We1, L2_ffn_be1, L2_ffn_We2, L2_ffn_be2, L2_ffn_c2s_W, L2_ffn_c2s_b, L2_ffn_dec_W, L2_ffn_dec_b, L2_ffn_ln_g, L2_ffn_ln_b, L3_xattn_Wq, L3_xattn_bq, L3_xattn_Wk, L3_xattn_bk, L3_xattn_Wv, L3_xattn_bv, L3_xattn_Wo, L3_xattn_bo, L3_ffn_Wg, L3_ffn_bg, L3_ffn_W1, L3_ffn_b1, L3_ffn_W2, L3_ffn_b2):
    import jax
    import jax.numpy as jnp

    def _L0_xattn_ref(queries, keys, values, Wq, bq, Wk, bk, Wv, bv, Wo, bo):
        import jax, jax.numpy as jnp
        import numpy as np
        B, L, D_MODEL, H, DK, DV = (4, 256, 128, 16, 64, 64)
        b, l, _ = queries.shape
        s = keys.shape[1]
        q = (queries @ Wq + bq).reshape(b, l, H, DK)
        k = (keys @ Wk + bk).reshape(b, s, H, DK)
        v = (values @ Wv + bv).reshape(b, s, H, DV)
        scale = 1.0 / np.sqrt(DK)
        scores = jnp.einsum('blhe,bshe->bhls', q, k)
        causal = jnp.triu(jnp.ones((l, s), bool), k=1)
        scores = jnp.where(causal[None, None], -jnp.inf, scores)
        A = jax.nn.softmax(scale * scores, axis=-1)
        out = jnp.einsum('bhls,bshd->blhd', A, v).reshape(b, l, H * DV)
        return out @ Wo + bo

    def _L0_ffn_ref(x, W_r, W_k, W_v, mu_r, mu_k):
        import jax, jax.numpy as jnp
        import numpy as np
        DIM = 128

        def _reference_tuple_inner(x, W_r, W_k, W_v, mu_r, mu_k):
            B, T, C = x.shape
            x_prev = jnp.concatenate([jnp.zeros((B, 1, C), x.dtype), x[:, :-1, :]], axis=1)
            xr = mu_r * x + (1.0 - mu_r) * x_prev
            xk = mu_k * x + (1.0 - mu_k) * x_prev
            r = jax.nn.sigmoid(jnp.einsum('btc,dc->btd', xr, W_r))
            k = jnp.einsum('btc,dc->btd', xk, W_k)
            k_act = jnp.square(jax.nn.relu(k))
            out = r * jnp.einsum('btc,dc->btd', k_act, W_v)
            new_state = x[:, -1, :]
            return (out, new_state)
        return _reference_tuple_inner(x, W_r, W_k, W_v, mu_r, mu_k)[0]

    def _L1_xattn_ref(q, v, k, w_query, b_query, w_value, b_value, w_key, b_key, w_projection, b_projection):
        import jax, jax.numpy as jnp
        import numpy as np
        B, T, D = (2, 256, 128)
        N, H = (16, 64)
        query = jnp.einsum('btd,dnh->bnth', q, w_query) + b_query
        value = jnp.einsum('btd,dnh->bnth', v, w_value) + b_value
        key_p = jnp.einsum('btd,dnh->bnth', k, w_key) + b_key
        scale = 1.0 / jnp.sqrt(jnp.asarray(H, query.dtype))
        scores = jnp.einsum('bnth,bnsh->bnts', query, key_p) * scale
        weights = jax.nn.softmax(scores, axis=-1)
        attn = jnp.einsum('bnts,bnsh->bnth', weights, value)
        out = jnp.einsum('bnth,ndh->btd', attn, w_projection) + b_projection
        return out

    def _L1_ffn_ref(x, g_info, W_qkv, W_proj, b_proj):
        import jax, jax.numpy as jnp
        import numpy as np
        B, N, C, H, REG = (1, 2309, 128, 16, 5)
        D = C // H
        Bx, Nx, Cx = x.shape
        scale = D ** (-0.5)
        qkv = (x @ W_qkv).reshape(Bx, Nx, 3, H, D)
        q, k, v = (qkv[:, :, 0], qkv[:, :, 1], qkv[:, :, 2])
        g_layer = g_info[0].reshape(-1, H, D)
        q_g = g_layer[0]
        q_pure = q[:, REG:]
        q_n = q_pure / jnp.linalg.norm(q_pure, axis=-1, keepdims=True)
        qg_n = q_g / jnp.linalg.norm(q_g, axis=-1, keepdims=True)
        sim = (qg_n[None, None] * q_n).sum(-1).mean(-1)
        sim = (sim - sim.min()) / (sim.max() - sim.min())
        pos = sim > 0.9
        logits = jnp.einsum('bqhd,bkhd->bhqk', q * scale, k)

        def masked_attn(tok_mask):
            key_mask = jnp.concatenate([jnp.ones((Bx, REG), bool), tok_mask], axis=1)
            l = jnp.where(key_mask[:, None, None, :], logits, -jnp.inf)
            a = jax.nn.softmax(l, axis=-1)
            return jnp.einsum('bhqk,bkhd->bqhd', a, v)
        x_pos = masked_attn(pos)
        x_neg = masked_attn(~pos)
        reg_out = (x_pos[:, :REG] + x_neg[:, :REG]) * 0.5
        tok_out = jnp.where(pos[:, :, None, None], x_pos[:, REG:], x_neg[:, REG:])
        out = jnp.concatenate([reg_out, tok_out], axis=1).reshape(Bx, Nx, Cx)
        return out @ W_proj + b_proj

    def _L2_xattn_ref(teacher_features, student_features):
        import jax, jax.numpy as jnp
        import numpy as np
        from jax import lax
        BIG = jnp.float32(1e+30)

        def _pairwise_euclidean(a, b):
            aa = jnp.sum(a * a, axis=-1)[:, None]
            bb = jnp.sum(b * b, axis=-1)[None, :]
            ab = a @ b.T
            return jnp.sqrt(jnp.maximum(aa + bb - 2.0 * ab, 0.0))

        def _dtw_cost(D):
            row0 = jnp.cumsum(D[0])

            def row_step(prev_row, d_row):
                first = d_row[0] + prev_row[0]

                def col_step(left, inp):
                    d_ij, up, diag = inp
                    r = d_ij + jnp.minimum(jnp.minimum(up, left), diag)
                    return (r, r)
                _, rest = lax.scan(col_step, first, (d_row[1:], prev_row[1:], prev_row[:-1]))
                row = jnp.concatenate([first[None], rest])
                return (row, row)
            _, rows = lax.scan(row_step, row0, D[1:])
            return jnp.concatenate([row0[None], rows], axis=0)

        def _backtrack(R, T1, T2):
            L = T1 + T2 - 1

            def step(carry, _):
                i, j, done = carry
                valid = jnp.logical_not(done)
                cd = jnp.where((i > 0) & (j > 0), R[jnp.maximum(i - 1, 0), jnp.maximum(j - 1, 0)], BIG)
                cu = jnp.where(i > 0, R[jnp.maximum(i - 1, 0), j], BIG)
                cl = jnp.where(j > 0, R[i, jnp.maximum(j - 1, 0)], BIG)
                choice = jnp.argmin(jnp.stack([cd, cu, cl]))
                ni = jnp.where(choice <= 1, i - 1, i)
                nj = jnp.where((choice == 0) | (choice == 2), j - 1, j)
                at_origin = (i == 0) & (j == 0)
                ni = jnp.where(at_origin, 0, ni)
                nj = jnp.where(at_origin, 0, nj)
                return ((ni, nj, done | at_origin), (i, j, valid))
            init = (jnp.int32(T1 - 1), jnp.int32(T2 - 1), jnp.bool_(False))
            _, (i_idx, j_idx, valid) = lax.scan(step, init, None, length=L)
            return (i_idx, j_idx, valid)

        def _align_one(small, large):
            T_small, d = small.shape
            T_large = large.shape[0]
            D = _pairwise_euclidean(small, large)
            R = _dtw_cost(D)
            i_idx, j_idx, valid = _backtrack(R, T_small, T_large)
            contrib = small[i_idx] * valid[:, None].astype(small.dtype)
            expanded = jnp.zeros((T_large, d), dtype=small.dtype).at[j_idx].add(contrib)
            return expanded
        return jax.vmap(_align_one)(teacher_features, student_features)

    def _L2_ffn_ref(inputs_embeds, enc_W, enc_b, s2c_W, s2c_b, rW1, rb1, rW2, rb2, We1, be1, We2, be2, c2s_W, c2s_b, dec_W, dec_b, ln_g, ln_b):
        import jax, jax.numpy as jnp
        import numpy as np
        B, S, D, H, M, E, K = (4, 256, 128, 256, 64, 8, 2)

        def _layernorm(x, g, b, eps=1e-05):
            mu = x.mean(-1, keepdims=True)
            var = ((x - mu) ** 2).mean(-1, keepdims=True)
            return (x - mu) * jax.lax.rsqrt(var + eps) * g + b

        def _forward(inputs_embeds, enc_W, enc_b, s2c_W, s2c_b, rW1, rb1, rW2, rb2, We1, be1, We2, be2, c2s_W, c2s_b, dec_W, dec_b, ln_g, ln_b):
            b, s, _ = inputs_embeds.shape
            spikes_enc = jax.nn.sigmoid(inputs_embeds @ enc_W + enc_b)
            flat = spikes_enc.reshape(b * s, H)
            cont = flat @ s2c_W + s2c_b
            logits = jnp.tanh(cont @ rW1 + rb1) @ rW2 + rb2
            probs = jax.nn.softmax(logits, axis=-1)
            topw, topi = jax.lax.top_k(probs, K)
            w = topw / topw.sum(-1, keepdims=True)
            gates = (jax.nn.one_hot(topi, E, dtype=cont.dtype) * w[..., None]).sum(1)
            h = jax.nn.relu(jnp.einsum('nm,emh->enh', cont, We1) + be1[:, None, :])
            expert_out = jnp.einsum('enh,ehm->enm', h, We2) + be2[:, None, :]
            output_flat = jnp.einsum('enm,ne->nm', expert_out, gates)
            spikes_moe = jax.nn.sigmoid(output_flat @ c2s_W + c2s_b).reshape(b, s, H)
            decoded = jax.nn.sigmoid(spikes_moe @ dec_W + dec_b)
            return _layernorm(decoded, ln_g, ln_b)
        return _forward(inputs_embeds, enc_W, enc_b, s2c_W, s2c_b, rW1, rb1, rW2, rb2, We1, be1, We2, be2, c2s_W, c2s_b, dec_W, dec_b, ln_g, ln_b)

    def _L3_xattn_ref(query, key, value, key_padding_mask, Wq, bq, Wk, bk, Wv, bv, Wo, bo):
        import jax, jax.numpy as jnp
        import numpy as np
        D_MODEL = 128
        NUM_HEADS = 16
        STRIDE = 4
        HEAD_DIM = D_MODEL // NUM_HEADS
        SCALE = HEAD_DIM ** (-0.5)
        B, T, _ = query.shape
        S = key.shape[1]
        q = (query @ Wq + bq).reshape(B, T, NUM_HEADS, HEAD_DIM).transpose(0, 2, 1, 3)
        k = (key @ Wk + bk).reshape(B, S, NUM_HEADS, HEAD_DIM).transpose(0, 2, 1, 3)
        v = (value @ Wv + bv).reshape(B, S, NUM_HEADS, HEAD_DIM).transpose(0, 2, 1, 3)
        scores = jnp.einsum('bhtd,bhsd->bhts', q, k) * SCALE
        s_idx = jnp.arange(S)[None, None, None, :]
        h_idx = jnp.arange(NUM_HEADS)[None, :, None, None]
        hepos_mask = (s_idx - h_idx) % STRIDE != 0
        scores = jnp.where(hepos_mask, -jnp.inf, scores)
        scores = jnp.where(key_padding_mask[:, None, None, :], -jnp.inf, scores)
        attn = jax.nn.softmax(scores, axis=-1)
        context = jnp.einsum('bhts,bhsd->bhtd', attn, v)
        context = context.transpose(0, 2, 1, 3).reshape(B, T, D_MODEL)
        return context @ Wo + bo

    def _L3_ffn_ref(x, Wg, bg, W1, b1, W2, b2):
        import jax, jax.numpy as jnp
        import numpy as np
        H = 128
        I = 128
        E = 8
        B, S, Hd = x.shape
        xf = x.reshape(-1, Hd)
        logits = xf @ Wg + bg
        gates = jax.nn.softmax(logits, axis=-1)
        idx = jnp.argmax(gates, axis=-1)
        h = jax.nn.gelu(jnp.einsum('th,ehi->tei', xf, W1) + b1, approximate=False)
        y = jnp.einsum('tei,eih->teh', h, W2) + b2
        out = jnp.take_along_axis(y, idx[:, None, None], axis=1)[:, 0, :]
        return out.reshape(B, S, Hd)
    x = x + _L0_xattn_ref(_layernorm(x, axis=-1), ctx_1024, ctx_1024, L0_xattn_Wq, L0_xattn_bq, L0_xattn_Wk, L0_xattn_bk, L0_xattn_Wv, L0_xattn_bv, L0_xattn_Wo, L0_xattn_bo)
    x = x + _L0_ffn_ref(_layernorm(x, axis=-1), L0_ffn_W_r, L0_ffn_W_k, L0_ffn_W_v, L0_ffn_mu_r, L0_ffn_mu_k)
    x = x + _L1_xattn_ref(_layernorm(x, axis=-1), ctx_1024, ctx_1024, L1_xattn_w_query, L1_xattn_b_query, L1_xattn_w_value, L1_xattn_b_value, L1_xattn_w_key, L1_xattn_b_key, L1_xattn_w_projection, L1_xattn_b_projection)
    x = x + _L1_ffn_ref(_layernorm(x, axis=-1), L1_ffn_g_info, L1_ffn_W_qkv, L1_ffn_W_proj, L1_ffn_b_proj)
    x = x + _L2_xattn_ref(ctx_1024, _layernorm(x, axis=-1))
    x = x + _L2_ffn_ref(_layernorm(x, axis=-1), L2_ffn_enc_W, L2_ffn_enc_b, L2_ffn_s2c_W, L2_ffn_s2c_b, L2_ffn_rW1, L2_ffn_rb1, L2_ffn_rW2, L2_ffn_rb2, L2_ffn_We1, L2_ffn_be1, L2_ffn_We2, L2_ffn_be2, L2_ffn_c2s_W, L2_ffn_c2s_b, L2_ffn_dec_W, L2_ffn_dec_b, L2_ffn_ln_g, L2_ffn_ln_b)
    x = x + _L3_xattn_ref(_layernorm(x, axis=-1), ctx_1024, ctx_1024, mask_BxS2_bf0, L3_xattn_Wq, L3_xattn_bq, L3_xattn_Wk, L3_xattn_bk, L3_xattn_Wv, L3_xattn_bv, L3_xattn_Wo, L3_xattn_bo)
    x = x + _L3_ffn_ref(_layernorm(x, axis=-1), L3_ffn_Wg, L3_ffn_bg, L3_ffn_W1, L3_ffn_b1, L3_ffn_W2, L3_ffn_b2)
    return x

_drawn_inputs = setup_inputs


def setup_inputs(seed=0):
    import zlib

    import numpy as np

    out = dict(_drawn_inputs(seed))
    spreads = {'L0_xattn_bq': (0.0, 0.1),
     'L0_xattn_bk': (0.0, 0.8),
     'L0_xattn_bv': (0.0, 0.1),
     'L0_xattn_bo': (0.0, 0.374),
     'L1_xattn_b_query': (0.0, 0.8),
     'L1_xattn_b_value': (0.0, 0.1),
     'L1_xattn_b_key': (0.0, 0.8),
     'L1_xattn_b_projection': (0.0, 0.1),
     'L1_ffn_b_proj': (0.0, 0.1),
     'L2_ffn_enc_b': (0.0, 0.8),
     'L2_ffn_s2c_b': (0.0, 0.8),
     'L2_ffn_rb1': (0.0, 0.8),
     'L2_ffn_rb2': (0.0, 0.8),
     'L2_ffn_be1': (0.0, 0.8),
     'L2_ffn_be2': (0.0, 0.8),
     'L2_ffn_c2s_b': (0.0, 0.8),
     'L2_ffn_dec_b': (0.0, 0.1),
     'L2_ffn_ln_g': (1.0, 0.2),
     'L2_ffn_ln_b': (0.0, 0.407),
     'L3_xattn_bq': (0.0, 0.8),
     'L3_xattn_bk': (0.0, 0.8),
     'L3_xattn_bv': (0.0, 0.429),
     'L3_xattn_bo': (0.0, 0.385),
     'L3_ffn_bg': (0.0, 0.487),
     'L3_ffn_b1': (0.0, 0.8),
     'L3_ffn_b2': (0.0, 0.393)}
    factors = {'L0_ffn_mu_r': 4.002,
     'L1_ffn_g_info': 8.0,
     'L1_ffn_W_qkv': 7.299,
     'L1_ffn_W_proj': 6.612,
     'L2_ffn_enc_W': 8.0,
     'L2_ffn_s2c_W': 8.0,
     'L2_ffn_rW1': 8.0,
     'L2_ffn_rW2': 8.0,
     'L2_ffn_We1': 8.0,
     'L2_ffn_We2': 8.0,
     'L2_ffn_c2s_W': 8.0,
     'L3_ffn_Wg': 2.903,
     'L3_ffn_W1': 8.0,
     'L3_ffn_W2': 8.0}
    for name, (base, spread) in spreads.items():
        noise = np.random.default_rng([zlib.crc32(name.encode()), seed]).standard_normal(out[name].shape)
        drawn = base * np.exp(spread * noise) if base else spread * noise
        out[name] = jnp.asarray(drawn.astype(out[name].dtype))
    for name, factor in factors.items():
        out[name] = (out[name] * factor).astype(out[name].dtype)
    return out
```

```python
from contextlib import ExitStack

import concourse.bass as bass
from concourse import mybir

F32 = mybir.dt.float32
BF16 = mybir.dt.bfloat16
U8 = mybir.dt.uint8
U32 = mybir.dt.uint32
ALU = mybir.AluOpType
ACT = mybir.ActivationFunctionType
AX = mybir.AxisListType
RMAX = bass.bass_isa.ReduceOp.max
ds = bass.ds

P = 128
D = 128
B, L, S2 = 4, 256, 512
TILES = B * L // P
QT = L // P
BIG = 1e30
HALFBANK, BANK = 256, 512
EPS = 1e-5

C_ID = 0
C_TRI = 128
C_HALO = 256
C_START = 257
C_REG = 258
C_IOTA = 266
C_CLASS = 274
C_NEG = 402
C_OWN = 407
C_DIAG = 471
C_SUM = 599
C_END = 604
REG = 5
HEADS8, D8 = 16, 8
SCALE8 = float(D8) ** -0.5


class Kit:

    def __init__(self, nc, stack):
        self.nc, self.stack = nc, stack
        self.local = None
        self.stage_done = self.sem("stage_done")

    def sb(self, name, shape, dt=F32):
        return self.stack.enter_context(self.nc.sbuf_tensor(name, shape, dt))

    def lb(self, name, shape, dt=F32):
        return self.local.enter_context(self.nc.sbuf_tensor(name, shape, dt))

    def sem(self, name):
        return self.stack.enter_context(self.nc.semaphore(name))

    def meet(self, eng, stage):
        eng.drain().then_inc(self.stage_done, 1)
        eng.wait_ge(self.stage_done, 4 * (stage + 1))

class LayerNorm:

    TPS = (6, 7)

    def __init__(self, k):
        self.k = k
        self.stats = k.sb("ln_stats", [P, TILES, 6])
        self.mv = k.sb("ln_mv", [P, TILES, 2])
        self.rstd = k.sb("ln_rstd", [P, TILES])
        self.half = k.sb("ln_minus_half", [P, P])
        self.s_half = k.sem("minus_half_set")
        self.s_stats = k.sem("ln_stats_done")
        self.s_mv = k.sem("ln_mean_var_done")
        self.s_var = k.sem("ln_var_eps_done")
        self.s_rstd = k.sem("ln_rstd_done")
        self.s_y = k.sem("ln_y_done")
        self.s_tps = k.sem("ln_transposed")
        self.s_yT = k.sem("ln_yT_done")

    def pool_rstd(self, pool, n):
        pool.wait_ge(self.s_mv, TILES * (n + 1))
        pool.tensor_scalar(self.rstd[:, :], self.mv[:, :, 1], EPS, None, ALU.add).then_inc(self.s_var, 1)
        pool.wait_ge(self.s_var, n + 1)
        pool.tensor_tensor(self.rstd[:, :], self.rstd[:, :], self.half[:, 0:TILES], ALU.pow).then_inc(self.s_rstd, 1)

    def vector_stats(self, v, n, src):
        for t in range(TILES):
            v.bn_stats(self.stats[:, t, :], src[:, t, :]).then_inc(self.s_stats, 1)
        for t in range(TILES):
            v.wait_ge(self.s_stats, TILES * n + t + 1)
            v.bn_aggr(self.mv[:, t, :], self.stats[:, t, :]).then_inc(self.s_mv, 1)

    def vector_norm(self, v, n, src, dst):
        v.wait_ge(self.s_rstd, n + 1)
        v.wait_ge(self.s_mv, TILES * (n + 1))
        for t in range(TILES):
            v.tensor_scalar(dst[:, t, :], src[:, t, :], self.mv[:, t, 0:1], self.rstd[:, t:t + 1],
                            ALU.subtract, ALU.mult).then_inc(self.s_y, 1)

    def tensor_transpose(self, pe, n, m):
        for t in range(TILES):
            pe.wait_ge(self.s_y, TILES * n + t + 1)
            mm = pe.transpose(self.k.PS[:, self.TPS[t // 4], (t % 4) * P:(t % 4) * P + P], self.k.y[:, t, :], self.k.ident)
            if t % 4 == 3:
                mm.then_inc(self.s_tps, 1)

    def scalar_yT(self, act, m):
        for h in range(2):
            act.wait_ge(self.s_tps, 2 * m + h + 1)
            act.copy(self.k.yT[:, h * BANK:h * BANK + BANK], self.k.PS[:, self.TPS[h], :]).then_inc(self.s_yT, 1)

class WideAttention:

    ROUNDS, UNITS, STEPS, HD = 8, B, 16, 64
    S, T, O, G = (0, 1), (2, 3), (4, 5), (6, 7)

    def __init__(self, k, name, norm, causal, wo_by_head):
        self.yT_in = 2 * (norm + 1)
        self.k, self.name, self.causal, self.wo_by_head = k, name, causal, wo_by_head
        n = name + "_"
        self.wq = k.lb(n + "wq", [P, P])
        self.wk = k.lb(n + "wk", [P, P])
        self.bq = k.lb(n + "bq", [P, 1])
        self.bk = k.lb(n + "bk", [P, 1])
        self.wv = k.lb(n + "wv", [P, 8 * P])
        self.bv = k.lb(n + "bv", [P, 8 * P])
        self.wo = k.lb(n + "wo", [P, 8, P])
        self.wo_in = k.lb(n + "wo_in", [P, 8, P]) if wo_by_head else None
        self.bo = k.lb(n + "bo", [P, P])
        self.qT = k.lb(n + "qT", [P, 2, L])
        self.kT = k.lb(n + "kT", [P, 2, S2])
        self.v = k.lb(n + "v", [P, 2, 4, P])
        self.probs = k.lb(n + "probs", [P, 2, S2])
        self.pT = k.lb(n + "pT", [P, 2, S2])
        self.nmax = k.lb(n + "nmax", [P, 4])
        self.sums = k.lb(n + "sums", [P, 8])
        self.inv = k.lb(n + "inv", [P, 2])
        self.att = k.lb(n + "att", [P, 2, QT, P])
        self.attT = k.lb(n + "attT", [P, 2, L])
        s = k.sem
        self.w_once = s(n + "weights_loaded")
        self.w_in = s(n + "round_weights_loaded")
        self.q_ps, self.k_ps, self.v_ps = s(n + "q_product"), s(n + "k_product"), s(n + "v_product")
        self.q_sb, self.k_sb, self.v_sb = s(n + "q_ready"), s(n + "k_ready"), s(n + "v_ready")
        self.sc, self.mx, self.ex, self.tr = s(n + "scores"), s(n + "max"), s(n + "probs"), s(n + "turned")
        self.pt_v, self.pt_a = s(n + "pT_even"), s(n + "pT_odd")
        self.av, self.iv, self.nm = s(n + "pv"), s(n + "inverse"), s(n + "normed")
        self.at_ps, self.at_sb = s(n + "attT_turned"), s(n + "attT_ready")
        self.wo_ps, self.x_add = s(n + "out_product"), s(n + "x_added")
        order = [("q", 0), ("k", 0), ("v", 0)]
        for b in range(B):
            if b + 1 < B:
                order += [("q", b + 1), ("k", b + 1), ("v", b + 1)]
            if b >= 1:
                order += [("t", b - 1), ("o", b - 1)]
        order += [("t", B - 1), ("o", B - 1)]
        assert len(order) % 2 == 0
        self.bank = {u: self.G[i % 2] for i, u in enumerate(order)}
        self.before = {u: order[i - 2] for i, u in enumerate(order) if i >= 2}

    def keys(self, n):
        return P * (n % QT + 1) if self.causal else S2

    def where(self, n):
        return n // 4, (n % 4) // 2, n % 2

    def load_once(self, sp, wv, bv, bo, wo, wq, wk, bq, bk):
        sp.dma_start(self.wq[:, :], wq[:, 0:P]).then_inc(self.w_in, 16)
        sp.dma_start(self.wk[:, :], wk[:, 0:P]).then_inc(self.w_in, 16)
        sp.dma_start(self.bq[:, :], bq[0:P].unsqueeze(1)).then_inc(self.w_in, 16)
        sp.dma_start(self.bk[:, :], bk[0:P].unsqueeze(1)).then_inc(self.w_in, 16)
        sp.dma_start(self.wv[:, :], wv).then_inc(self.w_once, 16)
        sp.dma_start(self.bv[:, :], bv.unsqueeze(0).to_broadcast((P, 8 * P))).then_inc(self.w_once, 16)
        sp.dma_start(self.bo[:, :], bo.unsqueeze(0).to_broadcast((P, P))).then_inc(self.w_once, 16)
        if self.wo_by_head:
            sp.dma_start(self.wo_in[:, :, :].rearrange("p r (u h) -> p (r u) h", u=2), wo.rearrange("n d h -> d n h")).then_inc(self.w_once, 16)
        else:
            sp.dma_start(self.wo[:, :, :], wo.rearrange("(r p) d -> p r d", p=P)).then_inc(self.w_once, 16)

    def load_rounds(self, sp, wq, wk, bq, bk):
        with sp.Fori(0, self.ROUNDS - 1) as it:
            sp.wait_ge(self.q_sb, it * B + B)
            sp.wait_ge(self.k_sb, it * B + B)
            nxt = it * P + P
            sp.dma_start(self.wq[:, :], wq[:, ds(nxt, P)]).then_inc(self.w_in, 16)
            sp.dma_start(self.wk[:, :], wk[:, ds(nxt, P)]).then_inc(self.w_in, 16)
            sp.dma_start(self.bq[:, :], bq[ds(nxt, P)].unsqueeze(1)).then_inc(self.w_in, 16)
            sp.dma_start(self.bk[:, :], bk[ds(nxt, P)].unsqueeze(1)).then_inc(self.w_in, 16)

    def tensor(self, pe):
        PS, ident = self.k.PS, self.k.ident
        pe.wait_ge(self.k.ln.s_yT, self.yT_in)
        pe.wait_ge(self.w_once, 64)
        if self.wo_by_head:
            for r in range(8):
                mm = pe.transpose(PS[:, self.G[r // 4], (r % 4) * P:(r % 4) * P + P], self.wo_in[:, r, :], ident)
            mm.then_inc(self.wo_ps, 1)
            pe.wait_ge(self.x_add, 1)

        def free(u, it):
            if u == ("k", 0):
                pe.wait_ge(self.x_add, it * B + 1)
            if u not in self.before:
                return
            kind, b = self.before[u]
            done, more = {"q": (self.q_sb, 0), "k": (self.k_sb, 0), "v": (self.v_sb, 0), "t": (self.at_sb, 0),
                          "o": (self.x_add, 1)}[kind]
            pe.wait_ge(done, it * B + b + 1 + more)

        def project(kind, b, it):
            out = PS[:, self.bank[kind, b], :]
            free((kind, b), it)
            if kind == "q":
                if b == 0:
                    pe.wait_ge(self.w_in, it * 64 + 64)
                pe.matmul(out[:, 0:L], self.wq[:, :], self.k.yT[:, b * L:b * L + L], start=True, stop=True).then_inc(self.q_ps, 1)
            elif kind == "k":
                n = L if self.causal else S2
                pe.matmul(out[:, 0:n], self.wk[:, :], self.k.ctxT[:, b, 0:n], start=True, stop=True).then_inc(self.k_ps, 1)
            elif kind == "v":
                for kt in range(2 if self.causal else 4):
                    mm = pe.matmul(out[:, kt * P:kt * P + P], self.k.ctxT[:, b, kt * P:kt * P + P], self.wv[:, ds(it * P, P)],
                                   start=True, stop=True)
                mm.then_inc(self.v_ps, 1)
            elif kind == "t":
                pe.wait_ge(self.nm, it * self.STEPS + 4 * b + 4)
                for qt in range(QT):
                    mm = pe.transpose(out[:, qt * P:qt * P + P], self.att[:, b % 2, qt, :], ident)
                mm.then_inc(self.at_ps, 1)
            else:
                pe.wait_ge(self.at_sb, it * B + b + 1)
                for qt in range(QT):
                    mm = pe.matmul(out[:, qt * P:qt * P + P], self.attT[:, b % 2, qt * P:qt * P + P],
                                   self.wo[:, ds(it, 1), :].rearrange("p a d -> p (a d)"), start=True, stop=True)
                mm.then_inc(self.wo_ps, 1)

        def scores(n, it):
            b, h, qt = self.where(n)
            if n % 4 == 0:
                pe.wait_ge(self.q_sb, it * B + b + 1)
                pe.wait_ge(self.k_sb, it * B + b + 1)
            if n >= 2:
                pe.wait_ge(self.ex, it * self.STEPS + n - 1)
            rows = slice(64 * h, 64 * h + 64)
            mm = pe.matmul(PS[:, self.S[n % 2], 0:self.keys(n)], self.qT[rows, b % 2, qt * P:qt * P + P],
                           self.kT[rows, b % 2, 0:self.keys(n)], start=True, stop=not self.causal)
            if self.causal:
                mm = pe.matmul(PS[:, self.S[n % 2], qt * P:qt * P + P], self.k.identb[:, :], self.k.trib[:, :],
                               start=False, stop=True)
            mm.then_inc(self.sc, 1)

        def turn(n, it):
            pe.wait_ge(self.ex, it * self.STEPS + n + 1)
            if n >= 2:
                pe.wait_ge(self.pt_a if n % 2 else self.pt_v, it * 8 + n // 2)
            for kt in range(self.keys(n) // P):
                mm = pe.transpose(PS[:, self.T[n % 2], kt * P:kt * P + P], self.probs[:, n % 2, kt * P:kt * P + P], ident)
            mm.then_inc(self.tr, 1)

        def times_v(n, it):
            b, h, qt = self.where(n)
            if n % 4 == 0:
                pe.wait_ge(self.v_sb, it * B + b + 1)
            pe.wait_ge(self.pt_a if n % 2 else self.pt_v, it * 8 + n // 2 + 1)
            if n >= 2:
                pe.wait_ge(self.nm, it * self.STEPS + n - 1)
            last = self.keys(n) // P - 1
            for kt in range(last + 1):
                mm = pe.matmul(PS[:, self.O[n % 2], 0:64], self.pT[:, n % 2, kt * P:kt * P + P],
                               self.v[:, b % 2, kt, 64 * h:64 * h + 64], start=(kt == 0), stop=(kt == last))
            mm.then_inc(self.av, 1)

        with pe.Fori(0, self.ROUNDS) as it:
            for kind in "qkv":
                project(kind, 0, it)
            for n in range(-2, self.STEPS + 1):
                b, r = n // 4, n % 4
                if 0 <= n < self.STEPS:
                    turn(n, it)
                if n + 2 < self.STEPS:
                    scores(n + 2, it)
                if n >= 1:
                    times_v(n - 1, it)
                if 0 <= n < self.STEPS:
                    if r == 0 and b + 1 < B:
                        project("q", b + 1, it)
                        project("k", b + 1, it)
                    if r == 1 and b + 1 < B:
                        project("v", b + 1, it)
                    if r == 1 and b >= 1:
                        project("t", b - 1, it)
                    if r == 2 and b >= 1:
                        project("o", b - 1, it)
            project("t", B - 1, it)
            project("o", B - 1, it)

    def vector(self, v):
        PS = self.k.PS
        v.wait_ge(self.w_once, 64)
        if self.wo_by_head:
            v.wait_ge(self.wo_ps, 1)
            for i in range(2):
                v.tensor_copy(self.wo[:, 4 * i:4 * i + 4, :], PS[:, self.G[i], :].rearrange("p (r d) -> p r d", r=4))
        v.tensor_tensor(self.k.x[:, :, :], self.k.x[:, :, :], self.bo[:, :].unsqueeze(1).to_broadcast((P, TILES, P)),
                        ALU.add).then_inc(self.x_add, 1)
        v.wait_ge(self.x_add, 1)
        wo_extra = 1 if self.wo_by_head else 0

        def take_q(b, it):
            v.wait_ge(self.q_ps, it * B + b + 1)
            v.tensor_scalar(self.qT[:, b % 2, :], PS[:, self.bank["q", b], 0:L], self.bq[:, 0:1], 0.125,
                            ALU.add, ALU.mult).then_inc(self.q_sb, 1)

        def take_v(b, it):
            v.wait_ge(self.v_ps, it * B + b + 1)
            n = 2 if self.causal else 4
            v.tensor_tensor(self.v[:, b % 2, 0:n, :], PS[:, self.bank["v", b], 0:n * P].rearrange("p (t d) -> p t d", t=n),
                            self.bv[:, ds(it * P, P)].unsqueeze(1).to_broadcast((P, n, P)), ALU.add).then_inc(self.v_sb, 1)

        def add_x(b, it):
            v.wait_ge(self.wo_ps, it * B + b + 1 + wo_extra)
            v.tensor_tensor(self.k.x[:, 2 * b:2 * b + 2, :], self.k.x[:, 2 * b:2 * b + 2, :],
                            PS[:, self.bank["o", b], 0:L].rearrange("p (t d) -> p t d", t=QT), ALU.add).then_inc(self.x_add, 1)

        with v.Fori(0, self.ROUNDS) as it:
            take_q(0, it)
            take_v(0, it)
            for n in range(-2, self.STEPS + 1):
                b, r = n // 4, n % 4
                if 0 <= n < self.STEPS and n % 2 == 0:
                    v.wait_ge(self.tr, it * self.STEPS + n + 1)
                    w = self.keys(n)
                    v.tensor_copy(self.pT[:, 0, 0:w], PS[:, self.T[0], 0:w]).then_inc(self.pt_v, 1)
                if n + 2 < self.STEPS:
                    m = n + 2
                    v.wait_ge(self.sc, it * self.STEPS + m + 1)
                    v.tensor_reduce(self.nmax[:, m % 4:m % 4 + 1], PS[:, self.S[m % 2], 0:self.keys(m)], AX.X, ALU.max,
                                    negate=True).then_inc(self.mx, 1)
                if n >= 1:
                    m = n - 1
                    bb, h, qt = self.where(m)
                    v.wait_ge(self.av, it * self.STEPS + m + 1)
                    v.reciprocal(self.inv[:, m % 2:m % 2 + 1], self.sums[:, m % 8:m % 8 + 1]).then_inc(self.iv, 1)
                    v.wait_ge(self.iv, it * self.STEPS + m + 1)
                    v.tensor_scalar(self.att[:, bb % 2, qt, 64 * h:64 * h + 64], PS[:, self.O[m % 2], 0:64],
                                    self.inv[:, m % 2:m % 2 + 1], None, ALU.mult).then_inc(self.nm, 1)
                if 0 <= n < self.STEPS:
                    if r == 0 and b + 1 < B:
                        take_q(b + 1, it)
                    if r == 1 and b + 1 < B:
                        take_v(b + 1, it)
                    if r == 2 and b >= 1:
                        add_x(b - 1, it)
            add_x(B - 1, it)

    def scalar(self, act):
        PS = self.k.PS

        def take_k(b, it):
            act.wait_ge(self.k_ps, it * B + b + 1)
            n = L if self.causal else S2
            act.activation(self.kT[:, b % 2, 0:n], PS[:, self.bank["k", b], 0:n], ACT.Identity, bias=self.bk[:, 0:1]).then_inc(self.k_sb, 1)

        def take_attT(b, it):
            act.wait_ge(self.at_ps, it * B + b + 1)
            act.copy(self.attT[:, b % 2, :], PS[:, self.bank["t", b], 0:L]).then_inc(self.at_sb, 1)

        with act.Fori(0, self.ROUNDS) as it:
            take_k(0, it)
            for n in range(-2, self.STEPS + 1):
                b, r = n // 4, n % 4
                if 0 <= n < self.STEPS and n % 2 == 1:
                    act.wait_ge(self.tr, it * self.STEPS + n + 1)
                    w = self.keys(n)
                    act.copy(self.pT[:, 1, 0:w], PS[:, self.T[1], 0:w]).then_inc(self.pt_a, 1)
                if n + 2 < self.STEPS:
                    m = n + 2
                    act.wait_ge(self.mx, it * self.STEPS + m + 1)
                    if m >= 2:
                        act.wait_ge(self.tr, it * self.STEPS + m - 1)
                    w = self.keys(m)
                    act.activation(self.probs[:, m % 2, 0:w], PS[:, self.S[m % 2], 0:w], ACT.Exp,
                                   bias=self.nmax[:, m % 4:m % 4 + 1], accum_out=self.sums[:, m % 8:m % 8 + 1]).then_inc(self.ex, 1)
                if 0 <= n < self.STEPS:
                    if r == 0 and b + 1 < B:
                        take_k(b + 1, it)
                    if r == 1 and b >= 1:
                        take_attT(b - 1, it)
            take_attT(B - 1, it)

class ShiftMix:

    def __init__(self, k, norm):
        self.yT_in = 2 * (norm + 1)
        self.k = k
        self.w_in = k.lb("mix_w_in", [P, 3, P])
        self.wT = k.lb("mix_wT", [P, 3, P])
        self.mu = k.lb("mix_mu", [P, 2])
        self.omu = k.lb("mix_one_minus_mu", [P, 2])
        self.xr = k.lb("mix_xr", [P, B, L])
        self.xk = k.lb("mix_xk", [P, B, L])
        self.kr = k.lb("mix_relu", [P, B * L])
        self.ka = k.lb("mix_k_act", [P, B * L])
        self.r = k.lb("mix_r", [P, TILES, P])
        self.t = k.lb("mix_t", [P, TILES, P])
        s = k.sem
        self.loaded, self.w_ps, self.w_sb = s("mix_loaded"), s("mix_w_turned"), s("mix_w_ready")
        self.mixed, self.own = s("mix_mixed"), s("mix_vector")
        self.k_ps, self.kr_sb, self.ka_sb = s("mix_k_product"), s("mix_relu_done"), s("mix_square_done")
        self.r_ps, self.r_sb, self.o_ps = s("mix_r_product"), s("mix_r_done"), s("mix_out_product")

    def load(self, sp, wr, wk, wv, mu_r, mu_k):
        for i, w in enumerate((wr, wk, wv)):
            sp.dma_start(self.w_in[:, i, :], w).then_inc(self.loaded, 16)
        for i, m in enumerate((mu_r, mu_k)):
            sp.dma_start(self.mu[:, i:i + 1], m.unsqueeze(1)).then_inc(self.loaded, 16)

    def tensor(self, pe):
        PS = self.k.PS
        pe.wait_ge(self.loaded, 80)
        for i in range(3):
            mm = pe.transpose(PS[:, 0, i * P:i * P + P], self.w_in[:, i, :], self.k.ident)
        mm.then_inc(self.w_ps, 1)
        pe.wait_ge(self.w_sb, 1)
        pe.wait_ge(self.mixed, 1)
        for f in range(2):
            pe.matmul(PS[:, 1 + f, :], self.wT[:, 1, :], self.xk[:, 2 * f:2 * f + 2, :].rearrange("p b l -> p (b l)"),
                      start=True, stop=True).then_inc(self.k_ps, 1)
        pe.wait_ge(self.mixed, 2)
        for t in range(TILES):
            mm = pe.matmul(PS[:, 3 + t // 4, (t % 4) * P:(t % 4) * P + P],
                           self.xr[:, t // 2, (t % 2) * P:(t % 2) * P + P], self.wT[:, 0, :], start=True, stop=True)
            if t % 4 == 3:
                mm.then_inc(self.r_ps, 1)
        for t in range(TILES):
            if t % 4 == 0:
                pe.wait_ge(self.ka_sb, t // 4 + 1)
            mm = pe.matmul(PS[:, (0, 5)[t // 4], (t % 4) * P:(t % 4) * P + P], self.ka[:, t * P:t * P + P], self.wT[:, 2, :],
                           start=True, stop=True)
            if t % 4 == 3:
                mm.then_inc(self.o_ps, 1)

    def vector(self, v):
        PS = self.k.PS
        v.wait_ge(self.loaded, 80)
        v.wait_ge(self.w_ps, 1)
        v.tensor_copy(self.wT[:, :, :], PS[:, 0, 0:3 * P].rearrange("p (i d) -> p i d", i=3)).then_inc(self.w_sb, 1)
        v.tensor_scalar(self.omu[:, :], self.mu[:, :], -1.0, 1.0, ALU.mult, ALU.add).then_inc(self.own, 1)
        v.wait_ge(self.k.ln.s_yT, self.yT_in)
        yT = self.k.yT[:, :].rearrange("p (b l) -> p b l", b=B)
        for i, dst in ((1, self.xk), (0, self.xr)):
            v.tensor_scalar(dst[:, :, :], yT, self.mu[:, i:i + 1], None, ALU.mult).then_inc(self.own, 1)
        for n, (i, dst) in enumerate(((1, self.xk), (0, self.xr))):
            v.wait_ge(self.own, 2 + n)
            v.scalar_tensor_tensor(dst[:, :, 1:L], yT[:, :, 0:L - 1], self.omu[:, i:i + 1], dst[:, :, 1:L],
                                   ALU.mult, ALU.add).then_inc(self.mixed, 1)
        for f in range(2):
            v.wait_ge(self.kr_sb, f + 1)
            r = slice(f * BANK, f * BANK + BANK)
            v.tensor_tensor(self.ka[:, r], self.kr[:, r], self.kr[:, r], ALU.mult).then_inc(self.ka_sb, 1)
        for f in range(2):
            v.wait_ge(self.o_ps, f + 1)
            v.wait_ge(self.r_sb, f + 1)
            r = slice(4 * f, 4 * f + 4)
            v.tensor_tensor(self.t[:, r, :], self.r[:, r, :], PS[:, (0, 5)[f], :].rearrange("p (t d) -> p t d", t=4),
                            ALU.mult).then_inc(self.own, 1)
            v.wait_ge(self.own, 4 + f)
            v.tensor_tensor(self.k.x[:, r, :], self.k.x[:, r, :], self.t[:, r, :], ALU.add)

    def scalar(self, act):
        PS = self.k.PS
        for f in range(2):
            act.wait_ge(self.k_ps, f + 1)
            act.activation(self.kr[:, f * BANK:f * BANK + BANK], PS[:, 1 + f, :], ACT.Relu).then_inc(self.kr_sb, 1)
        for f in range(2):
            act.wait_ge(self.r_ps, f + 1)
            act.activation(self.r[:, 4 * f:4 * f + 4, :], PS[:, 3 + f, :].rearrange("p (t d) -> p t d", t=4), ACT.Sigmoid).then_inc(self.r_sb, 1)

class NarrowAttention:

    S, T, O, G = (0, 1), (2, 3), (4, 5), (6, 7)
    ROWS = D8 + 2
    QR = HEADS8 * REG

    def __init__(self, k, name, norm, by_class):
        self.yT_in = 2 * (norm + 1)
        self.k, self.name, self.by_class = k, name, by_class
        n = name + "_"
        self.keys = L if by_class else S2
        self.width = L if by_class else S2 // 4
        self.heads = BANK // self.width
        self.steps = QT * HEADS8 // self.heads
        self.kts = self.width // P
        self.w_in = k.sb(n + "w_in", [P, 4, P])
        self.bo = k.sb(n + "bo", [P, P])
        if by_class:
            self.g = k.sb(n + "g", [P, P])
        else:
            self.bqp = k.sb(n + "bq", [P, 4])
            self.bkp = k.sb(n + "bk", [P, 4])
            self.bv_in = k.sb(n + "bv_in", [P, P])
            self.mask = k.sb(n + "mask", [1, B * S2 // 4], U32)
        s = k.sem
        self.loaded = s(n + "weights_loaded")
        self.padded = s(n + "weights_padded")
        self.zeroed = s(n + "zeroed")
        self.batch_in = s(n + "batch_in")
        self.product = s(n + "product")
        self.by_v, self.by_a = s(n + "taken_by_vector"), s(n + "taken_by_scalar")
        self.sc, self.mx, self.ex, self.tr = s(n + "scores"), s(n + "max"), s(n + "probs"), s(n + "turned")
        self.pt_v, self.pt_a = s(n + "pT_even"), s(n + "pT_odd")
        self.av, self.iv, self.nm = s(n + "pv"), s(n + "inverse"), s(n + "normed")
        self.cls_sb = s(n + "classes_ready")
        if by_class:
            self.own, self.powed, self.reduced = s(n + "find_vector"), s(n + "powed"), s(n + "ends_reduced")
            self.qn_ps, self.c_ps = s(n + "q_natural"), s(n + "classes_turned")
            self.rmx, self.riv = s(n + "r_max_done"), s(n + "r_inverse")
            self.before, self.after = [("q", 0), ("q", 1), ("k", 0), ("k", 1), ("v", 0)], [("t", 1), ("o", 1)]
            self.during = {0: [("rq", 0)], 1: [("rs", 0)], 2: [("rt", 0)], 3: [("rp", 0)], 9: [("rm", 0), ("t", 0)], 10: [("o", 0)]}
        else:
            self.before, self.after = [("q", 0), ("q", 1)] + [("k", t) for t in range(4)] + [("v", 0)], [("t", 1), ("o", 1)]
            self.during = {5: [("t", 0)], 6: [("o", 0)]}
        uses = self.before + [u for n in sorted(self.during) for u in self.during[n]] + self.after
        self.uses = uses
        self.bank = {u: self.G[i % 2] for i, u in enumerate(uses)}
        self.previous = {u: uses[i - 2] for i, u in enumerate(uses) if i >= 2}
        by_scalar = ("k", "rs", "rt", "t")
        self.a_uses = [u for u in uses if u[0] in by_scalar]
        self.v_uses = [u for u in uses if u[0] not in by_scalar]

    def place(self):
        k, by_class, n = self.k, self.by_class, self.name + "_"
        self.wq = k.lb(n + "wq", [P, 4 * P])
        self.wk = k.lb(n + "wk", [P, 4 * P])
        self.qp = k.lb(n + "q", [P, 4, L])
        self.kp = k.lb(n + "k", [P, 4, self.keys])
        self.v = k.lb(n + "v", [P, self.kts if by_class else 4, P if by_class else 32])
        self.yb = k.lb(n + "y_of_batch", [P, L])
        self.cqb = k.lb(n + "cq_of_batch", [2, L])
        self.ckb = k.lb(n + "ck_of_batch", [2, self.keys])
        self.ck = k.lb(n + "ck", [2, B * self.keys])
        self.probs = k.lb(n + "probs", [P, 2, BANK])
        self.pT = k.lb(n + "pT", [P, 2, BANK])
        self.nmax = k.lb(n + "nmax", [P, 2, self.heads])
        self.sums = k.lb(n + "sums", [P, QT, HEADS8])
        self.inv = k.lb(n + "inv", [P, QT, HEADS8])
        self.att = k.lb(n + "att", [P, QT, P])
        self.attT = k.lb(n + "attT", [P, QT, P])
        if by_class:
            self.cq = k.lb(n + "cq", [2, B * L])
            self.gn = k.lb(n + "gn", [P, HEADS8])
            self.prod = k.lb(n + "prod", [P, TILES, P])
            self.ss = k.lb(n + "ss", [P, TILES * HEADS8])
            self.dots = k.lb(n + "dots", [P, TILES * HEADS8])
            self.sim = k.lb(n + "sim", [P, TILES])
            self.ends = k.lb(n + "ends", [P, 2, TILES])
            self.ends_p = k.lb(n + "ends_of_partition", [P, 2])
            self.ends_all = k.lb(n + "ends_all", [P, 2])
            self.span = k.lb(n + "span", [P, 1])
            self.cls = k.lb(n + "cls", [P, TILES, 4])
            self.qbd = k.lb(n + "q_registers", [P, 4, HEADS8, REG])
            self.rmax = k.lb(n + "r_max", [P, 1])
            self.rsum = k.lb(n + "r_sum", [P, 1])
            self.rinv = k.lb(n + "r_inv", [P, 1])
            self.rprobs = k.lb(n + "r_probs", [P, L])
            self.rpT = k.lb(n + "r_pT", [P, 2 * self.QR])
            self.ratt = k.lb(n + "r_att", [P, P])
        else:
            self.bv = k.lb(n + "bv", [P, 4 * 32])
            self.wv = k.lb(n + "wv", [P, P])
            self.cb = k.lb(n + "ctx_of_batch", [P, S2])

    def wait_product(self, eng, u, it):
        eng.wait_ge(self.product, it * len(self.uses) + self.uses.index(u) + 1)

    def wait_taken(self, eng, u, it):
        if u in self.a_uses:
            eng.wait_ge(self.by_a, it * len(self.a_uses) + self.a_uses.index(u) + 1)
        else:
            eng.wait_ge(self.by_v, it * len(self.v_uses) + self.v_uses.index(u) + 2)

    def where(self, n):
        per = self.steps // QT
        qt, r = n // per, n % per
        return qt, r % 4, range(self.heads * (r // 4), self.heads * (r // 4) + self.heads)

    def load(self, sp, wq, wk, wv, wo, bo, bq=None, bk=None, bv=None, mask=None, g=None):
        for i, w in enumerate((wq, wk, wv, wo)):
            sp.dma_start(self.w_in[:, i, :], w).then_inc(self.loaded, 16)
        sp.dma_start(self.bo[:, :], bo.unsqueeze(0).to_broadcast((P, P))).then_inc(self.loaded, 16)
        if self.by_class:
            sp.dma_start(self.g[:, :], g.unsqueeze(0).to_broadcast((P, P))).then_inc(self.loaded, 16)
            self.n_loads = 6 * 16
        else:
            sp.dma_start(self.bv_in[:, :], bv.unsqueeze(0).to_broadcast((P, P))).then_inc(self.loaded, 16)
            sp.dma_start(self.mask[:, :], mask.rearrange("(o b) s -> o (b s)", o=1)).then_inc(self.loaded, 16)
            sp.wait_ge(self.zeroed, 2)
            for dst, b in ((self.bqp, bq), (self.bkp, bk)):
                for gr in range(4):
                    sp.dma_start(dst[32 * gr:32 * gr + D8, :], b.rearrange("(t g e) -> g e t", t=4, g=4)[gr]).then_inc(self.loaded, 16)
            self.n_loads = 15 * 16

    def pool_zero(self, pool):
        if not self.by_class:
            pool.memset(self.bqp[:, :], 0.0).then_inc(self.zeroed, 1)
            pool.memset(self.bkp[:, :], 0.0).then_inc(self.zeroed, 1)

    def pool_pad(self, pool):
        pool.memset(self.wq[:, :], 0.0).then_inc(self.zeroed, 1)
        pool.memset(self.wk[:, :], 0.0).then_inc(self.zeroed, 1)
        if not self.by_class:
            pool.memset(self.cqb[:, :], 1.0)
            pool.memset(self.ck[:, :], 0.0).then_inc(self.zeroed, 1)
        pool.wait_ge(self.loaded, self.n_loads)
        pool.wait_ge(self.zeroed, 2 if self.by_class else 5)
        for i, w in ((0, self.wq), (1, self.wk)):
            pool.tensor_copy(w[:, :].rearrange("p (h e) -> p h e", e=32)[:, :, 0:D8],
                             self.w_in[:, i, :].rearrange("p (h e) -> p h e", e=D8)).then_inc(self.padded, 1)
        if not self.by_class:
            for dst, src in ((self.wv, self.w_in[:, 2, :]), (self.bv, self.bv_in[:, :])):
                pool.tensor_copy(dst[:, :].rearrange("p (g t e) -> p g t e", g=4, t=4),
                                 src.rearrange("p (t g e) -> p g t e", g=4, t=4)).then_inc(self.padded, 1)

    def pool_batches(self, pool):
        pool.wait_ge(self.cls_sb, 2)
        pool.wait_ge(self.k.ln.s_yT, self.yT_in)

        def bring(at):
            pool.tensor_copy(self.yb[:, :], self.k.yT[:, ds(at * L, L)])
            if self.by_class:
                pool.tensor_copy(self.cqb[:, :], self.cq[:, ds(at * L, L)])
            else:
                pool.tensor_copy(self.cb[:, :], self.k.ctxT[:, ds(at, 1), :].rearrange("p a s -> p (a s)"))
            pool.tensor_copy(self.ckb[:, :], self.ck[:, ds(at * self.keys, self.keys)]).then_inc(self.batch_in, 1)

        bring(0)
        with pool.Fori(0, B - 1) as it:
            self.wait_product(pool, ("rq", 0) if self.by_class else ("v", 0), it)
            bring(it + 1)

    def pool_find(self, pool):
        pool.wait_ge(self.own, 2)
        pool.tensor_tensor(self.gn[:, :], self.gn[:, :], self.k.ln.half[:, 0:HEADS8], ALU.pow).then_inc(self.powed, 1)
        pool.wait_ge(self.own, 6)
        pool.tensor_tensor(self.ss[:, :], self.ss[:, :], self.k.ln.half[:, :], ALU.pow).then_inc(self.powed, 1)
        pool.wait_ge(self.own, 13)
        pool.partition_all_reduce(self.ends_all[:, :], self.ends_p[:, :], P, RMAX).then_inc(self.reduced, 1)

    def vector_find(self, v):
        cst = self.k.cst
        reg = cst[:, C_REG:C_REG + TILES]
        heads = lambda a: a.rearrange("p (h e) -> p h e", e=D8)
        v.wait_ge(self.loaded, self.n_loads)
        v.tensor_tensor(self.prod[:, 0, :], self.g[:, :], self.g[:, :], ALU.mult).then_inc(self.own, 1)
        v.wait_ge(self.own, 1)
        v.tensor_reduce(self.gn[:, :], heads(self.prod[:, 0, :]), AX.X, ALU.add).then_inc(self.own, 1)
        v.wait_ge(self.powed, 1)
        v.wait_ge(self.own, 2)
        v.tensor_tensor(heads(self.g[:, :]), heads(self.g[:, :]), self.gn[:, :].unsqueeze(2).to_broadcast((P, HEADS8, D8)),
                        ALU.mult).then_inc(self.own, 1)
        v.wait_ge(self.qn_ps, 1)
        qn = self.k.PS[:, 0:2, :].rearrange("p f (t d) -> p (f t) d", d=P)
        v.tensor_copy(self.prod[:, :, :], qn).then_inc(self.own, 1)
        v.wait_ge(self.own, 4)
        v.tensor_tensor(self.prod[:, :, :], self.prod[:, :, :], qn, ALU.mult).then_inc(self.own, 1)
        v.wait_ge(self.own, 5)
        flat = self.prod[:, :, :].rearrange("p t (h e) -> p (t h) e", e=D8)
        v.tensor_reduce(self.ss[:, :], flat, AX.X, ALU.add).then_inc(self.own, 1)
        v.wait_ge(self.own, 6)
        v.tensor_tensor(self.prod[:, :, :], qn, self.g[:, :].unsqueeze(1).to_broadcast((P, TILES, P)), ALU.mult).then_inc(self.own, 1)
        v.wait_ge(self.own, 7)
        v.tensor_reduce(self.dots[:, :], flat, AX.X, ALU.add).then_inc(self.own, 1)
        v.wait_ge(self.own, 8)
        v.wait_ge(self.powed, 2)
        v.tensor_tensor(self.dots[:, :], self.dots[:, :], self.ss[:, :], ALU.mult).then_inc(self.own, 1)
        v.wait_ge(self.own, 9)
        v.tensor_reduce(self.sim[:, :], self.dots[:, :].rearrange("p (t h) -> p t h", h=HEADS8), AX.X, ALU.add).then_inc(self.own, 1)
        v.wait_ge(self.own, 10)
        v.scalar_tensor_tensor(self.ends[:, 0, :], reg, -BIG, self.sim[:, :], ALU.mult, ALU.add).then_inc(self.own, 1)
        v.scalar_tensor_tensor(self.ends[:, 1, :], reg, -BIG, self.sim[:, :], ALU.mult, ALU.subtract).then_inc(self.own, 1)
        v.wait_ge(self.own, 12)
        v.tensor_reduce(self.ends_p[:, :], self.ends[:, :, :], AX.X, ALU.max).then_inc(self.own, 1)
        v.wait_ge(self.reduced, 1)
        v.tensor_tensor(self.span[:, :], self.ends_all[:, 0:1], self.ends_all[:, 1:2], ALU.add).then_inc(self.own, 1)
        v.wait_ge(self.own, 14)
        v.reciprocal(self.span[:, :], self.span[:, :]).then_inc(self.own, 1)
        v.wait_ge(self.own, 15)
        v.tensor_scalar(self.sim[:, :], self.sim[:, :], self.ends_all[:, 1:2], self.span[:, 0:1], ALU.add, ALU.mult).then_inc(self.own, 1)
        v.wait_ge(self.own, 16)
        c = self.cls
        v.scalar_tensor_tensor(c[:, :, 0], self.sim[:, :], 0.9, reg, ALU.is_gt, ALU.max).then_inc(self.own, 1)
        v.wait_ge(self.own, 17)
        v.tensor_scalar(c[:, :, 1], c[:, :, 0], -1.0, 1.0, ALU.mult, ALU.add).then_inc(self.own, 1)
        v.tensor_tensor(c[:, :, 3], reg, c[:, :, 0], ALU.subtract).then_inc(self.own, 1)
        v.wait_ge(self.own, 19)
        v.tensor_scalar(c[:, :, 2], c[:, :, 1], -BIG, None, ALU.mult).then_inc(self.own, 1)
        v.tensor_scalar(c[:, :, 3], c[:, :, 3], BIG, None, ALU.mult).then_inc(self.own, 1)
        v.wait_ge(self.c_ps, 1)
        for dst, bank in ((self.cq, 2), (self.ck, 4)):
            v.tensor_copy(dst[:, :].rearrange("p (f c) -> p f c", f=2), self.k.PS[0:2, bank:bank + 2, :]).then_inc(self.cls_sb, 1)

    def vector_padding(self, v):
        v.wait_ge(self.loaded, self.n_loads)
        v.wait_ge(self.zeroed, 5)
        v.tensor_scalar(self.ck[0:1, :], self.mask[:, :].bitcast(U8), -BIG, None, ALU.mult).then_inc(self.cls_sb, 2)

    def vector(self, v):
        PS, cst, x = self.k.PS, self.k.cst, self.k.x
        v.wait_ge(self.loaded, self.n_loads)
        v.tensor_tensor(x[:, :, :], x[:, :, :], self.bo[:, :].unsqueeze(1).to_broadcast((P, TILES, P)), ALU.add).then_inc(self.by_v, 1)
        if not self.by_class:
            v.wait_ge(self.padded, 4)

        def take(u, it):
            kind, i = u
            bank = PS[:, self.bank[u], :]
            self.wait_product(v, u, it)
            if kind == "q":
                if self.by_class:
                    v.tensor_scalar(self.qp[:, 2 * i:2 * i + 2, :], bank.rearrange("p (t l) -> p t l", t=2), SCALE8, None,
                                    ALU.mult).then_inc(self.by_v, 1)
                else:
                    for t in (2 * i, 2 * i + 1):
                        ins = v.tensor_scalar(self.qp[:, t, :], bank[:, (t % 2) * L:(t % 2) * L + L], self.bqp[:, t:t + 1], SCALE8,
                                              ALU.add, ALU.mult)
                    ins.then_inc(self.by_v, 1)
            elif kind == "v":
                if self.by_class:
                    v.tensor_copy(self.v[:, :, :], bank[:, 0:L].rearrange("p (t d) -> p t d", t=2)).then_inc(self.by_v, 1)
                else:
                    v.tensor_tensor(self.v[:, :, :].rearrange("p g c -> p (g c)"), bank[:, 0:P], self.bv[:, :], ALU.add).then_inc(self.by_v, 1)
            elif kind == "rq":
                v.tensor_tensor(self.qbd[:, :, :, :],
                                bank[:, 0:4 * REG].rearrange("p (t i) -> p t i", t=4).unsqueeze(2).to_broadcast((P, 4, HEADS8, REG)),
                                cst[:, C_OWN:C_OWN + 64].rearrange("p (t h) -> p t h", t=4).unsqueeze(3).to_broadcast((P, 4, HEADS8, REG)),
                                ALU.mult).then_inc(self.by_v, 1)
            elif kind == "rp":
                v.reciprocal(self.rinv[0:self.QR, :], self.rsum[0:self.QR, :]).then_inc(self.riv, 1)
                v.wait_ge(self.riv, it + 1)
                v.scalar_tensor_tensor(self.ratt[0:self.QR, :], bank[0:self.QR, 0:P], self.rinv[0:self.QR, 0:1],
                                       cst[0:self.QR, C_DIAG:C_DIAG + P], ALU.mult, ALU.mult).then_inc(self.by_v, 1)
            elif kind == "rm":
                self.wait_taken(v, ("t", 0), it)
                v.scalar_tensor_tensor(self.attT[:, 0, 0:REG], self.attT[:, 0, 0:REG], 0.5, bank[:, 0:REG], ALU.mult, ALU.add).then_inc(self.by_v, 1)
            else:
                row = x[:, ds(it * 2 + i, 1), :].rearrange("p a d -> p (a d)")
                v.tensor_tensor(row, row, bank[:, 0:P], ALU.add).then_inc(self.by_v, 1)

        def maximum(n, it):
            v.wait_ge(self.sc, it * self.steps + n + 1)
            v.tensor_reduce(self.nmax[:, n % 2, :], PS[:, self.S[n % 2], :].rearrange("p (j s) -> p j s", j=self.heads), AX.X, ALU.max,
                            negate=True).then_inc(self.mx, 1)

        per = self.steps // QT
        with v.Fori(0, B) as it:
            for u in self.before:
                if u in self.v_uses:
                    take(u, it)
            for n in range(-2, self.steps + 1):
                if 0 <= n < self.steps and n % 2 == 0:
                    v.wait_ge(self.tr, it * self.steps + n + 1)
                    v.tensor_copy(self.pT[:, 0, :], PS[:, self.T[0], :]).then_inc(self.pt_v, 1)
                if n + 2 < self.steps:
                    maximum(n + 2, it)
                if n >= per and n % per == 0:
                    qt = n // per - 1
                    v.wait_ge(self.av, it * self.steps + n)
                    v.reciprocal(self.inv[:, qt, :], self.sums[:, qt, :]).then_inc(self.iv, 1)
                    v.wait_ge(self.iv, it * QT + qt + 1)
                    v.tensor_tensor(self.att[:, qt, :].rearrange("p (h e) -> p h e", e=D8), PS[:, self.O[qt], 0:P].rearrange("p (h e) -> p h e", e=D8),
                                    self.inv[:, qt, :].unsqueeze(2).to_broadcast((P, HEADS8, D8)), ALU.mult).then_inc(self.nm, 1)
                for u in self.during.get(n, []):
                    if u == ("rs", 0):
                        self.wait_product(v, u, it)
                        v.tensor_reduce(self.rmax[0:self.QR, :], PS[0:self.QR, self.bank[u], 0:L], AX.X, ALU.max, negate=True).then_inc(self.rmx, 1)
                    elif u in self.v_uses:
                        take(u, it)
            for u in self.after:
                if u in self.v_uses:
                    take(u, it)

    def scalar(self, act):
        PS = self.k.PS

        def take(u, it):
            kind, i = u
            bank = PS[:, self.bank[u], :]
            self.wait_product(act, u, it)
            if kind == "k":
                if self.by_class:
                    act.copy(self.kp[:, 2 * i:2 * i + 2, :], bank.rearrange("p (t l) -> p t l", t=2)).then_inc(self.by_a, 1)
                else:
                    act.activation(self.kp[:, i, :], bank, ACT.Identity, bias=self.bkp[:, i:i + 1]).then_inc(self.by_a, 1)
            elif kind == "rs":
                act.wait_ge(self.rmx, it + 1)
                act.activation(self.rprobs[0:self.QR, :], bank[0:self.QR, 0:L], ACT.Exp, bias=self.rmax[0:self.QR, 0:1],
                               accum_out=self.rsum[0:self.QR, :]).then_inc(self.by_a, 1)
            elif kind == "rt":
                act.copy(self.rpT[:, :], bank[:, 0:2 * self.QR]).then_inc(self.by_a, 1)
            else:
                act.copy(self.attT[:, i, :], bank[:, 0:P]).then_inc(self.by_a, 1)

        def exponent(n, it):
            act.wait_ge(self.mx, it * self.steps + n + 1)
            if n >= 2:
                act.wait_ge(self.tr, it * self.steps + n - 1)
            qt, g, quads = self.where(n)
            for j, t in enumerate(quads):
                h = 4 * t + g
                cols = slice(j * self.width, j * self.width + self.width)
                ins = act.activation(self.probs[:, n % 2, cols], PS[:, self.S[n % 2], cols], ACT.Exp, bias=self.nmax[:, n % 2, j:j + 1],
                                     accum_out=self.sums[:, qt, h:h + 1])
            ins.then_inc(self.ex, 1)

        with act.Fori(0, B) as it:
            for u in self.before:
                if u in self.a_uses:
                    take(u, it)
            for n in range(-2, self.steps + 1):
                if 0 <= n < self.steps and n % 2 == 1:
                    act.wait_ge(self.tr, it * self.steps + n + 1)
                    act.copy(self.pT[:, 1, :], PS[:, self.T[1], :]).then_inc(self.pt_a, 1)
                if n + 2 < self.steps:
                    exponent(n + 2, it)
                for u in self.during.get(n, []):
                    if u in self.a_uses:
                        take(u, it)
            for u in self.after:
                if u in self.a_uses:
                    take(u, it)

    def tensor_find(self, pe):
        PS = self.k.PS
        pe.wait_ge(self.loaded, self.n_loads)
        pe.wait_ge(self.k.ln.s_yT, self.yT_in)
        for t in range(TILES):
            mm = pe.matmul(PS[:, t // 4, (t % 4) * P:(t % 4) * P + P], self.k.yT[:, t * P:t * P + P], self.w_in[:, 0, :], start=True, stop=True)
        mm.then_inc(self.qn_ps, 1)
        pe.wait_ge(self.own, 21)
        for side, bank in ((0, 2), (2, 4)):
            for t in range(TILES):
                mm = pe.transpose(PS[0:2, bank + t // 4, (t % 4) * P:(t % 4) * P + P], self.cls[:, t, side:side + 2], self.k.ident)
        mm.then_inc(self.c_ps, 1)

    def tensor(self, pe):
        PS, cst, ident = self.k.PS, self.k.cst, self.k.ident
        pe.wait_ge(self.padded, 2 if self.by_class else 4)
        pe.wait_ge(self.cls_sb, 2)
        src = self.yb if self.by_class else self.cb
        classes = cst[0:2, C_CLASS:C_CLASS + P]

        def product(u, it):
            kind, i = u
            bank = PS[:, self.bank[u], :]
            if u in self.previous:
                self.wait_taken(pe, self.previous[u], it)
            if kind == "q":
                for t in (2 * i, 2 * i + 1):
                    out = bank[:, (t % 2) * L:(t % 2) * L + L]
                    pe.matmul(out, self.wq[:, t * P:t * P + P], self.yb[:, :], start=True, stop=False)
                    mm = pe.matmul(out, classes, self.cqb[:, :], start=False, stop=True)
            elif kind == "k":
                for t in ((2 * i, 2 * i + 1) if self.by_class else (i,)):
                    out = bank[:, (t % 2) * L:(t % 2) * L + L] if self.by_class else bank
                    pe.matmul(out, self.wk[:, t * P:t * P + P], src[:, :], start=True, stop=False)
                    mm = pe.matmul(out, classes, self.ckb[:, :], start=False, stop=True)
            elif kind == "v":
                for j in range(self.kts if self.by_class else 4):
                    if self.by_class:
                        mm = pe.matmul(bank[:, j * P:j * P + P], src[:, j * P:j * P + P], self.w_in[:, 2, :], start=True, stop=True)
                    else:
                        mm = pe.matmul(bank[:, j * 32:j * 32 + 32], src[:, j::4], self.wv[:, j * 32:j * 32 + 32], start=True, stop=True)
            elif kind == "rq":
                for t in range(4):
                    pe.matmul(bank[:, t * REG:t * REG + REG], self.wq[:, t * P:t * P + P], self.yb[:, 0:REG], start=True, stop=False)
                    mm = pe.matmul(bank[:, t * REG:t * REG + REG], classes, cst[0:2, C_NEG:C_NEG + REG], start=False, stop=True)
            elif kind == "rs":
                self.wait_taken(pe, ("rq", 0), it)
                for t in range(4):
                    mm = pe.matmul(bank[0:self.QR, 0:L], self.qbd[:, t, :, :].rearrange("p h i -> p (h i)"), self.kp[:, t, :],
                                   start=(t == 0), stop=(t == 3))
            elif kind == "rt":
                self.wait_taken(pe, ("rs", 0), it)
                for kt in range(2):
                    mm = pe.transpose(bank[:, kt * self.QR:kt * self.QR + self.QR], self.rprobs[0:self.QR, kt * P:kt * P + P],
                                      ident[0:self.QR, 0:self.QR])
            elif kind == "rp":
                self.wait_taken(pe, ("rt", 0), it)
                for kt in range(2):
                    mm = pe.matmul(bank[0:self.QR, 0:P], self.rpT[:, kt * self.QR:kt * self.QR + self.QR], self.v[:, kt, :],
                                   start=(kt == 0), stop=(kt == 1))
            elif kind == "rm":
                self.wait_taken(pe, ("rp", 0), it)
                mm = pe.matmul(bank[:, 0:REG], self.ratt[0:self.QR, :], cst[0:self.QR, C_SUM:C_SUM + REG], start=True, stop=True)
            elif kind == "t":
                pe.wait_ge(self.nm, it * QT + i + 1)
                mm = pe.transpose(bank[:, 0:P], self.att[:, i, :], ident)
            else:
                self.wait_taken(pe, ("t", i), it)
                if self.by_class and i == 0:
                    self.wait_taken(pe, ("rm", 0), it)
                mm = pe.matmul(bank[:, 0:P], self.attT[:, i, :], self.w_in[:, 3, :], start=True, stop=True)
            mm.then_inc(self.product, 1)

        def scores(n, it):
            if n == 0:
                self.wait_taken(pe, self.before[-2], it)
                self.wait_taken(pe, ("q", 1), it)
            if n >= 2:
                pe.wait_ge(self.ex, it * self.steps + n - 1)
            qt, g, quads = self.where(n)
            rows = slice(32 * g, 32 * g + self.ROWS)
            for j, t in enumerate(quads):
                keys = self.kp[rows, t, :] if self.by_class else self.kp[rows, t, g::4]
                mm = pe.matmul(PS[:, self.S[n % 2], j * self.width:j * self.width + self.width], self.qp[rows, t, qt * P:qt * P + P], keys,
                               start=True, stop=True)
            mm.then_inc(self.sc, 1)

        def turn(n, it):
            pe.wait_ge(self.ex, it * self.steps + n + 1)
            if n >= 2:
                pe.wait_ge(self.pt_a if n % 2 else self.pt_v, it * (self.steps // 2) + n // 2)
            for j in range(BANK // P):
                mm = pe.transpose(PS[:, self.T[n % 2], j * P:j * P + P], self.probs[:, n % 2, j * P:j * P + P], ident)
            mm.then_inc(self.tr, 1)

        def times_v(n, it):
            if n == 0:
                self.wait_taken(pe, ("v", 0), it)
            pe.wait_ge(self.pt_a if n % 2 else self.pt_v, it * (self.steps // 2) + n // 2 + 1)
            qt, g, quads = self.where(n)
            for j, t in enumerate(quads):
                h = 4 * t + g
                for kt in range(self.kts):
                    vals = self.v[:, kt, D8 * h:D8 * h + D8] if self.by_class else self.v[:, g, D8 * t:D8 * t + D8]
                    mm = pe.matmul(PS[:, self.O[qt], D8 * h:D8 * h + D8],
                                   self.pT[:, n % 2, (j * self.kts + kt) * P:(j * self.kts + kt) * P + P], vals,
                                   start=(kt == 0), stop=(kt == self.kts - 1))
            mm.then_inc(self.av, 1)

        with pe.Fori(0, B) as it:
            pe.wait_ge(self.batch_in, it + 1)
            pe.wait_ge(self.by_v, it * len(self.v_uses) + 1)
            for u in self.before:
                product(u, it)
            for n in range(-2, self.steps + 1):
                if 0 <= n < self.steps:
                    turn(n, it)
                if n + 2 < self.steps:
                    scores(n + 2, it)
                if n >= 1:
                    times_v(n - 1, it)
                for u in self.during.get(n, []):
                    product(u, it)
            for u in self.after:
                product(u, it)

class Warping:

    LANES, E = S2 // 32, 32
    HAND = 2
    COLS = 32
    HALF = COLS // 2
    SLOTS = L + LANES * HAND
    ROUNDS = SLOTS // COLS
    ROW = 2 * (E + 1) + 2 * E + 1

    def __init__(self, k, norm):
        self.yT_in = 2 * (norm + 1)
        self.k = k
        E, SLOTS, COLS, LANES = self.E, self.SLOTS, self.COLS, self.LANES
        self.DL = k.lb("w_distances", [P, SLOTS + self.HALF, E])
        self.CUT = k.lb("w_up_table", [P, SLOTS, 66], BF16)
        self.MH = k.lb("w_path", [P, SLOTS, E], BF16)
        self.aa = k.lb("w_aa", [P, LANES])
        self.tick = k.lb("w_tick", [P, 1])
        self.bb = k.lb("w_bb", [P, L])

        def phase(*buffers):
            with ExitStack() as place:
                return [place.enter_context(k.nc.sbuf_tensor("w_" + n, s, d)) for n, s, d in buffers]

        self.sq, self.d2, self.ones = phase(("squares", [P, 2048], F32), ("d2", [P, 2, 2, L], F32), ("ones", [P, 32], F32))
        self.DLr, self.Dr, self.R, self.Mn, self.An, self.Gt, self.Lr, self.Ur, self.Tr = phase(
            ("d_ring_in", [P, COLS, E], F32), ("d_ring", [P, COLS, E], F32), ("R", [P, COLS + 1, E + 1], F32), ("min", [P, E], F32),
            ("min2", [P, 2, E], F32), ("gt2", [P, 2, E], F32), ("left", [P, COLS, E], BF16), ("up", [P, COLS, E], BF16),
            ("left_or_up", [P, COLS, E], BF16))
        self.CB, self.CTr, self.CUr = phase(("flags", [P, COLS, self.ROW], F32), ("table_ring", [P, COLS, E, 2], BF16),
                                            ("up_ring", [P, COLS, 2 * E], BF16))
        self.MF, = phase(("mask", [P, LANES, L], F32))
        self.CT = self.DL[:, 0:SLOTS, :].bitcast(BF16).rearrange("p s (e k) -> p s e k", k=2)
        self.MT = self.DL[:, 0:SLOTS // 2, :].bitcast(BF16).rearrange("p s (h e) -> p (s h) e", h=2)
        s = k.sem
        self.zeroed, self.sq_done = s("w_zeroed"), s("w_squares_done")
        self.bb_ps, self.bb_sb = s("w_bb_product"), s("w_bb_ready")
        self.ab_ps, self.d2_done, self.dist_done, self.root_done = s("w_ab_product"), s("w_d2_done"), s("w_clamped"), s("w_root_done")
        self.dve = s("w_column_chain")
        self.dl_in, self.dl_used, self.choices, self.sums, self.tables = (
            s("w_d_ring_in"), s("w_d_ring_used"), s("w_choices"), s("w_left_or_up"), s("w_tables_saved"))
        self.fwd0, self.tab_in, self.half_done = s("w_path_started"), s("w_tables_in"), s("w_half_done")
        self.mt_done, self.mf_v, self.mf_a, self.ex_ps = s("w_mask_turned"), s("w_mask_even"), s("w_mask_odd"), s("w_expanded")

    def pool_before(self, pool):
        pool.memset(self.DL[:, :, :], 0.0).then_inc(self.zeroed, 1)
        pool.memset(self.CUT[:, :, :], 1.0)
        pool.memset(self.ones[:, :], 1.0).then_inc(self.zeroed, 1)
        pool.wait_ge(self.zeroed, 2)
        pool.memset(self.DL[:, self.HAND - 1, 0:1], BIG).then_inc(self.zeroed, 1)

    def pool_forward(self, pool):
        with pool.Fori(0, self.ROUNDS) as it:
            for h in range(2):
                pool.wait_ge(self.choices, it * 2 + h + 1)
                r = slice(self.HALF * h, self.HALF * h + self.HALF)
                pool.tensor_tensor(self.Tr[:, r, :], self.Lr[:, r, :], self.Ur[:, r, :], ALU.add).then_inc(self.sums, 1)

    def tensor_distances(self, pe):
        PS, k, E = self.k.PS, self.k, self.E
        pe.wait_ge(self.sq_done, 1)
        pe.wait_ge(self.zeroed, 2)
        for b in range(B):
            mm = pe.matmul(PS[32 * b:32 * b + 32, 7, 0:L], self.ones[:, :], self.sq[:, b * L:b * L + L], start=True, stop=True)
        mm.then_inc(self.bb_ps, 1)
        for h in range(self.LANES // 2):
            if h >= 2:
                pe.wait_ge(self.d2_done, h - 1)
            for p in (2 * h, 2 * h + 1):
                for b in range(B):
                    mm = pe.matmul(PS[32 * b:32 * b + 32, h % 2, (p % 2) * L:(p % 2) * L + L],
                                   k.ctxT[:, b, E * p:E * p + E], k.yT[:, b * L:b * L + L], start=True, stop=True)
            mm.then_inc(self.ab_ps, 1)

    def tensor_expand(self, pe):
        PS = self.k.PS
        for jt in range(QT):
            for p in range(self.LANES):
                pe.wait_ge(self.mf_a if p % 2 else self.mf_v, jt * self.LANES // 2 + p // 2 + 1)
                for b in range(B):
                    mm = pe.matmul(PS[:, b, jt * D:jt * D + D], self.MF[32 * b:32 * b + 32, p, jt * P:jt * P + P],
                                   self.k.ctxP[32 * b:32 * b + 32, p, :], start=(p == 0), stop=(p == self.LANES - 1))
        mm.then_inc(self.ex_ps, 1)

    def scalar_distances(self, act):
        act.wait_ge(self.k.ln.s_yT, self.yT_in)
        act.activation(self.sq[:, 0:B * L], self.k.yT[:, :], ACT.Square).then_inc(self.sq_done, 1)
        act.wait_ge(self.zeroed, 3)
        for h in range(self.LANES // 2):
            for p in (2 * h, 2 * h + 1):
                act.wait_ge(self.dist_done, p + 1)
                act.activation(self.DL[:, self.HAND * (p + 1):self.HAND * (p + 1) + L, p], self.d2[:, h % 2, p % 2, :],
                               ACT.Sqrt).then_inc(self.root_done, 1)

    def scalar_forward(self, act):
        HALF, COLS = self.HALF, self.COLS
        act.copy(self.DLr[:, 0:HALF, :], self.DL[:, 0:HALF, :]).then_inc(self.dl_in, 1)
        with act.Fori(0, self.ROUNDS) as it:
            act.wait_ge(self.dl_used, it * 2 + 1)
            act.copy(self.DLr[:, HALF:COLS, :], self.DL[:, ds(it * COLS + HALF, HALF), :]).then_inc(self.dl_in, 1)
            act.copy(self.DLr[:, 0:HALF, :], self.DL[:, ds(it * COLS + COLS, HALF), :]).then_inc(self.dl_in, 1)
            for h in range(2):
                act.wait_ge(self.sums, it * 2 + h + 1)
                r = slice(HALF * h, HALF * h + HALF)
                slots = ds(it * COLS + HALF * h, HALF)
                act.activation(self.CT[:, slots, :, 0], self.Tr[:, r, :], ACT.Copy, bias=1.0, scale=-1.0)
                act.activation(self.CT[:, slots, :, 1], self.Lr[:, r, :], ACT.Copy)
                act.activation(self.CUT[:, slots, 1:65:2], self.Ur[:, r, :], ACT.Copy).then_inc(self.tables, 1)

    def scalar_backward(self, act):
        HALF, COLS, SLOTS = self.HALF, self.COLS, self.SLOTS
        act.wait_ge(self.fwd0, 1)

        def load_tables(slot, half):
            r = slice(HALF * half, HALF * half + HALF)
            act.copy(self.CTr[:, r, :, :], self.CT[:, ds(slot, HALF), :, :])
            act.copy(self.CUr[:, r, :], self.CUT[:, ds(slot, HALF), 2:66]).then_inc(self.tab_in, 1)

        def backward_round(it, last):
            for half in (1, 0):
                slot = SLOTS - COLS + HALF * half - it * COLS
                act.wait_ge(self.half_done, it * 2 + 2 - half)
                act.copy(self.MH[:, ds(slot, HALF), :], self.CB[:, HALF * half:HALF * half + HALF, 66:130:2])
                if not last:
                    load_tables(slot - COLS, half)

        load_tables(SLOTS - HALF, 1)
        load_tables(SLOTS - COLS, 0)
        with act.Fori(0, self.ROUNDS - 1) as it:
            backward_round(it, False)
        backward_round(self.ROUNDS - 1, True)

    def take_mask(self, eng, copy, jt, p, done):
        copy(self.MF[:, p, jt * P:jt * P + P],
             self.MT[:, self.HAND * (p + 1) + jt * P:self.HAND * (p + 1) + jt * P + P, p]).then_inc(done, 1)

    def scalar_expand(self, act):
        act.wait_ge(self.mt_done, 4)
        for jt in range(QT):
            for p in range(1, self.LANES, 2):
                self.take_mask(act, act.copy, jt, p, self.mf_a)

    def vector_distances(self, v):
        PS, k, ctxP = self.k.PS, self.k, self.k.ctxP[:, :, :].rearrange("p a d -> p (a d)")
        v.wait_ge(self.bb_ps, 1)
        v.tensor_copy(self.bb[:, :], PS[:, 7, 0:L]).then_inc(self.bb_sb, 1)
        v.wait_ge(self.bb_sb, 1)
        v.tensor_tensor(self.sq[:, :], ctxP, ctxP, ALU.mult).then_inc(self.bb_sb, 1)
        v.wait_ge(self.bb_sb, 2)
        v.tensor_reduce(self.aa[:, :], self.sq[:, :].rearrange("p (a d) -> p a d", d=D), AX.X, ALU.add).then_inc(self.bb_sb, 1)
        v.wait_ge(self.bb_sb, 3)
        for h in range(self.LANES // 2):
            v.wait_ge(self.ab_ps, h + 1)
            if h >= 2:
                v.wait_ge(self.root_done, 2 * h - 2)
            v.scalar_tensor_tensor(self.d2[:, h % 2, :, :], PS[:, h % 2, :].rearrange("p (a l) -> p a l", a=2), -2.0,
                                   self.bb[:, :].unsqueeze(1).to_broadcast((P, 2, L)), ALU.mult, ALU.add).then_inc(self.d2_done, 1)
            v.wait_ge(self.d2_done, h + 1)
            for p in (2 * h, 2 * h + 1):
                v.tensor_scalar(self.d2[:, h % 2, p % 2, :], self.d2[:, h % 2, p % 2, :], self.aa[:, p:p + 1], 0.0,
                                ALU.add, ALU.max).then_inc(self.dist_done, 1)

    def vector_forward(self, v):
        E, COLS, HALF, HAND, LANES, R = self.E, self.COLS, self.HALF, self.HAND, self.LANES, self.R
        Lr, Ur, An, Gt, Mn, dve = self.Lr, self.Ur, self.An, self.Gt, self.Mn, self.dve
        v.memset(R[:, :, :], BIG).then_inc(dve, 1)
        v.memset(Lr[:, :, :], 0.0).then_inc(self.tables, 2)
        v.wait_ge(self.dl_in, 1)

        def to_lanes(half):
            r = slice(HALF * half, HALF * half + HALF)
            v.transpose(self.Dr[:, r, :].rearrange("p c e -> p (c e)"), self.DLr[:, r, :].rearrange("p c e -> p (c e)")).then_inc(self.dl_used, 1)

        to_lanes(0)
        v.wait_ge(dve, 1)
        v.tensor_copy(R[:, HAND, 0:1], self.k.cst[:, C_HALO:C_HALO + 1]).then_inc(dve, 1)
        v.wait_ge(dve, 2)
        v.sem_clear(dve)
        above = [31] + list(range(LANES - 1)) + [31] * (32 - LANES)
        with v.Fori(0, self.ROUNDS) as it:
            k = 0
            chain = 0
            pair = None

            def choice(c, q):
                nonlocal k
                diag, left, up = R[:, c:c + 2, 0:E], R[:, c:c + 2, 1:E + 1], R[:, c + 1:c + 3, 0:E]
                if q == 0:
                    v.tensor_tensor(An[:, :, :], diag, up, ALU.min).then_inc(dve, 1)
                elif q == 1:
                    v.tensor_tensor(Gt[:, :, :], diag, up, ALU.is_gt).then_inc(dve, 1)
                elif q == 2:
                    if c % HALF == 0:
                        v.wait_ge(self.tables, it * 2 + 1 + c // HALF)
                    v.tensor_tensor(Lr[:, c:c + 2, :], An[:, :, :], left, ALU.is_gt).then_inc(dve, 1)
                else:
                    v.wait_ge(dve, k)
                    done = self.choices if c % HALF == HALF - 2 else dve
                    v.tensor_tensor(Ur[:, c:c + 2, :], Gt[:, :, :], Lr[:, c:c + 2, :], ALU.is_gt).then_inc(done, 1)
                    if done is self.choices:
                        return
                k += 1

            for c in range(COLS):
                if chain:
                    v.wait_ge(dve, chain)
                v.tensor_tensor(Mn[:, :], R[:, c, 0:E], R[:, c, 1:E + 1], ALU.min).then_inc(dve, 1)
                k += 1
                chain = k
                if pair is not None:
                    choice(pair, 0 if c % 2 == 0 else 2)
                if c == 0:
                    v.wait_ge(self.dl_in, it * 2 + 2)
                    to_lanes(1)
                    v.wait_ge(self.dl_used, it * 2 + 1)
                if c == HALF:
                    v.wait_ge(self.dl_in, it * 2 + 3)
                    to_lanes(0)
                    v.wait_ge(self.dl_used, it * 2 + 2)
                v.wait_ge(dve, chain)
                v.tensor_tensor_scan(R[:, c + 1, 1:E + 1], Mn[:, :], self.Dr[:, c, :], R[:, c + 1, 0:1], ALU.min, ALU.add).then_inc(dve, 1)
                k += 1
                chain = k
                if pair is not None:
                    choice(pair, 1 if c % 2 == 0 else 3)
                if c % 2 == 1:
                    pair = c - 1
                if c % HAND == HAND - 1:
                    n = (c + 1) % COLS + 1
                    v.wait_ge(dve, chain)
                    v.stream_shuffle(R[:, n:n + HAND, 0], R[:, c + 2 - HAND:c + 2, E], mask=above).then_inc(dve, 1)
                    k += 1
            for q in range(4):
                v.wait_ge(dve, k)
                choice(COLS - 2, q)
            v.tensor_copy(R[:, 0, :], R[:, COLS, :]).then_inc(dve, 1)
            k += 1
            v.wait_ge(dve, k)
            v.sem_clear(dve)

    def vector_backward(self, v):
        E, COLS, HALF, HAND, LANES, ROW, CB, dve = self.E, self.COLS, self.HALF, self.HAND, self.LANES, self.ROW, self.CB, self.dve
        below = list(range(1, LANES)) + [31] * (32 - LANES + 1)
        v.memset(CB[:, :, :], 0.0).then_inc(dve, 1)
        v.stream_shuffle(self.CUT[:, 0:self.SLOTS - HAND, 65], self.CUT[:, HAND:self.SLOTS, 1], mask=below).then_inc(dve, 1)
        v.wait_ge(dve, 2)
        v.tensor_copy(CB[:, COLS - 1, 65:66], self.k.cst[:, C_START:C_START + 1]).then_inc(self.fwd0, 1)
        v.wait_ge(self.fwd0, 1)
        v.sem_clear(dve)
        with v.Fori(0, self.ROUNDS) as it:
            k = 0
            for c in reversed(range(COLS)):
                if c % HALF == HALF - 1:
                    v.wait_ge(self.tab_in, it * 2 + (1 if c > HALF else 2))
                if k:
                    v.wait_ge(dve, k)
                v.tensor_tensor_scan(CB[:, c, 129:65:-1], self.CUr[:, c, 63::-1], CB[:, c, 65:1:-1], CB[:, c, 130:131],
                                     ALU.mult, ALU.add).then_inc(dve, 1)
                k += 1
                v.wait_ge(dve, k)
                if c % HAND == 0:
                    n = (c - HAND) % COLS
                    v.stream_shuffle(CB[:, n:n + HAND, 64:131:66], CB[:, c:c + HAND, 0:67:66], mask=below).then_inc(dve, 1)
                    k += 1
                sent = bass.AP(tensor=CB, offset=((c - 1) % COLS) * ROW, ap=[[COLS * ROW, P], [2, E], [3, 2]])
                v.tensor_tensor(sent, CB[:, c, 66:130:2].unsqueeze(2).to_broadcast((P, E, 2)), self.CTr[:, c, :, :],
                                ALU.mult).then_inc(self.half_done if c == HALF else dve, 1)
                if c == HALF:
                    v.wait_ge(self.half_done, it * 2 + 1)
                else:
                    k += 1
            v.wait_ge(dve, k)
            v.sem_clear(dve)
            v.memset(self.tick[:, :], 0.0).then_inc(self.half_done, 1)

    def vector_expand(self, v):
        n = self.SLOTS // 4 * self.E
        MT, MH = (a[:, :, :].rearrange("p s e -> p (s e)") for a in (self.MT, self.MH))
        for q in range(4):
            v.transpose(MT[:, q * n:q * n + n], MH[:, q * n:q * n + n]).then_inc(self.mt_done, 1)
        v.wait_ge(self.mt_done, 4)
        for jt in range(QT):
            for p in range(0, self.LANES, 2):
                self.take_mask(v, v.tensor_copy, jt, p, self.mf_v)
        v.wait_ge(self.ex_ps, 1)
        x = self.k.x
        for b in range(B):
            v.tensor_tensor(x[:, 2 * b:2 * b + 2, :], x[:, 2 * b:2 * b + 2, :], self.k.PS[:, b, 0:L].rearrange("p (t d) -> p t d", t=QT), ALU.add)

class SpikingMoE:

    NE, M, H = 8, 64, 256

    def __init__(self, k, norm):
        self.norm = norm
        self.k = k
        NE, M, H = self.NE, self.M, self.H
        self.enc_w, self.enc_b = k.sb("moe_enc_w", [P, H]), k.sb("moe_enc_b", [P, 2])
        self.s2c_w, self.s2c_b = k.sb("moe_s2c_w", [P, 2, M]), k.sb("moe_s2c_b", [M, 1])
        self.r1_w, self.r1_b = k.sb("moe_router1_w", [M, 64]), k.sb("moe_router1_b", [64, 1])
        self.r2_w, self.r2_b = k.sb("moe_router2_w", [64, NE]), k.sb("moe_router2_b", [P, NE])
        self.e1_w, self.e1_b = k.sb("moe_e1_w", [M, NE, P]), k.sb("moe_e1_b", [P, NE])
        self.e2_w, self.e2_b = k.sb("moe_e2_w", [P, NE, M]), k.sb("moe_e2_b", [1, NE * M])
        self.c2s_w, self.c2s_b = k.sb("moe_c2s_w", [M, H]), k.sb("moe_c2s_b", [P, 2])
        self.dec_w, self.dec_b = k.sb("moe_dec_w", [P, 2, D]), k.sb("moe_dec_b", [1, D])
        self.ln_g, self.ln_b = k.sb("moe_ln_g", [P, D]), k.sb("moe_ln_b", [P, D])
        s = k.sem
        self.loaded = s("moe_loaded")
        self.product = s("moe_product")
        self.by_v, self.by_a = s("moe_vector"), s("moe_scalar")
        self.ones_set = s("moe_ones_set")
        self.P_ENC, self.P_CONT, self.P_R1, self.P_R2 = 0, 4, 6, 8
        self.P_E1 = self.P_R2 + 1
        self.P_E2 = self.P_E1 + 16
        self.P_OFT = self.P_E2 + TILES
        self.P_C2S = self.P_OFT + 2
        self.P_DEC = self.P_C2S + 4

    def place(self):
        k, NE, M = self.k, self.NE, self.M
        self.ones = k.lb("moe_ones", [1, P])
        self.encT = k.lb("moe_encT", [P, 2, B * L])
        self.contT = k.lb("moe_contT", [M, B * L])
        self.tanhT = k.lb("moe_tanhT", [64, B * L])
        self.p = k.lb("moe_p", [P, TILES, NE])
        self.row = k.lb("moe_row", [P, TILES])
        self.top = k.lb("moe_top", [P, TILES, 8])
        self.at = k.lb("moe_top_at", [P, TILES, 8], U32)
        self.atf = k.lb("moe_top_at_float", [P, TILES, 2])
        self.w = k.lb("moe_w", [P, TILES, 2])
        self.gates = k.lb("moe_gates", [P, 2, TILES, NE])
        self.hT = k.lb("moe_hT", [P, NE, B * L])
        self.gated = k.lb("moe_gated", [P, 2, NE, M])
        self.of = k.lb("moe_of", [P, TILES, M])
        self.ofT = k.lb("moe_ofT", [M, B * L])
        self.spT = k.lb("moe_spT", [P, 2, B * L])

    def load(self, q, enc_W, enc_b, s2c_W, s2c_b, rW1, rb1, rW2, rb2, We1, be1, We2, be2, c2s_W, c2s_b, dec_W, dec_b, ln_g, ln_b):
        halves = lambda b: b.rearrange("(c p) -> p c", p=P)
        pairs = [(self.enc_w[:, :], enc_W), (self.enc_b[:, :], halves(enc_b)), (self.s2c_w[:, :, :], s2c_W.rearrange("(c p) m -> p c m", p=P)),
                 (self.s2c_b[:, :], s2c_b.unsqueeze(1)), (self.r1_w[:, :], rW1), (self.r1_b[:, :], rb1.unsqueeze(1)), (self.r2_w[:, :], rW2),
                 (self.r2_b[:, :], rb2.unsqueeze(0).to_broadcast((P, self.NE))), (self.e1_w[:, :, :], We1.rearrange("e m h -> m e h")),
                 (self.e1_b[:, :], be1.rearrange("e h -> h e")), (self.e2_w[:, :, :], We2.rearrange("e h m -> h e m")),
                 (self.e2_b[:, :], be2.rearrange("(o e) m -> o (e m)", o=1)), (self.c2s_w[:, :], c2s_W), (self.c2s_b[:, :], halves(c2s_b)),
                 (self.dec_w[:, :, :], dec_W.rearrange("(c p) d -> p c d", p=P)), (self.dec_b[:, :], dec_b.unsqueeze(0)),
                 (self.ln_g[:, :], ln_g.unsqueeze(0).to_broadcast((P, D))), (self.ln_b[:, :], ln_b.unsqueeze(0).to_broadcast((P, D)))]
        for dst, src in pairs:
            q.dma_start(dst, src).then_inc(self.loaded, 16)
        self.n_loads = 16 * len(pairs)

    def pool_ones(self, pool):
        pool.memset(self.ones[:, :], 1.0).then_inc(self.ones_set, 1)

    def tensor(self, pe):
        PS, k, NE, M = self.k.PS, self.k, self.NE, self.M
        pe.wait_ge(self.loaded, self.n_loads)
        for f in range(2):
            pe.wait_ge(k.ln.s_yT, 2 * self.norm + f + 1)
            for c in range(2):
                pe.matmul(PS[:, 2 * f + c, :], self.enc_w[:, c * P:c * P + P], k.yT[:, f * BANK:f * BANK + BANK],
                          start=True, stop=True).then_inc(self.product, 1)
        for f in range(2):
            pe.wait_ge(self.by_a, 2 * f + 2)
            for c in range(2):
                mm = pe.matmul(PS[0:M, 4 + f, :], self.s2c_w[:, c, :], self.encT[:, c, f * BANK:f * BANK + BANK], start=(c == 0), stop=(c == 1))
            mm.then_inc(self.product, 1)
        for f in range(2):
            pe.wait_ge(self.by_v, f + 1)
            pe.matmul(PS[0:64, 6 + f, :], self.r1_w[:, :], self.contT[:, f * BANK:f * BANK + BANK], start=True, stop=True).then_inc(self.product, 1)
        pe.wait_ge(self.by_a, 6)
        for t in range(TILES):
            mm = pe.matmul(PS[:, 0, t * NE:t * NE + NE], self.tanhT[:, t * P:t * P + P], self.r2_w[:, :], start=True, stop=True)
        mm.then_inc(self.product, 1)
        for i in range(16):
            e, f = i // 2, i % 2
            if i >= 4:
                if f:
                    pe.wait_ge(self.by_v, self.V_E1 + (i - 4) // 2 + 1)
                else:
                    pe.wait_ge(self.by_a, 7 + (i - 4) // 2 + 1)
            pe.matmul(PS[:, 1 + i % 4, :], self.e1_w[:, e, :], self.contT[:, f * BANK:f * BANK + BANK], start=True, stop=True).then_inc(self.product, 1)
        pe.wait_ge(self.by_a, 7 + 8)
        pe.wait_ge(self.by_v, self.V_E1 + 8)
        pe.wait_ge(self.ones_set, 1)
        for t in range(TILES):
            if t >= 2:
                pe.wait_ge(self.by_v, self.V_E2 + 2 * (t - 2) + 1)
            bank = PS[:, 5 + t % 2, :]
            pe.matmul(bank, self.ones[:, :], self.e2_b[:, :], start=True, stop=False)
            for e in range(NE):
                mm = pe.matmul(bank[:, e * M:e * M + M], self.hT[:, e, t * P:t * P + P], self.e2_w[:, e, :], start=False, stop=(e == NE - 1))
            mm.then_inc(self.product, 1)
        for f in range(2):
            pe.wait_ge(self.by_v, self.V_E2 + 2 * (4 * f + 4))
            for t in range(4 * f, 4 * f + 4):
                mm = pe.transpose(PS[0:M, 1 + f, (t % 4) * P:(t % 4) * P + P], self.of[:, t, :], k.ident)
            mm.then_inc(self.product, 1)
        for f in range(2):
            pe.wait_ge(self.by_v, self.V_OFT + f + 1)
            for c in range(2):
                pe.matmul(PS[:, (3, 4, 5, 6)[2 * f + c], :], self.c2s_w[:, c * P:c * P + P], self.ofT[:, f * BANK:f * BANK + BANK],
                          start=True, stop=True).then_inc(self.product, 1)
        for f in range(2):
            pe.wait_ge(self.by_a, 15 + 2 * f + 2)
            for t in range(4 * f, 4 * f + 4):
                out = PS[:, (7, 0)[f], (t % 4) * P:(t % 4) * P + P]
                pe.matmul(out, self.ones[:, :], self.dec_b[:, :], start=True, stop=False)
                for c in range(2):
                    mm = pe.matmul(out, self.spT[:, c, t * P:t * P + P], self.dec_w[:, c, :], start=False, stop=(c == 1))
            mm.then_inc(self.product, 1)

    V_E1 = 2 + 15 + 2 * TILES
    V_E2 = V_E1 + 8
    V_OFT = V_E2 + 2 * TILES

    def scalar(self, act):
        PS, k = self.k.PS, self.k
        halves = lambda f: slice(f * BANK, f * BANK + BANK)
        act.wait_ge(self.loaded, self.n_loads)
        for f in range(2):
            for c in range(2):
                act.wait_ge(self.product, 2 * f + c + 1)
                act.activation(self.encT[:, c, halves(f)], PS[:, 2 * f + c, :], ACT.Sigmoid, bias=self.enc_b[:, c:c + 1]).then_inc(self.by_a, 1)
        for f in range(2):
            act.wait_ge(self.product, self.P_R1 + f + 1)
            act.activation(self.tanhT[:, halves(f)], PS[0:64, 6 + f, :], ACT.Tanh, bias=self.r1_b[:, 0:1]).then_inc(self.by_a, 1)
        act.wait_ge(self.by_v, 5)
        act.activation(self.p[:, :, :], self.p[:, :, :], ACT.Exp).then_inc(self.by_a, 1)
        for i in range(0, 16, 2):
            act.wait_ge(self.product, self.P_E1 + i + 1)
            act.activation(self.hT[:, i // 2, halves(0)], PS[:, 1 + i % 4, :], ACT.Relu, bias=self.e1_b[:, i // 2:i // 2 + 1]).then_inc(self.by_a, 1)
        for f in range(2):
            for c in range(2):
                act.wait_ge(self.product, self.P_C2S + 2 * f + c + 1)
                act.activation(self.spT[:, c, halves(f)], PS[:, (3, 4, 5, 6)[2 * f + c], :], ACT.Sigmoid, bias=self.c2s_b[:, c:c + 1]).then_inc(self.by_a, 1)
        for f in range(2):
            act.wait_ge(self.product, self.P_DEC + f + 1)
            act.activation(k.y[:, 4 * f:4 * f + 4, :], PS[:, (7, 0)[f], :].rearrange("p (t d) -> p t d", t=4), ACT.Sigmoid).then_inc(self.by_a, 1)

    def vector(self, v):
        PS, NE, M = self.k.PS, self.NE, self.M
        n = 0

        def done(ins):
            nonlocal n
            ins.then_inc(self.by_v, 1)
            n += 1

        def own():
            v.wait_ge(self.by_v, n)

        v.wait_ge(self.loaded, self.n_loads)
        for f in range(2):
            v.wait_ge(self.product, self.P_CONT + f + 1)
            done(v.tensor_scalar(self.contT[:, f * BANK:f * BANK + BANK], PS[0:M, 4 + f, :], self.s2c_b[:, 0:1], None, ALU.add))
        by_e = lambda a: a.unsqueeze(2).to_broadcast((P, TILES, NE))
        v.wait_ge(self.product, self.P_R2 + 1)
        done(v.tensor_tensor(self.p[:, :, :], PS[:, 0, 0:TILES * NE].rearrange("p (t e) -> p t e", e=NE),
                             self.r2_b[:, :].unsqueeze(1).to_broadcast((P, TILES, NE)), ALU.add))
        own()
        done(v.tensor_reduce(self.row[:, :], self.p[:, :, :], AX.X, ALU.max, negate=True))
        own()
        done(v.tensor_tensor(self.p[:, :, :], self.p[:, :, :], by_e(self.row[:, :]), ALU.add))
        v.wait_ge(self.by_a, 7)
        done(v.tensor_reduce(self.row[:, :], self.p[:, :, :], AX.X, ALU.add))
        own()
        done(v.reciprocal(self.row[:, :], self.row[:, :]))
        own()
        done(v.tensor_tensor(self.p[:, :, :], self.p[:, :, :], by_e(self.row[:, :]), ALU.mult))
        own()
        for t in range(TILES):
            done(v.max(self.top[:, t, :], self.p[:, t, :]))
        own()
        for t in range(TILES):
            done(v.max_index(self.at[:, t, :], self.top[:, t, :], self.p[:, t, :]))
        own()
        done(v.tensor_copy(self.atf[:, :, :], self.at[:, :, 0:2]))
        done(v.tensor_tensor(self.row[:, :], self.top[:, :, 0], self.top[:, :, 1], ALU.add))
        own()
        done(v.reciprocal(self.row[:, :], self.row[:, :]))
        own()
        done(v.tensor_tensor(self.w[:, :, :], self.top[:, :, 0:2], self.row[:, :].unsqueeze(2).to_broadcast((P, TILES, 2)), ALU.mult))
        own()
        for i in range(2):
            done(v.tensor_tensor(self.gates[:, i, :, :], self.k.cst[:, C_IOTA:C_IOTA + NE].unsqueeze(1).to_broadcast((P, TILES, NE)),
                                 by_e(self.atf[:, :, i]), ALU.is_equal))
        own()
        for i in range(2):
            done(v.tensor_tensor(self.gates[:, i, :, :], self.gates[:, i, :, :], by_e(self.w[:, :, i]), ALU.mult))
        own()
        done(v.tensor_tensor(self.gates[:, 0, :, :], self.gates[:, 0, :, :], self.gates[:, 1, :, :], ALU.add))
        own()
        assert n == self.V_E1
        for i in range(1, 16, 2):
            v.wait_ge(self.product, self.P_E1 + i + 1)
            done(v.tensor_scalar(self.hT[:, i // 2, BANK:2 * BANK], PS[:, 1 + i % 4, :], self.e1_b[:, i // 2:i // 2 + 1], 0.0, ALU.add, ALU.max))
        assert n == self.V_E2
        for t in range(TILES):
            v.wait_ge(self.product, self.P_E2 + t + 1)
            done(v.tensor_tensor(self.gated[:, t % 2, :, :], PS[:, 5 + t % 2, :].rearrange("p (e m) -> p e m", e=NE),
                                 self.gates[:, 0, t, :].unsqueeze(2).to_broadcast((P, NE, M)), ALU.mult))
            own()
            done(v.tensor_reduce(self.of[:, t, :], self.gated[:, t % 2, :, :].rearrange("p e m -> p m e"), AX.X, ALU.add))
        for f in range(2):
            v.wait_ge(self.product, self.P_OFT + f + 1)
            done(v.tensor_copy(self.ofT[:, f * BANK:f * BANK + BANK], PS[0:M, 1 + f, :]))

    def vector_add(self, v):
        k = self.k
        tiles = lambda a: a[:, :].unsqueeze(1).to_broadcast((P, TILES, D))
        first = self.V_OFT + 2
        v.wait_ge(k.ln.s_y, TILES * (self.norm + 2))
        v.tensor_tensor(k.y[:, :, :], k.y[:, :, :], tiles(self.ln_g), ALU.mult).then_inc(self.by_v, 1)
        v.wait_ge(self.by_v, first + 1)
        v.tensor_tensor(k.y[:, :, :], k.y[:, :, :], tiles(self.ln_b), ALU.add).then_inc(self.by_v, 1)
        v.wait_ge(self.by_v, first + 2)
        v.tensor_tensor(k.x[:, :, :], k.x[:, :, :], k.y[:, :, :], ALU.add)

class TopOneMoE:

    NE = 8

    def __init__(self, k, norm):
        self.yT_in = 2 * (norm + 1)
        self.k = k
        NE = self.NE
        self.wg, self.bg = k.sb("top_wg", [P, NE]), k.sb("top_bg", [P, NE])
        self.w1, self.b1 = k.sb("top_w1", [P, NE, P]), k.sb("top_b1", [P, NE])
        self.w2, self.b2 = k.sb("top_w2", [P, NE, D]), k.sb("top_b2", [NE, D])
        s = k.sem
        self.loaded = s("top_loaded")
        self.product = s("top_product")
        self.by_v, self.by_a = s("top_vector"), s("top_scalar")

    def place(self):
        k, NE = self.k, self.NE
        self.p = k.lb("top_p", [P, TILES, NE])
        self.row = k.lb("top_row", [P, TILES])
        self.top = k.lb("top_top", [P, TILES, 8])
        self.at = k.lb("top_at", [P, TILES, 8], U32)
        self.atf = k.lb("top_at_float", [P, TILES])
        self.oh = k.lb("top_one_hot", [P, TILES, NE])
        self.ohT = k.lb("top_one_hotT", [NE, B * L])
        self.ohb = k.lb("top_one_hot_bf16", [NE, B * L], BF16)
        self.h = k.lb("top_h", [P, 4, BANK])
        self.hm = k.lb("top_h_gated", [P, NE, B * L])

    def load(self, q, Wg, bg, W1, b1, W2, b2):
        pairs = [(self.wg[:, :], Wg), (self.bg[:, :], bg.unsqueeze(0).to_broadcast((P, self.NE))), (self.w1[:, :, :], W1.rearrange("e h i -> h e i")),
                 (self.b1[:, :], b1.rearrange("e i -> i e")), (self.w2[:, :, :], W2.rearrange("e i h -> i e h")), (self.b2[:, :], b2)]
        for dst, src in pairs:
            q.dma_start(dst, src).then_inc(self.loaded, 16)
        self.n_loads = 16 * len(pairs)

    V_OH = 6 + 2 * TILES + 2
    P_OH = 2

    def tensor(self, pe):
        PS, k, NE = self.k.PS, self.k, self.NE
        pe.wait_ge(self.loaded, self.n_loads)
        pe.wait_ge(k.ln.s_yT, self.yT_in)
        for t in range(TILES):
            mm = pe.matmul(PS[:, 0, t * NE:t * NE + NE], k.yT[:, t * P:t * P + P], self.wg[:, :], start=True, stop=True)
        mm.then_inc(self.product, 1)
        pe.wait_ge(self.by_v, self.V_OH)
        for t in range(TILES):
            mm = pe.transpose(PS[0:NE, 1 + t // 4, (t % 4) * P:(t % 4) * P + P], self.oh[:, t, :], k.ident)
        mm.then_inc(self.product, 1)
        pe.wait_ge(self.by_v, self.V_OH + 2)
        for i in range(16):
            e, f = i // 2, i % 2
            if i >= 2:
                pe.wait_ge(self.by_a, i)
                pe.wait_ge(self.by_v, self.V_OH + 2 + i - 1)
            r = slice(f * BANK, f * BANK + BANK)
            pe.matmul(PS[:, (0, 3)[f], :], self.w1[:, e, :], k.yT[:, r], start=True, stop=True)
            pe.matmul(PS[:, (1, 2)[f], :], k.identb[0:NE, e:e + 1].to_broadcast((NE, P)), self.ohb[:, r], start=True, stop=True).then_inc(self.product, 1)
        for t in range(TILES):
            pe.wait_ge(self.by_v, self.V_OH + 2 + 16)
            out = PS[:, 4 + t // 4, (t % 4) * P:(t % 4) * P + P]
            pe.matmul(out, self.ohT[:, t * P:t * P + P], self.b2[:, :], start=True, stop=False)
            for e in range(NE):
                mm = pe.matmul(out, self.hm[:, e, t * P:t * P + P], self.w2[:, e, :], start=False, stop=(e == NE - 1))
            if t % 4 == 3:
                mm.then_inc(self.product, 1)

    def scalar(self, act):
        PS = self.k.PS
        act.wait_ge(self.loaded, self.n_loads)
        act.wait_ge(self.by_v, 3)
        act.activation(self.p[:, :, :], self.p[:, :, :], ACT.Exp).then_inc(self.by_a, 1)
        for i in range(16):
            act.wait_ge(self.product, 2 + i + 1)
            if i >= 4:
                act.wait_ge(self.by_v, self.V_OH + 2 + i - 3)
            act.activation(self.h[:, i % 4, :], PS[:, (0, 3)[i % 2], :], ACT.Gelu, bias=self.b1[:, i // 2:i // 2 + 1]).then_inc(self.by_a, 1)

    def vector(self, v):
        PS, NE = self.k.PS, self.NE
        n = 0

        def done(ins):
            nonlocal n
            ins.then_inc(self.by_v, 1)
            n += 1

        def own():
            v.wait_ge(self.by_v, n)

        by_e = lambda a: a.unsqueeze(2).to_broadcast((P, TILES, NE))
        v.wait_ge(self.loaded, self.n_loads)
        v.wait_ge(self.product, 1)
        done(v.tensor_tensor(self.p[:, :, :], PS[:, 0, 0:TILES * NE].rearrange("p (t e) -> p t e", e=NE),
                             self.bg[:, :].unsqueeze(1).to_broadcast((P, TILES, NE)), ALU.add))
        own()
        done(v.tensor_reduce(self.row[:, :], self.p[:, :, :], AX.X, ALU.max, negate=True))
        own()
        done(v.tensor_tensor(self.p[:, :, :], self.p[:, :, :], by_e(self.row[:, :]), ALU.add))
        v.wait_ge(self.by_a, 1)
        done(v.tensor_reduce(self.row[:, :], self.p[:, :, :], AX.X, ALU.add))
        own()
        done(v.reciprocal(self.row[:, :], self.row[:, :]))
        own()
        done(v.tensor_tensor(self.p[:, :, :], self.p[:, :, :], by_e(self.row[:, :]), ALU.mult))
        own()
        for t in range(TILES):
            done(v.max(self.top[:, t, :], self.p[:, t, :]))
        own()
        for t in range(TILES):
            done(v.max_index(self.at[:, t, :], self.top[:, t, :], self.p[:, t, :]))
        own()
        done(v.tensor_copy(self.atf[:, :], self.at[:, :, 0]))
        own()
        done(v.tensor_tensor(self.oh[:, :, :], self.k.cst[:, C_IOTA:C_IOTA + NE].unsqueeze(1).to_broadcast((P, TILES, NE)), by_e(self.atf[:, :]),
                             ALU.is_equal))
        assert n == self.V_OH
        v.wait_ge(self.product, 2)
        for dst in (self.ohT, self.ohb):
            done(v.tensor_copy(dst[:, :].rearrange("p (f c) -> p f c", f=2), PS[0:NE, 1:3, :]))
        for i in range(16):
            e, f = i // 2, i % 2
            v.wait_ge(self.by_a, 1 + i + 1)
            done(v.tensor_tensor(self.hm[:, e, f * BANK:f * BANK + BANK], self.h[:, i % 4, :], PS[:, (1, 2)[f], :], ALU.mult))
        x = self.k.x
        for f in range(2):
            v.wait_ge(self.product, 2 + 16 + f + 1)
            r = slice(4 * f, 4 * f + 4)
            v.tensor_tensor(x[:, r, :], x[:, r, :], PS[:, 4 + f, :].rearrange("p (t d) -> p t d", t=4), ALU.add)

def build(nc, a, cst_d, out):
    with ExitStack() as stack:
        k = Kit(nc, stack)
        k.PS = stack.enter_context(nc.psum_tensor("PS", [P, 8, BANK], F32))
        k.cst = k.sb("constants", [P, C_END])
        k.ident = k.cst[:, C_ID:C_ID + P]
        k.x = k.sb("x", [P, TILES, D])
        k.y = k.sb("y", [P, TILES, D])
        k.yT = k.sb("yT", [P, B * L])
        k.ctxT = k.sb("ctxT", [P, B, S2])
        k.ctxP = k.sb("ctx_by_lane", [P, S2 // 32, D])
        k.identb = k.sb("ident_bf16", [P, P], BF16)
        k.trib = k.sb("triangle_bf16", [P, P], BF16)
        k.ln = LayerNorm(k)
        warm = k.sb("warm", [P, 1])
        x_in, cst_in, ctx_in, ctxP_in = k.sem("x_in"), k.sem("constants_in"), k.sem("ctx_in"), k.sem("ctx_by_lane_in")
        ctx_turned, ctx_sb, cast_done, out_done = k.sem("ctx_turned"), k.sem("ctxT_ready"), k.sem("bf16_constants_ready"), k.sem("out_done")
        l1f = NarrowAttention(k, "l1f", 3, by_class=True)
        l2f = SpikingMoE(k, 5)
        l3x = NarrowAttention(k, "l3x", 6, by_class=False)
        l3f = TopOneMoE(k, 7)
        with ExitStack() as k.local:
            l0x = WideAttention(k, "l0x", 0, causal=True, wo_by_head=False)
            l1x = WideAttention(k, "l1x", 2, causal=False, wo_by_head=True)
            group = k.local
            with ExitStack() as k.local:
                ctx_nat = k.lb("ctx_natural", [P, B * S2 // P, D])
                l0f = ShiftMix(k, 1)
            k.local = group
            l1f.place()
        with ExitStack() as k.local:
            l2x = Warping(k, 4)
        with ExitStack() as k.local:
            l3x.place()
            group = k.local
            with ExitStack() as k.local:
                l2f.place()
            k.local = group
            l3f.place()
        stack.enter_context(nc.allow_non_contiguous_dma(reason="biases of at most 1024 elements, one to a partition"))
        block = stack.enter_context(nc.Block())

        @block.sync
        def _(sp):
            sp.dma_start(k.x[:, :, :], a["x"].rearrange("b (t p) d -> p (b t) d", p=P)).then_inc(x_in, 16)
            sp.dma_start(k.cst[:, :], cst_d).then_inc(cst_in, 16)
            ctx = a["ctx_1024"]
            sp.dma_start(ctx_nat[:, :, :], ctx.rearrange("b (t p) d -> p (b t) d", p=P)).then_inc(ctx_in, 16)
            wq, wk, bq, bk = (a["L0_xattn_" + n] for n in ("Wq", "Wk", "bq", "bk"))
            l0x.load_once(sp, a["L0_xattn_Wv"], a["L0_xattn_bv"], a["L0_xattn_bo"], a["L0_xattn_Wo"], wq, wk, bq, bk)
            l0f.load(sp, *(a["L0_ffn_" + n] for n in ("W_r", "W_k", "W_v", "mu_r", "mu_k")))
            wide = lambda n: a["L1_xattn_" + n].rearrange("d n h -> d (n h)")
            bias = lambda n: a["L1_xattn_" + n].rearrange("n o h -> (n o h)")
            wq1, wk1, bq1, bk1 = wide("w_query"), wide("w_key"), bias("b_query"), bias("b_key")
            l1x.load_once(sp, wide("w_value"), bias("b_value"), a["L1_xattn_b_projection"].rearrange("o d -> (o d)"), a["L1_xattn_w_projection"],
                          wq1, wk1, bq1, bk1)
            l0x.load_rounds(sp, wq, wk, bq, bk)
            for b in range(B):
                sp.dma_start(k.ctxP[32 * b:32 * b + 32, :, :], ctx[b].rearrange("(p e) d -> e p d", e=32)).then_inc(ctxP_in, 16)
            qkv = a["L1_ffn_W_qkv"]
            l1f.load(sp, qkv[:, 0:D], qkv[:, D:2 * D], qkv[:, 2 * D:3 * D], a["L1_ffn_W_proj"], a["L1_ffn_b_proj"], g=a["L1_ffn_g_info"][0, 0])
            l3x.load(sp, *(a["L3_xattn_" + n] for n in ("Wq", "Wk", "Wv", "Wo", "bo", "bq", "bk", "bv")), mask=a["mask_BxS2_bf0"])
            l2f.load(sp, *(a["L2_ffn_" + n] for n in ("enc_W", "enc_b", "s2c_W", "s2c_b", "rW1", "rb1", "rW2", "rb2", "We1", "be1", "We2", "be2",
                                                     "c2s_W", "c2s_b", "dec_W", "dec_b", "ln_g", "ln_b")))
            l3f.load(sp, *(a["L3_ffn_" + n] for n in ("Wg", "bg", "W1", "b1", "W2", "b2")))
            l1x.load_rounds(sp, wq1, wk1, bq1, bk1)
            sp.wait_ge(k.stage_done, 4 * 12)
            sp.dma_start(out.rearrange("b (t p) d -> p (b t) d", p=P), k.x[:, :, :]).then_inc(out_done, 16)
            sp.wait_ge(out_done, 16)

        @block.gpsimd
        def _(pool):
            ln = k.ln
            pool.memset(ln.half[:, :], -0.5).then_inc(ln.s_half, 1)
            l3x.pool_zero(pool)
            pool.wait_ge(cst_in, 16)
            pool.tensor_copy(k.identb[:, :], k.ident).then_inc(cast_done, 1)
            pool.tensor_copy(k.trib[:, :], k.cst[:, C_TRI:C_TRI + P]).then_inc(cast_done, 1)
            pool.wait_ge(ln.s_half, 1)
            ln.pool_rstd(pool, 0)
            k.meet(pool, 0)
            ln.pool_rstd(pool, 1)
            k.meet(pool, 1)
            ln.pool_rstd(pool, 2)
            l1f.pool_pad(pool)
            k.meet(pool, 2)
            ln.pool_rstd(pool, 3)
            l1f.pool_find(pool)
            l1f.pool_batches(pool)
            k.meet(pool, 3)
            ln.pool_rstd(pool, 4)
            l2x.pool_before(pool)
            k.meet(pool, 4)
            l2x.pool_forward(pool)
            k.meet(pool, 5)
            k.meet(pool, 6)
            k.meet(pool, 7)
            ln.pool_rstd(pool, 5)
            l2f.pool_ones(pool)
            l3x.pool_pad(pool)
            ln.pool_rstd(pool, 6)
            k.meet(pool, 8)
            ln.pool_rstd(pool, 7)
            l3x.pool_batches(pool)
            k.meet(pool, 9)
            ln.pool_rstd(pool, 8)
            k.meet(pool, 10)
            k.meet(pool, 11)

        @block.tensor
        def _(pe):
            ln = k.ln
            pe.wait_ge(cst_in, 16)
            pe.wait_ge(ctx_in, 16)
            for t in range(B * S2 // P):
                mm = pe.transpose(k.PS[:, t // 4, (t % 4) * P:(t % 4) * P + P], ctx_nat[:, t, :], k.ident)
                if t % 4 == 3:
                    mm.then_inc(ctx_turned, 1)
            ln.tensor_transpose(pe, 0, 0)
            pe.wait_ge(cast_done, 2)
            pe.wait_ge(ctx_sb, B)
            l0x.tensor(pe)
            k.meet(pe, 0)
            ln.tensor_transpose(pe, 1, 1)
            l0f.tensor(pe)
            k.meet(pe, 1)
            ln.tensor_transpose(pe, 2, 2)
            l1x.tensor(pe)
            k.meet(pe, 2)
            ln.tensor_transpose(pe, 3, 3)
            l1f.tensor_find(pe)
            l1f.tensor(pe)
            k.meet(pe, 3)
            ln.tensor_transpose(pe, 4, 4)
            l2x.tensor_distances(pe)
            k.meet(pe, 4)
            k.meet(pe, 5)
            k.meet(pe, 6)
            pe.wait_ge(ctxP_in, 64)
            l2x.tensor_expand(pe)
            k.meet(pe, 7)
            ln.tensor_transpose(pe, 5, 5)
            l2f.tensor(pe)
            k.meet(pe, 8)
            ln.tensor_transpose(pe, 7, 6)
            l3x.tensor(pe)
            k.meet(pe, 9)
            ln.tensor_transpose(pe, 8, 7)
            l3f.tensor(pe)
            k.meet(pe, 10)
            k.meet(pe, 11)

        @block.scalar
        def _(act):
            ln = k.ln
            prime = ln.half[:, 0:1]
            act.wait_ge(ln.s_half, 1)
            for b in range(B):
                act.wait_ge(ctx_turned, b + 1)
                act.copy(k.ctxT[:, b, :], k.PS[:, b, :]).then_inc(ctx_sb, 1)
            ln.scalar_yT(act, 0)
            act.activation(warm[:, :], prime, ACT.Exp)
            l0x.scalar(act)
            k.meet(act, 0)
            ln.scalar_yT(act, 1)
            l0f.scalar(act)
            k.meet(act, 1)
            ln.scalar_yT(act, 2)
            act.activation(warm[:, :], prime, ACT.Exp)
            l1x.scalar(act)
            k.meet(act, 2)
            ln.scalar_yT(act, 3)
            act.activation(warm[:, :], prime, ACT.Exp)
            l1f.scalar(act)
            k.meet(act, 3)
            ln.scalar_yT(act, 4)
            l2x.scalar_distances(act)
            k.meet(act, 4)
            l2x.scalar_forward(act)
            k.meet(act, 5)
            l2x.scalar_backward(act)
            k.meet(act, 6)
            l2x.scalar_expand(act)
            k.meet(act, 7)
            ln.scalar_yT(act, 5)
            l2f.scalar(act)
            k.meet(act, 8)
            ln.scalar_yT(act, 6)
            act.activation(warm[:, :], prime, ACT.Exp)
            l3x.scalar(act)
            k.meet(act, 9)
            ln.scalar_yT(act, 7)
            l3f.scalar(act)
            k.meet(act, 10)
            k.meet(act, 11)

        @block.vector
        def _(v):
            ln, x, y = k.ln, k.x, k.y
            v.wait_ge(x_in, 16)

            def norm(n, src=x):
                ln.vector_stats(v, n, src)
                ln.vector_norm(v, n, src, y)
                v.wait_ge(ln.s_y, TILES * (n + 1))

            norm(0)
            l0x.vector(v)
            k.meet(v, 0)
            norm(1)
            l0f.vector(v)
            k.meet(v, 1)
            norm(2)
            l1x.vector(v)
            k.meet(v, 2)
            norm(3)
            v.wait_ge(cst_in, 16)
            l1f.vector_find(v)
            l1f.vector(v)
            k.meet(v, 3)
            norm(4)
            v.wait_ge(ctxP_in, 64)
            l2x.vector_distances(v)
            k.meet(v, 4)
            l2x.vector_forward(v)
            k.meet(v, 5)
            l2x.vector_backward(v)
            k.meet(v, 6)
            l2x.vector_expand(v)
            k.meet(v, 7)
            norm(5)
            l2f.vector(v)
            v.wait_ge(l2f.by_a, 21)
            norm(6, y)
            l2f.vector_add(v)
            k.meet(v, 8)
            norm(7)
            l3x.vector_padding(v)
            l3x.vector(v)
            k.meet(v, 9)
            norm(8)
            l3f.vector(v)
            k.meet(v, 10)
            k.meet(v, 11)



def constants():
    import numpy as np
    c = np.zeros((P, C_END), dtype=np.float32)
    p = np.arange(P)
    c[:, C_ID:C_ID + P] = np.eye(P)
    c[:, C_TRI:C_TRI + P] = np.where(p[None, :] <= p[:, None], 0.0, -BIG)
    c[:, C_HALO] = np.where(p % 32 == 0, 0.0, BIG)
    c[:, C_START] = p % 32 == S2 // 32 - 1
    for t in range(0, TILES, QT):
        c[0:REG, C_REG + t] = 1.0
    c[:, C_IOTA:C_IOTA + 8] = np.arange(8)
    for row in range(2):
        c[row, C_CLASS + D8 + row:C_CLASS + P:32] = 1.0
    c[1, C_NEG:C_NEG + REG] = 1.0
    for h in range(HEADS8):
        own = (p // 32 == h % 4) & (p % 32 < D8 + 2)
        c[own, C_OWN + (h // 4) * HEADS8 + h] = SCALE8
        for i in range(REG):
            c[h * REG + i, C_DIAG + D8 * h:C_DIAG + D8 * h + D8] = 1.0
            c[h * REG + i, C_SUM + i] = 0.5
    return c


def kernel(**inputs):
    import numpy as np
    import concourse.bacc as bacc
    from concourse.bass_utils import run_bass_kernel_spmd

    nc = bacc.Bacc("TRN2", target_bir_lowering=False, num_devices=1)
    arrays, args = {}, {}
    for name, value in inputs.items():
        a = np.ascontiguousarray(value)
        if a.dtype == np.bool_:
            a = a.view(np.uint32)
        arrays[name + "_dram"] = a
        args[name] = nc.dram_tensor(name + "_dram", a.shape, mybir.dt.from_np(a.dtype), kind="ExternalInput").ap()
    arrays["constants_dram"] = constants()
    cst = nc.dram_tensor("constants_dram", arrays["constants_dram"].shape, F32, kind="ExternalInput").ap()
    out = nc.dram_tensor("out_dram", (B, L, D), F32, kind="ExternalOutput").ap()
    build(nc, args, cst, out)
    r = run_bass_kernel_spmd(nc, [arrays], core_ids=[0])
    return r.results[0]["out_dram"]
```

```python
from contextlib import ExitStack

import concourse.bass as bass
from concourse import mybir

F32 = mybir.dt.float32
BF16 = mybir.dt.bfloat16
U8 = mybir.dt.uint8
U32 = mybir.dt.uint32
ALU = mybir.AluOpType
ACT = mybir.ActivationFunctionType
AX = mybir.AxisListType
ds = bass.ds

P = 128
D = 128
B, L, S2 = 4, 256, 512
TILES = B * L // P
QT = L // P
BIG = 1e30
HALFBANK, BANK = 256, 512
EPS = 1e-5

C_ID = 0
C_TRI = 128
C_HALO = 256
C_START = 257
C_REG = 258
C_IOTA = 266
C_CLASS = 274
C_NEG = 402
C_OWN = 407
C_DIAG = 471
C_SUM = 983
C_ONE = 988
C_END = 1116
REG = 5
HEADS8, D8 = 16, 8
SCALE8 = float(D8) ** -0.5


class Kit:

    def __init__(self, nc, stack):
        self.nc, self.stack = nc, stack
        self.local = None
        self.stage_done = self.sem("stage_done")

    def sb(self, name, shape, dt=F32):
        return self.stack.enter_context(self.nc.sbuf_tensor(name, shape, dt))

    def lb(self, name, shape, dt=F32):
        return self.local.enter_context(self.nc.sbuf_tensor(name, shape, dt))

    def sem(self, name):
        return self.stack.enter_context(self.nc.semaphore(name))

    def meet(self, eng, stage):
        eng.drain().then_inc(self.stage_done, 1)
        eng.wait_ge(self.stage_done, 4 * (stage + 1))

class LayerNorm:

    TPS = (6, 7)

    def __init__(self, k):
        self.k = k
        self.stats = k.sb("ln_stats", [P, TILES, 6])
        self.mv = k.sb("ln_mv", [P, TILES, 2])
        self.rstd = k.sb("ln_rstd", [P, TILES])
        self.half = k.sb("ln_minus_half", [P, P])
        self.s_half = k.sem("minus_half_set")
        self.s_stats = k.sem("ln_stats_done")
        self.s_mv = k.sem("ln_mean_var_done")
        self.s_var = k.sem("ln_var_eps_done")
        self.s_rstd = k.sem("ln_rstd_done")
        self.s_y = k.sem("ln_y_done")
        self.s_tps = k.sem("ln_transposed")
        self.s_yT = k.sem("ln_yT_done")

    def pool_rstd(self, pool, n):
        pool.wait_ge(self.s_mv, TILES * (n + 1))
        pool.tensor_scalar(self.rstd[:, :], self.mv[:, :, 1], EPS, None, ALU.add).then_inc(self.s_var, 1)
        pool.wait_ge(self.s_var, n + 1)
        pool.tensor_tensor(self.rstd[:, :], self.rstd[:, :], self.half[:, 0:TILES], ALU.pow).then_inc(self.s_rstd, 1)

    def vector_stats(self, v, n, src):
        for t in range(TILES):
            v.bn_stats(self.stats[:, t, :], src[:, t, :]).then_inc(self.s_stats, 1)
        for t in range(TILES):
            v.wait_ge(self.s_stats, TILES * n + t + 1)
            v.bn_aggr(self.mv[:, t, :], self.stats[:, t, :]).then_inc(self.s_mv, 1)

    def vector_norm(self, v, n, src, dst):
        v.wait_ge(self.s_rstd, n + 1)
        v.wait_ge(self.s_mv, TILES * (n + 1))
        for t in range(TILES):
            v.tensor_scalar(dst[:, t, :], src[:, t, :], self.mv[:, t, 0:1], self.rstd[:, t:t + 1],
                            ALU.subtract, ALU.mult).then_inc(self.s_y, 1)

    def tensor_transpose(self, pe, n, m):
        for t in range(TILES):
            pe.wait_ge(self.s_y, TILES * n + t + 1)
            mm = pe.transpose(self.k.PS[:, self.TPS[t // 4], (t % 4) * P:(t % 4) * P + P], self.k.y[:, t, :], self.k.ident)
            if t % 4 == 3:
                mm.then_inc(self.s_tps, 1)

    def scalar_yT(self, act, m):
        for h in range(2):
            act.wait_ge(self.s_tps, 2 * m + h + 1)
            act.copy(self.k.yT[:, h * BANK:h * BANK + BANK], self.k.PS[:, self.TPS[h], :]).then_inc(self.s_yT, 1)

class WideAttention:

    ROUNDS, UNITS, STEPS, HD = 8, B, 16, 64
    S, T, O, G = (0, 1), (2, 3), (4, 5), (6, 7)

    def __init__(self, k, name, norm, causal, wo_by_head):
        self.yT_in = 2 * (norm + 1)
        self.k, self.name, self.causal, self.wo_by_head = k, name, causal, wo_by_head
        n = name + "_"
        most = L if causal else S2
        self.wq = k.lb(n + "wq", [P, P])
        self.wk = k.lb(n + "wk", [P, P])
        self.bq = k.lb(n + "bq", [P, 1])
        self.bk = k.lb(n + "bk", [P, 1])
        self.wv = k.lb(n + "wv", [P, 8 * P])
        self.bv = k.lb(n + "bv", [P, 8 * P])
        self.wo = k.lb(n + "wo", [P, 8, P])
        self.wo_in = k.lb(n + "wo_in", [P, 8, P]) if wo_by_head else None
        self.bo = k.lb(n + "bo", [P, P])
        self.qT = k.lb(n + "qT", [P, 2, L])
        self.kT = k.lb(n + "kT", [P, 2, most])
        self.v = k.lb(n + "v", [P, 2, most // P, P])
        self.probs = k.lb(n + "probs", [P, 2, most])
        self.pT = k.lb(n + "pT", [P, 2, most])
        self.nmax = k.lb(n + "nmax", [P, 4])
        self.sums = k.lb(n + "sums", [P, 8])
        self.inv = k.lb(n + "inv", [P, 2, QT, P])
        self.spread = k.lb(n + "inverse_spread", [P, 2, L])
        self.attT = k.lb(n + "attT", [P, 2, L])
        s = k.sem
        self.w_once = s(n + "weights_loaded")
        self.w_in = s(n + "round_weights_loaded")
        self.q_ps, self.k_ps, self.v_ps = s(n + "q_product"), s(n + "k_product"), s(n + "v_product")
        self.q_sb, self.k_sb, self.v_sb = s(n + "q_ready"), s(n + "k_ready"), s(n + "v_ready")
        self.sc, self.mx, self.ex, self.tr = s(n + "scores"), s(n + "max"), s(n + "probs"), s(n + "turned")
        self.pt_v, self.pt_a = s(n + "pT_even"), s(n + "pT_odd")
        self.av, self.iv, self.nm = s(n + "pv"), s(n + "inverse"), s(n + "attT_normed")
        self.sp_ps, self.sp_sb = s(n + "inverse_spread_product"), s(n + "inverse_spread_ready")
        self.wo_ps, self.x_add = s(n + "out_product"), s(n + "x_added")
        order = [("q", 0), ("k", 0), ("v", 0)]
        for b in range(B):
            if b + 1 < B:
                order += [("q", b + 1), ("k", b + 1), ("v", b + 1)]
            if b >= 1:
                order += [("t", b - 1), ("o", b - 1)]
        order += [("t", B - 1), ("o", B - 1)]
        assert len(order) % 2 == 0
        self.bank = {u: self.G[i % 2] for i, u in enumerate(order)}
        self.before = {u: order[i - 2] for i, u in enumerate(order) if i >= 2}

    def keys(self, n):
        return P * (n % QT + 1) if self.causal else S2

    def where(self, n):
        return n // 4, (n % 4) // 2, n % 2

    def load_once(self, sp, wv, bv, bo, wo, wq, wk, bq, bk):
        sp.dma_start(self.wq[:, :], wq[:, 0:P]).then_inc(self.w_in, 16)
        sp.dma_start(self.wk[:, :], wk[:, 0:P]).then_inc(self.w_in, 16)
        sp.dma_start(self.bq[:, :], bq[0:P].unsqueeze(1)).then_inc(self.w_in, 16)
        sp.dma_start(self.bk[:, :], bk[0:P].unsqueeze(1)).then_inc(self.w_in, 16)
        sp.dma_start(self.wv[:, :], wv).then_inc(self.w_once, 16)
        sp.dma_start(self.bv[:, :], bv.unsqueeze(0).to_broadcast((P, 8 * P))).then_inc(self.w_once, 16)
        sp.dma_start(self.bo[:, :], bo.unsqueeze(0).to_broadcast((P, P))).then_inc(self.w_once, 16)
        if self.wo_by_head:
            sp.dma_start(self.wo_in[:, :, :].rearrange("p r (u h) -> p (r u) h", u=2), wo.rearrange("n d h -> d n h")).then_inc(self.w_once, 16)
        else:
            sp.dma_start(self.wo[:, :, :], wo.rearrange("(r p) d -> p r d", p=P)).then_inc(self.w_once, 16)

    def load_rounds(self, sp, wq, wk, bq, bk):
        with sp.Fori(0, self.ROUNDS - 1) as it:
            sp.wait_ge(self.q_sb, it * B + B)
            sp.wait_ge(self.k_sb, it * B + B)
            nxt = it * P + P
            sp.dma_start(self.wq[:, :], wq[:, ds(nxt, P)]).then_inc(self.w_in, 16)
            sp.dma_start(self.wk[:, :], wk[:, ds(nxt, P)]).then_inc(self.w_in, 16)
            sp.dma_start(self.bq[:, :], bq[ds(nxt, P)].unsqueeze(1)).then_inc(self.w_in, 16)
            sp.dma_start(self.bk[:, :], bk[ds(nxt, P)].unsqueeze(1)).then_inc(self.w_in, 16)

    def tensor(self, pe):
        PS, ident = self.k.PS, self.k.ident
        pe.wait_ge(self.k.ln.s_yT, self.yT_in)
        pe.wait_ge(self.w_once, 64)
        if self.wo_by_head:
            for r in range(8):
                mm = pe.transpose(PS[:, self.G[r // 4], (r % 4) * P:(r % 4) * P + P], self.wo_in[:, r, :], ident)
            mm.then_inc(self.wo_ps, 1)
            pe.wait_ge(self.x_add, 1)

        def free(u, it):
            if u == ("k", 0):
                pe.wait_ge(self.x_add, it * B + 1)
            if u not in self.before:
                return
            kind, b = self.before[u]
            done, more = {"q": (self.q_sb, 0), "k": (self.k_sb, 0), "v": (self.v_sb, 0), "t": (self.sp_sb, 0),
                          "o": (self.x_add, 1)}[kind]
            pe.wait_ge(done, it * B + b + 1 + more)

        def project(kind, b, it):
            out = PS[:, self.bank[kind, b], :]
            free((kind, b), it)
            if kind == "q":
                if b == 0:
                    pe.wait_ge(self.w_in, it * 64 + 64)
                pe.matmul(out[:, 0:L], self.wq[:, :], self.k.yT[:, b * L:b * L + L], start=True, stop=True).then_inc(self.q_ps, 1)
            elif kind == "k":
                n = L if self.causal else S2
                pe.matmul(out[:, 0:n], self.wk[:, :], self.k.ctxT[:, b, 0:n], start=True, stop=True).then_inc(self.k_ps, 1)
            elif kind == "v":
                for kt in range(2 if self.causal else 4):
                    mm = pe.matmul(out[:, kt * P:kt * P + P], self.k.ctxT[:, b, kt * P:kt * P + P], self.wv[:, ds(it * P, P)],
                                   start=True, stop=True)
                mm.then_inc(self.v_ps, 1)
            elif kind == "t":
                pe.wait_ge(self.iv, it * B + b + 1)
                for qt in range(QT):
                    mm = pe.matmul(out[:, qt * P:qt * P + P], self.inv[:, b % 2, qt, :], ident, start=True, stop=True)
                mm.then_inc(self.sp_ps, 1)
            else:
                pe.wait_ge(self.nm, it * B + b + 1)
                for qt in range(QT):
                    mm = pe.matmul(out[:, qt * P:qt * P + P], self.attT[:, b % 2, qt * P:qt * P + P],
                                   self.wo[:, ds(it, 1), :].rearrange("p a d -> p (a d)"), start=True, stop=True)
                mm.then_inc(self.wo_ps, 1)

        def scores(n, it):
            b, h, qt = self.where(n)
            if n % 4 == 0:
                pe.wait_ge(self.q_sb, it * B + b + 1)
                pe.wait_ge(self.k_sb, it * B + b + 1)
            if n >= 2:
                pe.wait_ge(self.ex, it * self.STEPS + n - 1)
            rows = slice(64 * h, 64 * h + 64)
            mm = pe.matmul(PS[:, self.S[n % 2], 0:self.keys(n)], self.qT[rows, b % 2, qt * P:qt * P + P],
                           self.kT[rows, b % 2, 0:self.keys(n)], start=True, stop=not self.causal)
            if self.causal:
                mm = pe.matmul(PS[:, self.S[n % 2], qt * P:qt * P + P], self.k.identb[:, :], self.k.trib[:, :],
                               start=False, stop=True)
            mm.then_inc(self.sc, 1)

        def turn(n, it):
            pe.wait_ge(self.ex, it * self.STEPS + n + 1)
            if n >= 2:
                pe.wait_ge(self.pt_a if n % 2 else self.pt_v, it * 8 + n // 2)
            for kt in range(self.keys(n) // P):
                mm = pe.transpose(PS[:, self.T[n % 2], kt * P:kt * P + P], self.probs[:, n % 2, kt * P:kt * P + P], ident)
            mm.then_inc(self.tr, 1)

        def times_v(n, it):
            b, h, qt = self.where(n)
            if n % 4 == 0:
                pe.wait_ge(self.v_sb, it * B + b + 1)
            pe.wait_ge(self.pt_a if n % 2 else self.pt_v, it * 8 + n // 2 + 1)
            if n % 4 == 0 and b >= 2:
                pe.wait_ge(self.nm, it * B + b - 1)
            last = self.keys(n) // P - 1
            for kt in range(last + 1):
                mm = pe.matmul(PS[64 * h:64 * h + 64, self.O[b % 2], qt * P:qt * P + P], self.v[:, b % 2, kt, 64 * h:64 * h + 64],
                               self.pT[:, n % 2, kt * P:kt * P + P], start=(kt == 0), stop=(kt == last))
            mm.then_inc(self.av, 1)

        with pe.Fori(0, self.ROUNDS) as it:
            for kind in "qkv":
                project(kind, 0, it)
            for n in range(-2, self.STEPS + 1):
                b, r = n // 4, n % 4
                if 0 <= n < self.STEPS:
                    turn(n, it)
                if n + 2 < self.STEPS:
                    scores(n + 2, it)
                if n >= 1:
                    times_v(n - 1, it)
                if 0 <= n < self.STEPS:
                    if r == 0 and b + 1 < B:
                        project("q", b + 1, it)
                        project("k", b + 1, it)
                    if r == 1 and b + 1 < B:
                        project("v", b + 1, it)
                    if r == 1 and b >= 1:
                        project("t", b - 1, it)
                    if r == 3 and b >= 1:
                        project("o", b - 1, it)
            project("t", B - 1, it)
            project("o", B - 1, it)

    def vector(self, v):
        PS = self.k.PS
        v.wait_ge(self.w_once, 64)
        if self.wo_by_head:
            v.wait_ge(self.wo_ps, 1)
            for i in range(2):
                v.tensor_copy(self.wo[:, 4 * i:4 * i + 4, :], PS[:, self.G[i], :].rearrange("p (r d) -> p r d", r=4))
        v.tensor_tensor(self.k.x[:, :, :], self.k.x[:, :, :], self.bo[:, :].unsqueeze(1).to_broadcast((P, TILES, P)),
                        ALU.add).then_inc(self.x_add, 1)
        v.wait_ge(self.x_add, 1)
        wo_extra = 1 if self.wo_by_head else 0

        def take_q(b, it):
            v.wait_ge(self.q_ps, it * B + b + 1)
            v.tensor_scalar(self.qT[:, b % 2, :], PS[:, self.bank["q", b], 0:L], self.bq[:, 0:1], 0.125,
                            ALU.add, ALU.mult).then_inc(self.q_sb, 1)

        def take_v(b, it):
            v.wait_ge(self.v_ps, it * B + b + 1)
            n = 2 if self.causal else 4
            v.tensor_tensor(self.v[:, b % 2, 0:n, :], PS[:, self.bank["v", b], 0:n * P].rearrange("p (t d) -> p t d", t=n),
                            self.bv[:, ds(it * P, P)].unsqueeze(1).to_broadcast((P, n, P)), ALU.add).then_inc(self.v_sb, 1)

        def invert(b, it):
            v.wait_ge(self.ex, it * self.STEPS + 4 * b + 4)
            sums = self.sums[:, 4 * (b % 2):4 * (b % 2) + 4].rearrange("p (h t) -> p t h", t=QT)
            v.reciprocal(self.inv[:, b % 2, :, :].rearrange("p t (h f) -> p t h f", h=2),
                         sums.unsqueeze(3).to_broadcast((P, QT, 2, 64))).then_inc(self.iv, 1)

        def normalise(b, it):
            v.wait_ge(self.sp_sb, it * B + b + 1)
            v.wait_ge(self.av, it * self.STEPS + 4 * b + 4)
            v.tensor_tensor(self.attT[:, b % 2, :], PS[:, self.O[b % 2], 0:L], self.spread[:, b % 2, :], ALU.mult).then_inc(self.nm, 1)

        def add_x(b, it):
            v.wait_ge(self.wo_ps, it * B + b + 1 + wo_extra)
            v.tensor_tensor(self.k.x[:, 2 * b:2 * b + 2, :], self.k.x[:, 2 * b:2 * b + 2, :],
                            PS[:, self.bank["o", b], 0:L].rearrange("p (t d) -> p t d", t=QT), ALU.add).then_inc(self.x_add, 1)

        with v.Fori(0, self.ROUNDS) as it:
            take_q(0, it)
            take_v(0, it)
            for n in range(-2, self.STEPS + 1):
                b, r = n // 4, n % 4
                if 0 <= n < self.STEPS and n % 2 == 0:
                    v.wait_ge(self.tr, it * self.STEPS + n + 1)
                    w = self.keys(n)
                    v.tensor_copy(self.pT[:, 0, 0:w], PS[:, self.T[0], 0:w]).then_inc(self.pt_v, 1)
                if n + 2 < self.STEPS:
                    m = n + 2
                    v.wait_ge(self.sc, it * self.STEPS + m + 1)
                    v.tensor_reduce(self.nmax[:, m % 4:m % 4 + 1], PS[:, self.S[m % 2], 0:self.keys(m)], AX.X, ALU.max,
                                    negate=True).then_inc(self.mx, 1)
                if 0 <= n < self.STEPS:
                    if r == 0 and b + 1 < B:
                        take_q(b + 1, it)
                    if r == 1 and b + 1 < B:
                        take_v(b + 1, it)
                    if r == 0 and b >= 1:
                        invert(b - 1, it)
                    if r == 2 and b >= 1:
                        normalise(b - 1, it)
                    if r == 3 and b >= 1:
                        add_x(b - 1, it)
            invert(B - 1, it)
            normalise(B - 1, it)
            add_x(B - 1, it)

    def scalar(self, act):
        PS = self.k.PS

        def take_k(b, it):
            act.wait_ge(self.k_ps, it * B + b + 1)
            n = L if self.causal else S2
            act.activation(self.kT[:, b % 2, 0:n], PS[:, self.bank["k", b], 0:n], ACT.Identity, bias=self.bk[:, 0:1]).then_inc(self.k_sb, 1)

        def take_spread(b, it):
            act.wait_ge(self.sp_ps, it * B + b + 1)
            act.copy(self.spread[:, b % 2, :], PS[:, self.bank["t", b], 0:L]).then_inc(self.sp_sb, 1)

        with act.Fori(0, self.ROUNDS) as it:
            take_k(0, it)
            for n in range(-2, self.STEPS + 1):
                b, r = n // 4, n % 4
                if 0 <= n < self.STEPS and n % 2 == 1:
                    act.wait_ge(self.tr, it * self.STEPS + n + 1)
                    w = self.keys(n)
                    act.copy(self.pT[:, 1, 0:w], PS[:, self.T[1], 0:w]).then_inc(self.pt_a, 1)
                if n + 2 < self.STEPS:
                    m = n + 2
                    act.wait_ge(self.mx, it * self.STEPS + m + 1)
                    if m >= 2:
                        act.wait_ge(self.tr, it * self.STEPS + m - 1)
                    w = self.keys(m)
                    act.activation(self.probs[:, m % 2, 0:w], PS[:, self.S[m % 2], 0:w], ACT.Exp,
                                   bias=self.nmax[:, m % 4:m % 4 + 1], accum_out=self.sums[:, m % 8:m % 8 + 1]).then_inc(self.ex, 1)
                if 0 <= n < self.STEPS:
                    if r == 0 and b + 1 < B:
                        take_k(b + 1, it)
                    if r == 1 and b >= 1:
                        take_spread(b - 1, it)
            take_spread(B - 1, it)

class ShiftMix:

    def __init__(self, k, norm):
        self.yT_in = 2 * (norm + 1)
        self.k = k
        self.w_in = k.lb("mix_w_in", [P, 3, P])
        self.wT = k.lb("mix_wT", [P, 3, P])
        self.mu = k.lb("mix_mu", [P, 2])
        self.omu = k.lb("mix_one_minus_mu", [P, 2])
        self.xr = k.lb("mix_xr", [P, B, L])
        self.xk = k.lb("mix_xk", [P, B, L])
        self.kr = k.lb("mix_relu", [P, B * L])
        self.ka = k.lb("mix_k_act", [P, B * L])
        self.r = k.lb("mix_r", [P, TILES, P])
        self.t = k.lb("mix_t", [P, TILES, P])
        s = k.sem
        self.loaded, self.w_ps, self.w_sb = s("mix_loaded"), s("mix_w_turned"), s("mix_w_ready")
        self.mixed, self.own = s("mix_mixed"), s("mix_vector")
        self.k_ps, self.kr_sb, self.ka_sb = s("mix_k_product"), s("mix_relu_done"), s("mix_square_done")
        self.r_ps, self.r_sb, self.o_ps = s("mix_r_product"), s("mix_r_done"), s("mix_out_product")

    def load(self, sp, wr, wk, wv, mu_r, mu_k):
        for i, w in enumerate((wr, wk, wv)):
            sp.dma_start(self.w_in[:, i, :], w).then_inc(self.loaded, 16)
        for i, m in enumerate((mu_r, mu_k)):
            sp.dma_start(self.mu[:, i:i + 1], m.unsqueeze(1)).then_inc(self.loaded, 16)

    def tensor(self, pe):
        PS = self.k.PS
        pe.wait_ge(self.loaded, 80)
        for i in range(3):
            mm = pe.transpose(PS[:, 0, i * P:i * P + P], self.w_in[:, i, :], self.k.ident)
        mm.then_inc(self.w_ps, 1)
        pe.wait_ge(self.w_sb, 1)
        pe.wait_ge(self.mixed, 1)
        for f in range(2):
            pe.matmul(PS[:, 1 + f, :], self.wT[:, 1, :], self.xk[:, 2 * f:2 * f + 2, :].rearrange("p b l -> p (b l)"),
                      start=True, stop=True).then_inc(self.k_ps, 1)
        pe.wait_ge(self.mixed, 2)
        for t in range(TILES):
            mm = pe.matmul(PS[:, 3 + t // 4, (t % 4) * P:(t % 4) * P + P],
                           self.xr[:, t // 2, (t % 2) * P:(t % 2) * P + P], self.wT[:, 0, :], start=True, stop=True)
            if t % 4 == 3:
                mm.then_inc(self.r_ps, 1)
        for t in range(TILES):
            if t % 4 == 0:
                pe.wait_ge(self.ka_sb, t // 4 + 1)
            mm = pe.matmul(PS[:, (0, 5)[t // 4], (t % 4) * P:(t % 4) * P + P], self.ka[:, t * P:t * P + P], self.wT[:, 2, :],
                           start=True, stop=True)
            if t % 4 == 3:
                mm.then_inc(self.o_ps, 1)

    def vector(self, v):
        PS = self.k.PS
        v.wait_ge(self.loaded, 80)
        v.wait_ge(self.w_ps, 1)
        v.tensor_copy(self.wT[:, :, :], PS[:, 0, 0:3 * P].rearrange("p (i d) -> p i d", i=3)).then_inc(self.w_sb, 1)
        v.tensor_scalar(self.omu[:, :], self.mu[:, :], -1.0, 1.0, ALU.mult, ALU.add).then_inc(self.own, 1)
        v.wait_ge(self.k.ln.s_yT, self.yT_in)
        yT = self.k.yT[:, :].rearrange("p (b l) -> p b l", b=B)
        for i, dst in ((1, self.xk), (0, self.xr)):
            v.tensor_scalar(dst[:, :, :], yT, self.mu[:, i:i + 1], None, ALU.mult).then_inc(self.own, 1)
        for n, (i, dst) in enumerate(((1, self.xk), (0, self.xr))):
            v.wait_ge(self.own, 2 + n)
            v.scalar_tensor_tensor(dst[:, :, 1:L], yT[:, :, 0:L - 1], self.omu[:, i:i + 1], dst[:, :, 1:L],
                                   ALU.mult, ALU.add).then_inc(self.mixed, 1)
        for f in range(2):
            v.wait_ge(self.kr_sb, f + 1)
            r = slice(f * BANK, f * BANK + BANK)
            v.tensor_tensor(self.ka[:, r], self.kr[:, r], self.kr[:, r], ALU.mult).then_inc(self.ka_sb, 1)
        for f in range(2):
            v.wait_ge(self.o_ps, f + 1)
            v.wait_ge(self.r_sb, f + 1)
            r = slice(4 * f, 4 * f + 4)
            v.tensor_tensor(self.t[:, r, :], self.r[:, r, :], PS[:, (0, 5)[f], :].rearrange("p (t d) -> p t d", t=4),
                            ALU.mult).then_inc(self.own, 1)
            v.wait_ge(self.own, 4 + f)
            v.tensor_tensor(self.k.x[:, r, :], self.k.x[:, r, :], self.t[:, r, :], ALU.add)

    def scalar(self, act):
        PS = self.k.PS
        for f in range(2):
            act.wait_ge(self.k_ps, f + 1)
            act.activation(self.kr[:, f * BANK:f * BANK + BANK], PS[:, 1 + f, :], ACT.Relu).then_inc(self.kr_sb, 1)
        for f in range(2):
            act.wait_ge(self.r_ps, f + 1)
            act.activation(self.r[:, 4 * f:4 * f + 4, :], PS[:, 3 + f, :].rearrange("p (t d) -> p t d", t=4), ACT.Sigmoid).then_inc(self.r_sb, 1)

class NarrowAttention:

    S, T, O, G = (0, 1), (2, 3), (4, 5), (6, 7)
    ROWS = D8 + 2
    QR = HEADS8 * REG

    def __init__(self, k, name, norm, by_class):
        self.yT_in = 2 * (norm + 1)
        self.k, self.name, self.by_class = k, name, by_class
        n = name + "_"
        self.keys = L if by_class else S2
        self.width = L if by_class else S2 // 4
        self.heads = BANK // self.width
        self.steps = QT * HEADS8 // self.heads
        self.kts = self.width // P
        self.w_in = k.sb(n + "w_in", [P, 3, P])
        self.wo = k.sb(n + "wo", [P, 4, P])
        self.bo = k.sb(n + "bo", [P, P])
        if by_class:
            self.g = k.sb(n + "g", [P, P])
        else:
            self.bqp = k.sb(n + "bq", [P, 4])
            self.bkp = k.sb(n + "bk", [P, 4])
            self.bv_in = k.sb(n + "bv_in", [P, P])
            self.mask = k.sb(n + "mask", [1, B * S2 // 4], U32)
        s = k.sem
        self.loaded = s(n + "weights_loaded")
        self.padded = s(n + "weights_padded")
        self.zeroed = s(n + "zeroed")
        self.batch_in = s(n + "batch_in")
        self.product = s(n + "product")
        self.by_v, self.by_a = s(n + "taken_by_vector"), s(n + "taken_by_scalar")
        self.sc, self.mx, self.ex, self.tr = s(n + "scores"), s(n + "max"), s(n + "probs"), s(n + "turned")
        self.pt_v, self.pt_a = s(n + "pT_even"), s(n + "pT_odd")
        self.av, self.iv, self.nm = s(n + "pv"), s(n + "inverse"), s(n + "normed")
        self.cls_sb = s(n + "classes_ready")
        if by_class:
            self.own, self.powed, self.reduced = s(n + "find_vector"), s(n + "powed"), s(n + "ends_reduced")
            self.qn_ps, self.c_ps = s(n + "q_natural"), s(n + "classes_turned")
            self.rmx, self.riv = s(n + "r_max_done"), s(n + "r_inverse")
            self.ahead = {6: [("q", 0)], 7: [("q", 1)], 8: [("k", 0)], 10: [("k", 1)], 12: [("v", 0)], 13: [("v", 1)], 14: [("rq", 0)]}
            self.own_uses = {2: [("rs", 0)], 4: [("rt", 0)], 5: [("rp", 0)], 9: [("rm", 0), ("t", 0)], 11: [("o", 0)]}
            self.late = {1: [("t", 1)], 3: [("o", 1)]}
        else:
            self.ahead = {1: [("q", 0)], 2: [("q", 1)], 3: [("k", 0)], 4: [("k", 1), ("k", 2)], 5: [("k", 3)], 7: [("v", 0)]}
            self.own_uses = {5: [("t", 0)], 6: [("o", 0)]}
            self.late = {1: [("t", 1)], 2: [("o", 1)]}
        self.first = [u + (0,) for n in sorted(self.ahead) for u in self.ahead[n]]
        self.at = {}
        for n in range(2 * self.steps):
            par, r = n // self.steps, n % self.steps
            self.at[n] = ([u + (0,) for u in self.late.get(r, [])] if par else []) + [u + (par,) for u in self.own_uses.get(r, [])] \
                + [u + (1 - par,) for u in self.ahead.get(r, [])]
        self.last = [("t", 1, 1), ("o", 1, 1)]
        self.uses = [u for n in range(2 * self.steps) for u in self.at[n]] + self.last
        by_scalar = ("k", "rs", "rt", "t")
        self.is_a = lambda u: u[0] in by_scalar
        self.first_a, self.first_v = sum(map(self.is_a, self.first)), sum(not self.is_a(u) for u in self.first)
        self.a_uses = [u for u in self.uses if self.is_a(u)]
        self.v_uses = [u for u in self.uses if not self.is_a(u)]

    def bank(self, u, ahead):
        return self.G[(self.first.index(u) if ahead else len(self.first) + self.uses.index(u)) % 2]

    def wait_product(self, eng, u, it, ahead=False):
        if ahead:
            eng.wait_ge(self.product, self.first.index(u) + 1)
        else:
            eng.wait_ge(self.product, it * len(self.uses) + len(self.first) + self.uses.index(u) + 1)

    def wait_taken(self, eng, u, it, ahead=False):
        seq = self.first if ahead else self.uses
        same = [w for w in seq if self.is_a(w) == self.is_a(u)]
        n = same.index(u) + 1
        if self.is_a(u):
            eng.wait_ge(self.by_a, n if ahead else it * len(same) + self.first_a + n)
        else:
            eng.wait_ge(self.by_v, n + 1 if ahead else it * len(same) + self.first_v + n + 1)

    def place(self):
        k, by_class, n = self.k, self.by_class, self.name + "_"
        self.wq = k.lb(n + "wq", [P, 4 * P])
        self.wk = k.lb(n + "wk", [P, 4 * P])
        self.qp = k.lb(n + "q", [P, 2, 4, L])
        self.kp = k.lb(n + "k", [P, 2, 4, self.keys])
        self.wv = k.lb(n + "wv", [P, 4 * P])
        self.v = k.lb(n + "v", [P, 2, self.kts * 4 * P])
        self.yb = k.lb(n + "y_of_batch", [P, L])
        self.cqb = k.lb(n + "cq_of_batch", [2, L], BF16)
        self.ckb = k.lb(n + "ck_of_batch", [2, self.keys], BF16)
        self.ck = k.lb(n + "ck", [2, B * self.keys], BF16)
        self.probs = k.lb(n + "probs", [P, 2, BANK])
        self.pT = k.lb(n + "pT", [P, 2, BANK])
        self.nmax = k.lb(n + "nmax", [P, 2, self.heads])
        self.sums = k.lb(n + "sums", [P, QT, HEADS8])
        self.inv = k.lb(n + "inv", [P, QT, 4 * P])
        self.spread = k.lb(n + "inverse_spread", [P, QT, 4 * P])
        self.attT = k.lb(n + "attT", [P, QT, 4, P])
        if by_class:
            self.cq = k.lb(n + "cq", [2, B * L], BF16)
            self.gn = k.lb(n + "gn", [P, HEADS8])
            self.prod = self.probs[:, :, :].rearrange("p a (t d) -> p (a t) d", d=P)
            self.ss = k.lb(n + "ss", [P, TILES * HEADS8])
            self.dots = k.lb(n + "dots", [P, TILES * HEADS8])
            self.sim = k.lb(n + "sim", [P, TILES])
            self.ends = k.lb(n + "ends", [P, 2, TILES])
            self.ends_p = k.lb(n + "ends_of_partition", [P, 2])
            self.ends_2 = k.lb(n + "ends_diagonal", [2, 2])
            self.ends_1 = k.lb(n + "ends_row", [2, 1])
            self.ends_all = k.lb(n + "ends_all", [P, 2])
            self.span = k.lb(n + "span", [P, 1])
            self.cls = k.lb(n + "cls", [P, TILES, 4])
            self.qbd = k.lb(n + "q_registers", [P, 4, HEADS8, REG])
            self.rmax = k.lb(n + "r_max", [P, 1])
            self.rsum = k.lb(n + "r_sum", [P, 1])
            self.rinv = k.lb(n + "r_inv", [P, 1])
            self.rprobs = k.lb(n + "r_probs", [P, L])
            self.rpT = k.lb(n + "r_pT", [P, 2 * self.QR])
            self.ratt = k.lb(n + "r_att", [P, 4 * P])
        else:
            self.bv = k.lb(n + "bv", [P, 4 * P])
            self.cb = k.lb(n + "ctx_of_batch", [P, S2])

    def where(self, n):
        per = self.steps // QT
        qt, r = n % self.steps // per, n % per
        return qt, r % 4, range(self.heads * (r // 4), self.heads * (r // 4) + self.heads)

    def load(self, sp, wq, wk, wv, wo, bo, bq=None, bk=None, bv=None, mask=None, g=None):
        sp.wait_ge(self.zeroed, 1)
        for g4 in range(4):
            sp.dma_start(self.wo[32 * g4:32 * g4 + D8, :, :], wo.rearrange("(t g e) d -> g e t d", t=4, g=4)[g4]).then_inc(self.loaded, 16)
        for i, w in enumerate((wq, wk, wv)):
            sp.dma_start(self.w_in[:, i, :], w).then_inc(self.loaded, 16)
        sp.dma_start(self.bo[:, :], bo.unsqueeze(0).to_broadcast((P, P))).then_inc(self.loaded, 16)
        if self.by_class:
            sp.dma_start(self.g[:, :], g.unsqueeze(0).to_broadcast((P, P))).then_inc(self.loaded, 16)
            self.n_loads = 9 * 16
        else:
            sp.dma_start(self.bv_in[:, :], bv.unsqueeze(0).to_broadcast((P, P))).then_inc(self.loaded, 16)
            sp.dma_start(self.mask[:, :], mask.rearrange("(o b) s -> o (b s)", o=1)).then_inc(self.loaded, 16)
            sp.wait_ge(self.zeroed, 3)
            for dst, b in ((self.bqp, bq), (self.bkp, bk)):
                for gr in range(4):
                    sp.dma_start(dst[32 * gr:32 * gr + D8, :], b.rearrange("(t g e) -> g e t", t=4, g=4)[gr]).then_inc(self.loaded, 16)
            self.n_loads = 18 * 16

    def pool_zero(self, pool):
        pool.memset(self.wo[:, :, :], 0.0).then_inc(self.zeroed, 1)
        if not self.by_class:
            pool.memset(self.bqp[:, :], 0.0).then_inc(self.zeroed, 1)
            pool.memset(self.bkp[:, :], 0.0).then_inc(self.zeroed, 1)

    def pool_pad(self, pool):
        pool.memset(self.wq[:, :], 0.0).then_inc(self.zeroed, 1)
        pool.memset(self.wk[:, :], 0.0).then_inc(self.zeroed, 1)
        pool.memset(self.wv[:, :], 0.0).then_inc(self.zeroed, 1)
        if not self.by_class:
            pool.memset(self.cqb[:, :], 1.0)
            pool.memset(self.bv[:, :], 0.0)
            pool.memset(self.ck[:, :], 0.0).then_inc(self.zeroed, 1)
        pool.wait_ge(self.loaded, self.n_loads)
        pool.wait_ge(self.zeroed, 4 if self.by_class else 7)
        for i, w in ((0, self.wq), (1, self.wk), (2, self.wv)) if self.by_class else ((0, self.wq), (1, self.wk)):
            pool.tensor_copy(w[:, :].rearrange("p (h e) -> p h e", e=32)[:, :, 0:D8],
                             self.w_in[:, i, :].rearrange("p (h e) -> p h e", e=D8)).then_inc(self.padded, 1)
        if not self.by_class:
            for dst, src in ((self.wv, self.w_in[:, 2, :]), (self.bv, self.bv_in[:, :])):
                pool.tensor_copy(dst[:, :].rearrange("p (g t e) -> p g t e", g=4, t=4)[:, :, :, 0:D8],
                                 src.rearrange("p (t g e) -> p g t e", g=4, t=4)).then_inc(self.padded, 1)

    def pool_batches(self, pool):
        pool.wait_ge(self.cls_sb, 2)
        pool.wait_ge(self.k.ln.s_yT, self.yT_in)

        def bring(at):
            pool.tensor_copy(self.yb[:, :], self.k.yT[:, ds(at * L, L)])
            if self.by_class:
                pool.tensor_copy(self.cqb[:, :], self.cq[:, ds(at * L, L)])
            else:
                pool.tensor_copy(self.cb[:, :], self.k.ctxT[:, ds(at, 1), :].rearrange("p a s -> p (a s)"))
            pool.tensor_copy(self.ckb[:, :], self.ck[:, ds(at * self.keys, self.keys)]).then_inc(self.batch_in, 1)

        bring(0)
        for b in range(1, B):
            kind = "rq" if self.by_class else "v"
            if b == 1:
                self.wait_product(pool, (kind, 0, 0), 0, ahead=True)
            else:
                self.wait_product(pool, (kind, 0, (b - 1) % 2), (b - 2) // 2)
            bring(b)
        pool.drain().then_inc(self.batch_in, 1)

    def pool_find(self, pool):
        pool.wait_ge(self.own, 2)
        pool.tensor_tensor(self.gn[:, :], self.gn[:, :], self.k.ln.half[:, 0:HEADS8], ALU.pow).then_inc(self.powed, 1)
        pool.wait_ge(self.own, 6)
        pool.tensor_tensor(self.ss[:, :], self.ss[:, :], self.k.ln.half[:, :], ALU.pow).then_inc(self.powed, 1)

    def vector_find(self, v):
        cst = self.k.cst
        reg = cst[:, C_REG:C_REG + TILES]
        heads = lambda a: a.rearrange("p (h e) -> p h e", e=D8)
        v.wait_ge(self.loaded, self.n_loads)
        v.tensor_tensor(self.prod[:, 0, :], self.g[:, :], self.g[:, :], ALU.mult).then_inc(self.own, 1)
        v.wait_ge(self.own, 1)
        v.tensor_reduce(self.gn[:, :], heads(self.prod[:, 0, :]), AX.X, ALU.add).then_inc(self.own, 1)
        v.wait_ge(self.powed, 1)
        v.wait_ge(self.own, 2)
        v.tensor_tensor(heads(self.g[:, :]), heads(self.g[:, :]), self.gn[:, :].unsqueeze(2).to_broadcast((P, HEADS8, D8)),
                        ALU.mult).then_inc(self.own, 1)
        v.wait_ge(self.qn_ps, 1)
        qn = self.k.PS[:, 0:2, :].rearrange("p f (t d) -> p (f t) d", d=P)
        v.tensor_copy(self.prod, qn).then_inc(self.own, 1)
        v.wait_ge(self.own, 4)
        v.tensor_tensor(self.prod, self.prod, qn, ALU.mult).then_inc(self.own, 1)
        v.wait_ge(self.own, 5)
        flat = self.prod.rearrange("p t (h e) -> p (t h) e", e=D8)
        v.tensor_reduce(self.ss[:, :], flat, AX.X, ALU.add).then_inc(self.own, 1)
        v.wait_ge(self.own, 6)
        v.tensor_tensor(self.prod, qn, self.g[:, :].unsqueeze(1).to_broadcast((P, TILES, P)), ALU.mult).then_inc(self.own, 1)
        v.wait_ge(self.own, 7)
        v.tensor_reduce(self.dots[:, :], flat, AX.X, ALU.add).then_inc(self.own, 1)
        v.wait_ge(self.own, 8)
        v.wait_ge(self.powed, 2)
        v.tensor_tensor(self.dots[:, :], self.dots[:, :], self.ss[:, :], ALU.mult).then_inc(self.own, 1)
        v.wait_ge(self.own, 9)
        v.tensor_reduce(self.sim[:, :], self.dots[:, :].rearrange("p (t h) -> p t h", h=HEADS8), AX.X, ALU.add).then_inc(self.own, 1)
        v.wait_ge(self.own, 10)
        v.scalar_tensor_tensor(self.ends[:, 0, :], reg, -BIG, self.sim[:, :], ALU.mult, ALU.add).then_inc(self.own, 1)
        v.scalar_tensor_tensor(self.ends[:, 1, :], reg, -BIG, self.sim[:, :], ALU.mult, ALU.subtract).then_inc(self.own, 1)
        v.wait_ge(self.own, 12)
        v.tensor_reduce(self.ends_p[:, :], self.ends[:, :, :], AX.X, ALU.max).then_inc(self.own, 1)
        v.wait_ge(self.reduced, 1)
        v.tensor_reduce(self.ends_1[:, :], self.k.PS[0:2, 2, 0:P], AX.X, ALU.max).then_inc(self.own, 1)
        v.wait_ge(self.own, 14)
        v.tensor_scalar(self.ends_2[:, :], cst[0:2, C_ID:C_ID + 2], self.ends_1[:, 0:1], None, ALU.mult).then_inc(self.own, 1)
        v.wait_ge(self.reduced, 2)
        v.tensor_copy(self.ends_all[:, :], self.k.PS[:, 3, 0:2]).then_inc(self.own, 1)
        v.wait_ge(self.own, 16)
        v.tensor_tensor(self.span[:, :], self.ends_all[:, 0:1], self.ends_all[:, 1:2], ALU.add).then_inc(self.own, 1)
        v.wait_ge(self.own, 17)
        v.reciprocal(self.span[:, :], self.span[:, :]).then_inc(self.own, 1)
        v.wait_ge(self.own, 18)
        v.tensor_scalar(self.sim[:, :], self.sim[:, :], self.ends_all[:, 1:2], self.span[:, 0:1], ALU.add, ALU.mult).then_inc(self.own, 1)
        v.wait_ge(self.own, 19)
        c = self.cls
        v.scalar_tensor_tensor(c[:, :, 0], self.sim[:, :], 0.9, reg, ALU.is_gt, ALU.max).then_inc(self.own, 1)
        v.wait_ge(self.own, 20)
        v.tensor_scalar(c[:, :, 1], c[:, :, 0], -1.0, 1.0, ALU.mult, ALU.add).then_inc(self.own, 1)
        v.tensor_tensor(c[:, :, 3], reg, c[:, :, 0], ALU.subtract).then_inc(self.own, 1)
        v.wait_ge(self.own, 22)
        v.tensor_scalar(c[:, :, 2], c[:, :, 1], -BIG, None, ALU.mult).then_inc(self.own, 1)
        v.tensor_scalar(c[:, :, 3], c[:, :, 3], BIG, None, ALU.mult).then_inc(self.own, 1)
        v.wait_ge(self.c_ps, 1)
        for dst, bank in ((self.cq, 2), (self.ck, 4)):
            v.tensor_copy(dst[:, :].rearrange("p (f c) -> p f c", f=2), self.k.PS[0:2, bank:bank + 2, :]).then_inc(self.cls_sb, 1)

    def vector_padding(self, v):
        v.wait_ge(self.loaded, self.n_loads)
        v.wait_ge(self.zeroed, 7)
        v.tensor_scalar(self.ck[0:1, :], self.mask[:, :].bitcast(U8), -BIG, None, ALU.mult).then_inc(self.cls_sb, 2)

    def vector(self, v):
        PS, cst, x = self.k.PS, self.k.cst, self.k.x
        v.wait_ge(self.loaded, self.n_loads)
        v.tensor_tensor(x[:, :, :], x[:, :, :], self.bo[:, :].unsqueeze(1).to_broadcast((P, TILES, P)), ALU.add).then_inc(self.by_v, 1)
        if not self.by_class:
            v.wait_ge(self.padded, 4)

        def take(u, it, ahead=False):
            kind, i, par = u
            bank = PS[:, self.bank(u, ahead), :]
            self.wait_product(v, u, it, ahead)
            if kind == "q":
                if self.by_class:
                    v.tensor_scalar(self.qp[:, par, 2 * i:2 * i + 2, :], bank.rearrange("p (t l) -> p t l", t=2), SCALE8, None,
                                    ALU.mult).then_inc(self.by_v, 1)
                else:
                    for t in (2 * i, 2 * i + 1):
                        ins = v.tensor_scalar(self.qp[:, par, t, :], bank[:, (t % 2) * L:(t % 2) * L + L], self.bqp[:, t:t + 1], SCALE8,
                                              ALU.add, ALU.mult)
                    ins.then_inc(self.by_v, 1)
            elif kind == "v":
                if self.by_class:
                    v.tensor_copy(self.v[:, par, i * BANK:i * BANK + BANK], bank).then_inc(self.by_v, 1)
                else:
                    v.tensor_tensor(self.v[:, par, :], bank, self.bv[:, :], ALU.add).then_inc(self.by_v, 1)
            elif kind == "rq":
                v.tensor_tensor(self.qbd[:, :, :, :],
                                bank[:, 0:4 * REG].rearrange("p (t i) -> p t i", t=4).unsqueeze(2).to_broadcast((P, 4, HEADS8, REG)),
                                cst[:, C_OWN:C_OWN + 64].rearrange("p (t h) -> p t h", t=4).unsqueeze(3).to_broadcast((P, 4, HEADS8, REG)),
                                ALU.mult).then_inc(self.by_v, 1)
            elif kind == "rp":
                v.reciprocal(self.rinv[0:self.QR, :], self.rsum[0:self.QR, :]).then_inc(self.riv, 1)
                v.wait_ge(self.riv, it * 2 + par + 1)
                v.scalar_tensor_tensor(self.ratt[0:self.QR, :], bank[0:self.QR, :], self.rinv[0:self.QR, 0:1],
                                       cst[0:self.QR, C_DIAG:C_DIAG + 4 * P], ALU.mult, ALU.mult).then_inc(self.by_v, 1)
            elif kind == "rm":
                v.wait_ge(self.nm, it * 2 * QT + par * QT + 1)
                first = self.attT[:, 0, :, 0:REG]
                v.scalar_tensor_tensor(first, first, 0.5, bank[:, 0:4 * REG].rearrange("p (t i) -> p t i", t=4), ALU.mult, ALU.add).then_inc(self.by_v, 1)
            else:
                row = x[:, ds(it * 2 * QT + par * QT + i, 1), :].rearrange("p a d -> p (a d)")
                v.tensor_tensor(row, row, bank[:, 0:P], ALU.add).then_inc(self.by_v, 1)

        def normalise(u, it):
            _, qt, par = u
            self.wait_taken(v, u, it)
            v.wait_ge(self.av, it * 2 * self.steps + par * self.steps + (qt + 1) * per)
            v.tensor_tensor(self.attT[:, qt, :, :].rearrange("p t l -> p (t l)"), PS[:, self.O[qt], :], self.spread[:, qt, :],
                            ALU.mult).then_inc(self.nm, 1)

        def maximum(n, it):
            v.wait_ge(self.sc, it * 2 * self.steps + n + 1)
            v.tensor_reduce(self.nmax[:, n % 2, :], PS[:, self.S[n % 2], :].rearrange("p (j s) -> p j s", j=self.heads), AX.X, ALU.max,
                            negate=True).then_inc(self.mx, 1)

        per = self.steps // QT
        def invert(n, it):
            qt = self.where(n)[0]
            v.wait_ge(self.ex, it * 2 * self.steps + n + 1)
            v.reciprocal(self.inv[:, qt, :].rearrange("p (h f) -> p h f", f=32),
                         self.sums[:, qt, :].unsqueeze(2).to_broadcast((P, HEADS8, 32))).then_inc(self.iv, 1)

        for u in self.first:
            if not self.is_a(u):
                take(u, 0, ahead=True)
        with v.Fori(0, B // 2) as it:
            for n in range(-2, 2 * self.steps + 1):
                if 0 <= n < 2 * self.steps and n % 2 == 0:
                    v.wait_ge(self.tr, it * 2 * self.steps + n + 1)
                    v.tensor_copy(self.pT[:, 0, :], PS[:, self.T[0], :]).then_inc(self.pt_v, 1)
                if n + 2 < 2 * self.steps:
                    maximum(n + 2, it)
                if n >= per and n % per == 0:
                    invert(n - 1, it)
                for u in sorted(self.at.get(n, []), key=lambda u: u[0] != "t"):
                    if u[0] == "t":
                        normalise(u, it)
                    elif u[0] == "rs":
                        self.wait_product(v, u, it)
                        v.tensor_reduce(self.rmax[0:self.QR, :], PS[0:self.QR, self.bank(u, False), 0:L], AX.X, ALU.max, negate=True).then_inc(self.rmx, 1)
                    elif not self.is_a(u):
                        take(u, it)
            normalise(self.last[0], it)
            take(self.last[1], it)

    def scalar(self, act):
        PS = self.k.PS

        def take(u, it, ahead=False):
            kind, i, par = u
            bank = PS[:, self.bank(u, ahead), :]
            self.wait_product(act, u, it, ahead)
            if kind == "k":
                if self.by_class:
                    act.copy(self.kp[:, par, 2 * i:2 * i + 2, :], bank.rearrange("p (t l) -> p t l", t=2)).then_inc(self.by_a, 1)
                else:
                    act.activation(self.kp[:, par, i, :], bank, ACT.Identity, bias=self.bkp[:, i:i + 1]).then_inc(self.by_a, 1)
            elif kind == "rs":
                act.wait_ge(self.rmx, it * 2 + par + 1)
                act.activation(self.rprobs[0:self.QR, :], bank[0:self.QR, 0:L], ACT.Exp, bias=self.rmax[0:self.QR, 0:1],
                               accum_out=self.rsum[0:self.QR, :]).then_inc(self.by_a, 1)
            elif kind == "rt":
                act.copy(self.rpT[:, :], bank[:, 0:2 * self.QR]).then_inc(self.by_a, 1)
            else:
                act.copy(self.spread[:, i, :], bank).then_inc(self.by_a, 1)

        def exponent(n, it):
            act.wait_ge(self.mx, it * 2 * self.steps + n + 1)
            if n >= 2:
                act.wait_ge(self.tr, it * 2 * self.steps + n - 1)
            qt, g, quads = self.where(n)
            for j, t in enumerate(quads):
                h = 4 * t + g
                cols = slice(j * self.width, j * self.width + self.width)
                ins = act.activation(self.probs[:, n % 2, cols], PS[:, self.S[n % 2], cols], ACT.Exp, bias=self.nmax[:, n % 2, j:j + 1],
                                     accum_out=self.sums[:, qt, h:h + 1])
            ins.then_inc(self.ex, 1)

        for u in self.first:
            if self.is_a(u):
                take(u, 0, ahead=True)
        with act.Fori(0, B // 2) as it:
            for n in range(-2, 2 * self.steps):
                if n >= 0 and n % 2 == 1:
                    act.wait_ge(self.tr, it * 2 * self.steps + n + 1)
                    act.copy(self.pT[:, 1, :], PS[:, self.T[1], :]).then_inc(self.pt_a, 1)
                if n + 2 < 2 * self.steps:
                    exponent(n + 2, it)
                for u in self.at.get(n, []):
                    if self.is_a(u):
                        take(u, it)
            take(self.last[0], it)

    def tensor_find(self, pe):
        PS = self.k.PS
        pe.wait_ge(self.loaded, self.n_loads)
        pe.wait_ge(self.k.ln.s_yT, self.yT_in)
        for t in range(TILES):
            mm = pe.matmul(PS[:, t // 4, (t % 4) * P:(t % 4) * P + P], self.k.yT[:, t * P:t * P + P], self.w_in[:, 0, :], start=True, stop=True)
        mm.then_inc(self.qn_ps, 1)
        pe.wait_ge(self.own, 13)
        pe.transpose(PS[0:2, 2, 0:P], self.ends_p[:, :], self.k.ident).then_inc(self.reduced, 1)
        pe.wait_ge(self.own, 15)
        pe.matmul(PS[:, 3, 0:2], self.k.cst[0:2, C_ONE:C_ONE + P], self.ends_2[:, :], start=True, stop=True).then_inc(self.reduced, 1)
        pe.wait_ge(self.own, 24)
        for side, bank in ((0, 2), (2, 4)):
            for t in range(TILES):
                mm = pe.transpose(PS[0:2, bank + t // 4, (t % 4) * P:(t % 4) * P + P], self.cls[:, t, side:side + 2], self.k.ident)
        mm.then_inc(self.c_ps, 1)

    def tensor(self, pe):
        PS, cst, ident = self.k.PS, self.k.cst, self.k.ident
        pe.wait_ge(self.padded, 3 if self.by_class else 4)
        pe.wait_ge(self.cls_sb, 2)
        src = self.yb if self.by_class else self.cb
        classes, negative = self.k.classb[:, 0:P], self.k.classb[:, P:P + REG]

        def product(u, it, ahead=False):
            kind, i, par = u
            bank = PS[:, self.bank(u, ahead), :]
            seq = self.first if ahead else self.uses
            if seq.index(u) >= 2:
                self.wait_taken(pe, seq[seq.index(u) - 2], it, ahead)
            if u[0:2] == ("q", 0):
                pe.wait_ge(self.batch_in, 1 if ahead else it * 2 + (2 if par else 3))
            if kind == "q":
                for t in (2 * i, 2 * i + 1):
                    out = bank[:, (t % 2) * L:(t % 2) * L + L]
                    pe.matmul(out, self.wq[:, t * P:t * P + P], self.yb[:, :], start=True, stop=False)
                    mm = pe.matmul(out, classes, self.cqb[:, :], start=False, stop=True)
            elif kind == "k":
                for t in ((2 * i, 2 * i + 1) if self.by_class else (i,)):
                    out = bank[:, (t % 2) * L:(t % 2) * L + L] if self.by_class else bank
                    pe.matmul(out, self.wk[:, t * P:t * P + P], src[:, :], start=True, stop=False)
                    mm = pe.matmul(out, classes, self.ckb[:, :], start=False, stop=True)
            elif kind == "v":
                if self.by_class:
                    mm = pe.matmul(bank, src[:, i * P:i * P + P], self.wv[:, :], start=True, stop=True)
                else:
                    for j in range(4):
                        mm = pe.matmul(bank[:, j * P:j * P + P], src[:, j::4], self.wv[:, j * P:j * P + P], start=True, stop=True)
            elif kind == "rq":
                for t in range(4):
                    pe.matmul(bank[:, t * REG:t * REG + REG], self.wq[:, t * P:t * P + P], self.yb[:, 0:REG], start=True, stop=False)
                    mm = pe.matmul(bank[:, t * REG:t * REG + REG], classes, negative, start=False, stop=True)
            elif kind == "rs":
                if par:
                    self.wait_taken(pe, ("rq", 0, 1), it)
                for t in range(4):
                    mm = pe.matmul(bank[0:self.QR, 0:L], self.qbd[:, t, :, :].rearrange("p h i -> p (h i)"), self.kp[:, par, t, :],
                                   start=(t == 0), stop=(t == 3))
            elif kind == "rt":
                self.wait_taken(pe, ("rs", 0, par), it)
                for kt in range(2):
                    mm = pe.transpose(bank[:, kt * self.QR:kt * self.QR + self.QR], self.rprobs[0:self.QR, kt * P:kt * P + P],
                                      ident[0:self.QR, 0:self.QR])
            elif kind == "rp":
                self.wait_taken(pe, ("rt", 0, par), it)
                for kt in range(2):
                    mm = pe.matmul(bank[0:self.QR, :], self.rpT[:, kt * self.QR:kt * self.QR + self.QR], self.v[:, par, kt * BANK:kt * BANK + BANK],
                                   start=(kt == 0), stop=(kt == 1))
            elif kind == "rm":
                self.wait_taken(pe, ("rp", 0, par), it)
                for t in range(4):
                    mm = pe.matmul(bank[:, t * REG:t * REG + REG], self.ratt[0:self.QR, t * P:t * P + P], cst[0:self.QR, C_SUM:C_SUM + REG],
                                   start=True, stop=True)
            elif kind == "t":
                pe.wait_ge(self.iv, it * 2 * QT + par * QT + i + 1)
                for t in range(4):
                    mm = pe.matmul(bank[:, t * P:t * P + P], self.inv[:, i, t * P:t * P + P], ident,
                                   start=True, stop=True)
            else:
                pe.wait_ge(self.nm, it * 2 * QT + par * QT + i + 1)
                if self.by_class and i == 0:
                    self.wait_taken(pe, ("rm", 0, par), it)
                for t in range(4):
                    mm = pe.matmul(bank[:, 0:P], self.attT[:, i, t, :], self.wo[:, t, :], start=(t == 0), stop=(t == 3))
            mm.then_inc(self.product, 1)

        def scores(n, it):
            par = n // self.steps
            if n == self.steps:
                self.wait_taken(pe, ("k", 1 if self.by_class else 3, 1), it)
                self.wait_taken(pe, ("q", 1, 1), it)
            if n >= 2:
                pe.wait_ge(self.ex, it * 2 * self.steps + n - 1)
            qt, g, quads = self.where(n)
            rows = slice(32 * g, 32 * g + self.ROWS)
            for j, t in enumerate(quads):
                keys = self.kp[rows, par, t, :] if self.by_class else self.kp[rows, par, t, g::4]
                mm = pe.matmul(PS[:, self.S[n % 2], j * self.width:j * self.width + self.width], self.qp[rows, par, t, qt * P:qt * P + P], keys,
                               start=True, stop=True)
            mm.then_inc(self.sc, 1)

        def turn(n, it):
            pe.wait_ge(self.ex, it * 2 * self.steps + n + 1)
            if n >= 2:
                pe.wait_ge(self.pt_a if n % 2 else self.pt_v, it * self.steps + n // 2)
            for j in range(BANK // P):
                mm = pe.transpose(PS[:, self.T[n % 2], j * P:j * P + P], self.probs[:, n % 2, j * P:j * P + P], ident)
            mm.then_inc(self.tr, 1)

        def times_v(n, it):
            par = n // self.steps
            if n == self.steps:
                self.wait_taken(pe, ("v", 1 if self.by_class else 0, 1), it)
            pe.wait_ge(self.pt_a if n % 2 else self.pt_v, it * self.steps + n // 2 + 1)
            qt, g, quads = self.where(n)
            for j, t in enumerate(quads):
                h = 4 * t + g
                for kt in range(self.kts):
                    at = kt * BANK + 32 * h if self.by_class else 32 * (4 * g + t)
                    mm = pe.matmul(PS[32 * g:32 * g + 32, self.O[qt], t * P:t * P + P], self.v[:, par, at:at + 32],
                                   self.pT[:, n % 2, (j * self.kts + kt) * P:(j * self.kts + kt) * P + P],
                                   start=(kt == 0), stop=(kt == self.kts - 1))
            mm.then_inc(self.av, 1)

        for u in self.first:
            product(u, 0, ahead=True)
        with pe.Fori(0, B // 2) as it:
            pe.wait_ge(self.by_v, it * len(self.v_uses) + self.first_v + 1)
            pe.wait_ge(self.by_a, it * len(self.a_uses) + self.first_a)
            for n in range(-2, 2 * self.steps + 1):
                if 0 <= n < 2 * self.steps:
                    turn(n, it)
                if n + 2 < 2 * self.steps:
                    scores(n + 2, it)
                if n >= 1:
                    times_v(n - 1, it)
                for u in self.at.get(n, []):
                    product(u, it)
            for u in self.last:
                product(u, it)

class Warping:

    LANES, E = S2 // 32, 32
    HAND = 2
    COLS = 32
    HALF = COLS // 2
    SLOTS = L + LANES * HAND
    ROUNDS = SLOTS // COLS
    ROW = 2 * (E + 1) + 2 * E + 1

    def __init__(self, k, norm):
        self.yT_in = 2 * (norm + 1)
        self.k = k
        E, SLOTS, COLS, LANES = self.E, self.SLOTS, self.COLS, self.LANES
        self.DL = k.lb("w_distances", [P, SLOTS + self.HALF, E])
        self.CUT = k.lb("w_up_table", [P, SLOTS, 66], BF16)
        self.MH = k.lb("w_path", [P, SLOTS, E], BF16)
        self.aa = k.lb("w_aa", [P, LANES])
        self.tick = k.lb("w_tick", [P, 1])
        self.bb = k.lb("w_bb", [P, L])

        def phase(*buffers):
            with ExitStack() as place:
                return [place.enter_context(k.nc.sbuf_tensor("w_" + n, s, d)) for n, s, d in buffers]

        self.sq, self.d2, self.ones = phase(("squares", [P, 2048], F32), ("d2", [P, 2, 2, L], F32), ("ones", [P, 32], F32))
        self.DLr, self.Dr, self.R, self.Mn, self.An, self.Gt, self.Lr, self.Ur, self.Tr = phase(
            ("d_ring_in", [P, COLS, E], F32), ("d_ring", [P, COLS, E], F32), ("R", [P, COLS + 1, E + 1], F32), ("min", [P, E], F32),
            ("min2", [P, 2, E], F32), ("gt2", [P, 2, E], F32), ("left", [P, COLS, E], BF16), ("up", [P, COLS, E], BF16),
            ("left_or_up", [P, COLS, E], BF16))
        self.CB, self.CTr, self.CUr = phase(("flags", [P, COLS, self.ROW], F32), ("table_ring", [P, COLS, E, 2], BF16),
                                            ("up_ring", [P, COLS, 2 * E], BF16))
        self.MF, = phase(("mask", [P, LANES, L], F32))
        self.CT = self.DL[:, 0:SLOTS, :].bitcast(BF16).rearrange("p s (e k) -> p s e k", k=2)
        self.MT = self.DL[:, 0:SLOTS // 2, :].bitcast(BF16).rearrange("p s (h e) -> p (s h) e", h=2)
        s = k.sem
        self.zeroed, self.sq_done = s("w_zeroed"), s("w_squares_done")
        self.bb_ps, self.bb_sb = s("w_bb_product"), s("w_bb_ready")
        self.ab_ps, self.d2_done, self.dist_done, self.root_done = s("w_ab_product"), s("w_d2_done"), s("w_clamped"), s("w_root_done")
        self.dve = s("w_column_chain")
        self.dl_in, self.dl_used, self.choices, self.sums, self.tables = (
            s("w_d_ring_in"), s("w_d_ring_used"), s("w_choices"), s("w_left_or_up"), s("w_tables_saved"))
        self.fwd0, self.tab_in, self.half_done = s("w_path_started"), s("w_tables_in"), s("w_half_done")
        self.mt_done, self.mf_v, self.mf_a, self.ex_ps = s("w_mask_turned"), s("w_mask_even"), s("w_mask_odd"), s("w_expanded")

    def pool_before(self, pool):
        pool.memset(self.DL[:, :, :], 0.0).then_inc(self.zeroed, 1)
        pool.memset(self.CUT[:, :, :], 1.0)
        pool.memset(self.ones[:, :], 1.0).then_inc(self.zeroed, 1)
        pool.wait_ge(self.zeroed, 2)
        pool.memset(self.DL[:, self.HAND - 1, 0:1], BIG).then_inc(self.zeroed, 1)

    def pool_forward(self, pool):
        with pool.Fori(0, self.ROUNDS) as it:
            for h in range(2):
                pool.wait_ge(self.choices, it * 2 + h + 1)
                r = slice(self.HALF * h, self.HALF * h + self.HALF)
                pool.tensor_tensor(self.Tr[:, r, :], self.Lr[:, r, :], self.Ur[:, r, :], ALU.add).then_inc(self.sums, 1)

    def tensor_distances(self, pe):
        PS, k, E = self.k.PS, self.k, self.E
        pe.wait_ge(self.sq_done, 1)
        pe.wait_ge(self.zeroed, 2)
        for b in range(B):
            mm = pe.matmul(PS[32 * b:32 * b + 32, 7, 0:L], self.ones[:, :], self.sq[:, b * L:b * L + L], start=True, stop=True)
        mm.then_inc(self.bb_ps, 1)
        for h in range(self.LANES // 2):
            if h >= 2:
                pe.wait_ge(self.d2_done, h - 1)
            for p in (2 * h, 2 * h + 1):
                for b in range(B):
                    mm = pe.matmul(PS[32 * b:32 * b + 32, h % 2, (p % 2) * L:(p % 2) * L + L],
                                   k.ctxT[:, b, E * p:E * p + E], k.yT[:, b * L:b * L + L], start=True, stop=True)
            mm.then_inc(self.ab_ps, 1)

    def tensor_expand(self, pe):
        PS = self.k.PS
        for jt in range(QT):
            for p in range(self.LANES):
                pe.wait_ge(self.mf_a if p % 2 else self.mf_v, jt * self.LANES // 2 + p // 2 + 1)
                for b in range(B):
                    mm = pe.matmul(PS[:, b, jt * D:jt * D + D], self.MF[32 * b:32 * b + 32, p, jt * P:jt * P + P],
                                   self.k.ctxP[32 * b:32 * b + 32, p, :], start=(p == 0), stop=(p == self.LANES - 1))
        mm.then_inc(self.ex_ps, 1)

    def scalar_distances(self, act):
        act.wait_ge(self.k.ln.s_yT, self.yT_in)
        act.activation(self.sq[:, 0:B * L], self.k.yT[:, :], ACT.Square).then_inc(self.sq_done, 1)
        act.wait_ge(self.zeroed, 3)
        for h in range(self.LANES // 2):
            for p in (2 * h, 2 * h + 1):
                act.wait_ge(self.dist_done, p + 1)
                act.activation(self.DL[:, self.HAND * (p + 1):self.HAND * (p + 1) + L, p], self.d2[:, h % 2, p % 2, :],
                               ACT.Sqrt).then_inc(self.root_done, 1)

    def scalar_forward(self, act):
        HALF, COLS = self.HALF, self.COLS
        act.copy(self.DLr[:, 0:HALF, :], self.DL[:, 0:HALF, :]).then_inc(self.dl_in, 1)
        with act.Fori(0, self.ROUNDS) as it:
            act.wait_ge(self.dl_used, it * 2 + 1)
            act.copy(self.DLr[:, HALF:COLS, :], self.DL[:, ds(it * COLS + HALF, HALF), :]).then_inc(self.dl_in, 1)
            act.copy(self.DLr[:, 0:HALF, :], self.DL[:, ds(it * COLS + COLS, HALF), :]).then_inc(self.dl_in, 1)
            for h in range(2):
                act.wait_ge(self.sums, it * 2 + h + 1)
                r = slice(HALF * h, HALF * h + HALF)
                slots = ds(it * COLS + HALF * h, HALF)
                act.activation(self.CT[:, slots, :, 0], self.Tr[:, r, :], ACT.Copy, bias=1.0, scale=-1.0)
                act.activation(self.CT[:, slots, :, 1], self.Lr[:, r, :], ACT.Copy)
                act.activation(self.CUT[:, slots, 1:65:2], self.Ur[:, r, :], ACT.Copy).then_inc(self.tables, 1)

    def scalar_backward(self, act):
        HALF, COLS, SLOTS = self.HALF, self.COLS, self.SLOTS
        act.wait_ge(self.fwd0, 1)

        def load_tables(slot, half):
            r = slice(HALF * half, HALF * half + HALF)
            act.copy(self.CTr[:, r, :, :], self.CT[:, ds(slot, HALF), :, :])
            act.copy(self.CUr[:, r, :], self.CUT[:, ds(slot, HALF), 2:66]).then_inc(self.tab_in, 1)

        def backward_round(it, last):
            for half in (1, 0):
                slot = SLOTS - COLS + HALF * half - it * COLS
                act.wait_ge(self.half_done, it * 2 + 2 - half)
                act.copy(self.MH[:, ds(slot, HALF), :], self.CB[:, HALF * half:HALF * half + HALF, 66:130:2])
                if not last:
                    load_tables(slot - COLS, half)

        load_tables(SLOTS - HALF, 1)
        load_tables(SLOTS - COLS, 0)
        with act.Fori(0, self.ROUNDS - 1) as it:
            backward_round(it, False)
        backward_round(self.ROUNDS - 1, True)

    def take_mask(self, eng, copy, jt, p, done):
        copy(self.MF[:, p, jt * P:jt * P + P],
             self.MT[:, self.HAND * (p + 1) + jt * P:self.HAND * (p + 1) + jt * P + P, p]).then_inc(done, 1)

    def scalar_expand(self, act):
        act.wait_ge(self.mt_done, 4)
        for jt in range(QT):
            for p in range(1, self.LANES, 2):
                self.take_mask(act, act.copy, jt, p, self.mf_a)

    def vector_distances(self, v):
        PS, k, ctxP = self.k.PS, self.k, self.k.ctxP[:, :, :].rearrange("p a d -> p (a d)")
        v.wait_ge(self.bb_ps, 1)
        v.tensor_copy(self.bb[:, :], PS[:, 7, 0:L]).then_inc(self.bb_sb, 1)
        v.wait_ge(self.bb_sb, 1)
        v.tensor_tensor(self.sq[:, :], ctxP, ctxP, ALU.mult).then_inc(self.bb_sb, 1)
        v.wait_ge(self.bb_sb, 2)
        v.tensor_reduce(self.aa[:, :], self.sq[:, :].rearrange("p (a d) -> p a d", d=D), AX.X, ALU.add).then_inc(self.bb_sb, 1)
        v.wait_ge(self.bb_sb, 3)
        for h in range(self.LANES // 2):
            v.wait_ge(self.ab_ps, h + 1)
            if h >= 2:
                v.wait_ge(self.root_done, 2 * h - 2)
            v.scalar_tensor_tensor(self.d2[:, h % 2, :, :], PS[:, h % 2, :].rearrange("p (a l) -> p a l", a=2), -2.0,
                                   self.bb[:, :].unsqueeze(1).to_broadcast((P, 2, L)), ALU.mult, ALU.add).then_inc(self.d2_done, 1)
            v.wait_ge(self.d2_done, h + 1)
            for p in (2 * h, 2 * h + 1):
                v.tensor_scalar(self.d2[:, h % 2, p % 2, :], self.d2[:, h % 2, p % 2, :], self.aa[:, p:p + 1], 0.0,
                                ALU.add, ALU.max).then_inc(self.dist_done, 1)

    def vector_forward(self, v):
        E, COLS, HALF, HAND, LANES, R = self.E, self.COLS, self.HALF, self.HAND, self.LANES, self.R
        Lr, Ur, An, Gt, Mn, dve = self.Lr, self.Ur, self.An, self.Gt, self.Mn, self.dve
        v.memset(R[:, :, :], BIG).then_inc(dve, 1)
        v.memset(Lr[:, :, :], 0.0).then_inc(self.tables, 2)
        v.wait_ge(self.dl_in, 1)

        def to_lanes(half):
            r = slice(HALF * half, HALF * half + HALF)
            v.transpose(self.Dr[:, r, :].rearrange("p c e -> p (c e)"), self.DLr[:, r, :].rearrange("p c e -> p (c e)")).then_inc(self.dl_used, 1)

        to_lanes(0)
        v.wait_ge(dve, 1)
        v.tensor_copy(R[:, HAND, 0:1], self.k.cst[:, C_HALO:C_HALO + 1]).then_inc(dve, 1)
        v.wait_ge(dve, 2)
        v.sem_clear(dve)
        above = [31] + list(range(LANES - 1)) + [31] * (32 - LANES)
        with v.Fori(0, self.ROUNDS) as it:
            k = 0
            chain = 0
            pair = None

            def choice(c, q):
                nonlocal k
                diag, left, up = R[:, c:c + 2, 0:E], R[:, c:c + 2, 1:E + 1], R[:, c + 1:c + 3, 0:E]
                if q == 0:
                    v.tensor_tensor(An[:, :, :], diag, up, ALU.min).then_inc(dve, 1)
                elif q == 1:
                    v.tensor_tensor(Gt[:, :, :], diag, up, ALU.is_gt).then_inc(dve, 1)
                elif q == 2:
                    if c % HALF == 0:
                        v.wait_ge(self.tables, it * 2 + 1 + c // HALF)
                    v.tensor_tensor(Lr[:, c:c + 2, :], An[:, :, :], left, ALU.is_gt).then_inc(dve, 1)
                else:
                    v.wait_ge(dve, k)
                    done = self.choices if c % HALF == HALF - 2 else dve
                    v.tensor_tensor(Ur[:, c:c + 2, :], Gt[:, :, :], Lr[:, c:c + 2, :], ALU.is_gt).then_inc(done, 1)
                    if done is self.choices:
                        return
                k += 1

            for c in range(COLS):
                if chain:
                    v.wait_ge(dve, chain)
                v.tensor_tensor(Mn[:, :], R[:, c, 0:E], R[:, c, 1:E + 1], ALU.min).then_inc(dve, 1)
                k += 1
                chain = k
                if pair is not None:
                    choice(pair, 0 if c % 2 == 0 else 2)
                if c == 0:
                    v.wait_ge(self.dl_in, it * 2 + 2)
                    to_lanes(1)
                    v.wait_ge(self.dl_used, it * 2 + 1)
                if c == HALF:
                    v.wait_ge(self.dl_in, it * 2 + 3)
                    to_lanes(0)
                    v.wait_ge(self.dl_used, it * 2 + 2)
                v.wait_ge(dve, chain)
                v.tensor_tensor_scan(R[:, c + 1, 1:E + 1], Mn[:, :], self.Dr[:, c, :], R[:, c + 1, 0:1], ALU.min, ALU.add).then_inc(dve, 1)
                k += 1
                chain = k
                if pair is not None:
                    choice(pair, 1 if c % 2 == 0 else 3)
                if c % 2 == 1:
                    pair = c - 1
                if c % HAND == HAND - 1:
                    n = (c + 1) % COLS + 1
                    v.wait_ge(dve, chain)
                    v.stream_shuffle(R[:, n:n + HAND, 0], R[:, c + 2 - HAND:c + 2, E], mask=above).then_inc(dve, 1)
                    k += 1
            for q in range(4):
                v.wait_ge(dve, k)
                choice(COLS - 2, q)
            v.tensor_copy(R[:, 0, :], R[:, COLS, :]).then_inc(dve, 1)
            k += 1
            v.wait_ge(dve, k)
            v.sem_clear(dve)

    def vector_backward(self, v):
        E, COLS, HALF, HAND, LANES, ROW, CB, dve = self.E, self.COLS, self.HALF, self.HAND, self.LANES, self.ROW, self.CB, self.dve
        below = list(range(1, LANES)) + [31] * (32 - LANES + 1)
        v.memset(CB[:, :, :], 0.0).then_inc(dve, 1)
        v.stream_shuffle(self.CUT[:, 0:self.SLOTS - HAND, 65], self.CUT[:, HAND:self.SLOTS, 1], mask=below).then_inc(dve, 1)
        v.wait_ge(dve, 2)
        v.tensor_copy(CB[:, COLS - 1, 65:66], self.k.cst[:, C_START:C_START + 1]).then_inc(self.fwd0, 1)
        v.wait_ge(self.fwd0, 1)
        v.sem_clear(dve)
        with v.Fori(0, self.ROUNDS) as it:
            k = 0
            for c in reversed(range(COLS)):
                if c % HALF == HALF - 1:
                    v.wait_ge(self.tab_in, it * 2 + (1 if c > HALF else 2))
                if k:
                    v.wait_ge(dve, k)
                v.tensor_tensor_scan(CB[:, c, 129:65:-1], self.CUr[:, c, 63::-1], CB[:, c, 65:1:-1], CB[:, c, 130:131],
                                     ALU.mult, ALU.add).then_inc(dve, 1)
                k += 1
                v.wait_ge(dve, k)
                if c % HAND == 0:
                    n = (c - HAND) % COLS
                    v.stream_shuffle(CB[:, n:n + HAND, 64:131:66], CB[:, c:c + HAND, 0:67:66], mask=below).then_inc(dve, 1)
                    k += 1
                sent = bass.AP(tensor=CB, offset=((c - 1) % COLS) * ROW, ap=[[COLS * ROW, P], [2, E], [3, 2]])
                v.tensor_tensor(sent, CB[:, c, 66:130:2].unsqueeze(2).to_broadcast((P, E, 2)), self.CTr[:, c, :, :],
                                ALU.mult).then_inc(self.half_done if c == HALF else dve, 1)
                if c == HALF:
                    v.wait_ge(self.half_done, it * 2 + 1)
                else:
                    k += 1
            v.wait_ge(dve, k)
            v.sem_clear(dve)
            v.memset(self.tick[:, :], 0.0).then_inc(self.half_done, 1)

    def vector_expand(self, v):
        n = self.SLOTS // 4 * self.E
        MT, MH = (a[:, :, :].rearrange("p s e -> p (s e)") for a in (self.MT, self.MH))
        for q in range(4):
            v.transpose(MT[:, q * n:q * n + n], MH[:, q * n:q * n + n]).then_inc(self.mt_done, 1)
        v.wait_ge(self.mt_done, 4)
        for jt in range(QT):
            for p in range(0, self.LANES, 2):
                self.take_mask(v, v.tensor_copy, jt, p, self.mf_v)
        v.wait_ge(self.ex_ps, 1)
        x = self.k.x
        for b in range(B):
            v.tensor_tensor(x[:, 2 * b:2 * b + 2, :], x[:, 2 * b:2 * b + 2, :], self.k.PS[:, b, 0:L].rearrange("p (t d) -> p t d", t=QT), ALU.add)

class SpikingMoE:

    NE, M, H = 8, 64, 256

    def __init__(self, k, norm):
        self.norm = norm
        self.k = k
        NE, M, H = self.NE, self.M, self.H
        self.enc_w, self.enc_b = k.sb("moe_enc_w", [P, H]), k.sb("moe_enc_b", [P, 2])
        self.s2c_w, self.s2c_b = k.sb("moe_s2c_w", [P, 2, M]), k.sb("moe_s2c_b", [M, 1])
        self.r1_w, self.r1_b = k.sb("moe_router1_w", [M, 64]), k.sb("moe_router1_b", [64, 1])
        self.r2_w, self.r2_b = k.sb("moe_router2_w", [64, NE]), k.sb("moe_router2_b", [P, NE])
        self.e1_w, self.e1_b = k.sb("moe_e1_w", [M, NE, P]), k.sb("moe_e1_b", [P, NE])
        self.e2_w, self.e2_b = k.sb("moe_e2_w", [P, NE, M]), k.sb("moe_e2_b", [1, NE * M])
        self.c2s_w, self.c2s_b = k.sb("moe_c2s_w", [M, H]), k.sb("moe_c2s_b", [P, 2])
        self.dec_w, self.dec_b = k.sb("moe_dec_w", [P, 2, D]), k.sb("moe_dec_b", [1, D])
        self.ln_g, self.ln_b = k.sb("moe_ln_g", [P, D]), k.sb("moe_ln_b", [P, D])
        s = k.sem
        self.loaded = s("moe_loaded")
        self.product = s("moe_product")
        self.by_v, self.by_a = s("moe_vector"), s("moe_scalar")
        self.ones_set = s("moe_ones_set")
        self.P_ENC, self.P_CONT, self.P_R1, self.P_R2 = 0, 4, 6, 8
        self.P_E1 = self.P_R2 + 1
        self.P_E2 = self.P_E1 + 16
        self.P_OFT = self.P_E2 + TILES
        self.P_C2S = self.P_OFT + 2
        self.P_DEC = self.P_C2S + 4

    def place(self):
        k, NE, M = self.k, self.NE, self.M
        self.ones = k.lb("moe_ones", [1, P])
        self.encT = k.lb("moe_encT", [P, 2, B * L])
        self.contT = k.lb("moe_contT", [M, B * L])
        self.tanhT = k.lb("moe_tanhT", [64, B * L])
        self.p = k.lb("moe_p", [P, TILES, NE])
        self.row = k.lb("moe_row", [P, TILES])
        self.top = k.lb("moe_top", [P, TILES, 8])
        self.at = k.lb("moe_top_at", [P, TILES, 8], U32)
        self.atf = k.lb("moe_top_at_float", [P, TILES, 2])
        self.w = k.lb("moe_w", [P, TILES, 2])
        self.gates = k.lb("moe_gates", [P, 2, TILES, NE])
        self.hT = k.lb("moe_hT", [P, NE, B * L])
        self.gated = k.lb("moe_gated", [P, 2, NE, M])
        self.of = k.lb("moe_of", [P, TILES, M])
        self.ofT = k.lb("moe_ofT", [M, B * L])
        self.spT = k.lb("moe_spT", [P, 2, B * L])

    def load(self, q, enc_W, enc_b, s2c_W, s2c_b, rW1, rb1, rW2, rb2, We1, be1, We2, be2, c2s_W, c2s_b, dec_W, dec_b, ln_g, ln_b):
        halves = lambda b: b.rearrange("(c p) -> p c", p=P)
        pairs = [(self.enc_w[:, :], enc_W), (self.enc_b[:, :], halves(enc_b)), (self.s2c_w[:, :, :], s2c_W.rearrange("(c p) m -> p c m", p=P)),
                 (self.s2c_b[:, :], s2c_b.unsqueeze(1)), (self.r1_w[:, :], rW1), (self.r1_b[:, :], rb1.unsqueeze(1)), (self.r2_w[:, :], rW2),
                 (self.r2_b[:, :], rb2.unsqueeze(0).to_broadcast((P, self.NE))), (self.e1_w[:, :, :], We1.rearrange("e m h -> m e h")),
                 (self.e1_b[:, :], be1.rearrange("e h -> h e")), (self.e2_w[:, :, :], We2.rearrange("e h m -> h e m")),
                 (self.e2_b[:, :], be2.rearrange("(o e) m -> o (e m)", o=1)), (self.c2s_w[:, :], c2s_W), (self.c2s_b[:, :], halves(c2s_b)),
                 (self.dec_w[:, :, :], dec_W.rearrange("(c p) d -> p c d", p=P)), (self.dec_b[:, :], dec_b.unsqueeze(0)),
                 (self.ln_g[:, :], ln_g.unsqueeze(0).to_broadcast((P, D))), (self.ln_b[:, :], ln_b.unsqueeze(0).to_broadcast((P, D)))]
        for dst, src in pairs:
            q.dma_start(dst, src).then_inc(self.loaded, 16)
        self.n_loads = 16 * len(pairs)

    def pool_ones(self, pool):
        pool.memset(self.ones[:, :], 1.0).then_inc(self.ones_set, 1)

    def tensor(self, pe):
        PS, k, NE, M = self.k.PS, self.k, self.NE, self.M
        pe.wait_ge(self.loaded, self.n_loads)
        for f in range(2):
            pe.wait_ge(k.ln.s_yT, 2 * self.norm + f + 1)
            for c in range(2):
                pe.matmul(PS[:, 2 * f + c, :], self.enc_w[:, c * P:c * P + P], k.yT[:, f * BANK:f * BANK + BANK],
                          start=True, stop=True).then_inc(self.product, 1)
        for f in range(2):
            pe.wait_ge(self.by_a, 2 * f + 2)
            for c in range(2):
                mm = pe.matmul(PS[0:M, 4 + f, :], self.s2c_w[:, c, :], self.encT[:, c, f * BANK:f * BANK + BANK], start=(c == 0), stop=(c == 1))
            mm.then_inc(self.product, 1)
        for f in range(2):
            pe.wait_ge(self.by_v, f + 1)
            pe.matmul(PS[0:64, 6 + f, :], self.r1_w[:, :], self.contT[:, f * BANK:f * BANK + BANK], start=True, stop=True).then_inc(self.product, 1)
        pe.wait_ge(self.by_a, 6)
        for t in range(TILES):
            mm = pe.matmul(PS[:, 0, t * NE:t * NE + NE], self.tanhT[:, t * P:t * P + P], self.r2_w[:, :], start=True, stop=True)
        mm.then_inc(self.product, 1)
        for i in range(16):
            e, f = i // 2, i % 2
            if i >= 4:
                if f:
                    pe.wait_ge(self.by_v, self.V_E1 + (i - 4) // 2 + 1)
                else:
                    pe.wait_ge(self.by_a, 7 + (i - 4) // 2 + 1)
            pe.matmul(PS[:, 1 + i % 4, :], self.e1_w[:, e, :], self.contT[:, f * BANK:f * BANK + BANK], start=True, stop=True).then_inc(self.product, 1)
        pe.wait_ge(self.by_a, 7 + 8)
        pe.wait_ge(self.by_v, self.V_E1 + 8)
        pe.wait_ge(self.ones_set, 1)
        for t in range(TILES):
            if t >= 2:
                pe.wait_ge(self.by_v, self.V_E2 + 2 * (t - 2) + 1)
            bank = PS[:, 5 + t % 2, :]
            pe.matmul(bank, self.ones[:, :], self.e2_b[:, :], start=True, stop=False)
            for e in range(NE):
                mm = pe.matmul(bank[:, e * M:e * M + M], self.hT[:, e, t * P:t * P + P], self.e2_w[:, e, :], start=False, stop=(e == NE - 1))
            mm.then_inc(self.product, 1)
        for f in range(2):
            pe.wait_ge(self.by_v, self.V_E2 + 2 * (4 * f + 4))
            for t in range(4 * f, 4 * f + 4):
                mm = pe.transpose(PS[0:M, 1 + f, (t % 4) * P:(t % 4) * P + P], self.of[:, t, :], k.ident)
            mm.then_inc(self.product, 1)
        for f in range(2):
            pe.wait_ge(self.by_v, self.V_OFT + f + 1)
            for c in range(2):
                pe.matmul(PS[:, (3, 4, 5, 6)[2 * f + c], :], self.c2s_w[:, c * P:c * P + P], self.ofT[:, f * BANK:f * BANK + BANK],
                          start=True, stop=True).then_inc(self.product, 1)
        for f in range(2):
            pe.wait_ge(self.by_a, 15 + 2 * f + 2)
            for t in range(4 * f, 4 * f + 4):
                out = PS[:, (7, 0)[f], (t % 4) * P:(t % 4) * P + P]
                pe.matmul(out, self.ones[:, :], self.dec_b[:, :], start=True, stop=False)
                for c in range(2):
                    mm = pe.matmul(out, self.spT[:, c, t * P:t * P + P], self.dec_w[:, c, :], start=False, stop=(c == 1))
            mm.then_inc(self.product, 1)

    V_E1 = 2 + 15 + 2 * TILES
    V_E2 = V_E1 + 8
    V_OFT = V_E2 + 2 * TILES

    def scalar(self, act):
        PS, k = self.k.PS, self.k
        halves = lambda f: slice(f * BANK, f * BANK + BANK)
        act.wait_ge(self.loaded, self.n_loads)
        for f in range(2):
            for c in range(2):
                act.wait_ge(self.product, 2 * f + c + 1)
                act.activation(self.encT[:, c, halves(f)], PS[:, 2 * f + c, :], ACT.Sigmoid, bias=self.enc_b[:, c:c + 1]).then_inc(self.by_a, 1)
        for f in range(2):
            act.wait_ge(self.product, self.P_R1 + f + 1)
            act.activation(self.tanhT[:, halves(f)], PS[0:64, 6 + f, :], ACT.Tanh, bias=self.r1_b[:, 0:1]).then_inc(self.by_a, 1)
        act.wait_ge(self.by_v, 5)
        act.activation(self.p[:, :, :], self.p[:, :, :], ACT.Exp).then_inc(self.by_a, 1)
        for i in range(0, 16, 2):
            act.wait_ge(self.product, self.P_E1 + i + 1)
            act.activation(self.hT[:, i // 2, halves(0)], PS[:, 1 + i % 4, :], ACT.Relu, bias=self.e1_b[:, i // 2:i // 2 + 1]).then_inc(self.by_a, 1)
        for f in range(2):
            for c in range(2):
                act.wait_ge(self.product, self.P_C2S + 2 * f + c + 1)
                act.activation(self.spT[:, c, halves(f)], PS[:, (3, 4, 5, 6)[2 * f + c], :], ACT.Sigmoid, bias=self.c2s_b[:, c:c + 1]).then_inc(self.by_a, 1)
        for f in range(2):
            act.wait_ge(self.product, self.P_DEC + f + 1)
            act.activation(k.y[:, 4 * f:4 * f + 4, :], PS[:, (7, 0)[f], :].rearrange("p (t d) -> p t d", t=4), ACT.Sigmoid).then_inc(self.by_a, 1)

    def vector(self, v):
        PS, NE, M = self.k.PS, self.NE, self.M
        n = 0

        def done(ins):
            nonlocal n
            ins.then_inc(self.by_v, 1)
            n += 1

        def own():
            v.wait_ge(self.by_v, n)

        v.wait_ge(self.loaded, self.n_loads)
        for f in range(2):
            v.wait_ge(self.product, self.P_CONT + f + 1)
            done(v.tensor_scalar(self.contT[:, f * BANK:f * BANK + BANK], PS[0:M, 4 + f, :], self.s2c_b[:, 0:1], None, ALU.add))
        by_e = lambda a: a.unsqueeze(2).to_broadcast((P, TILES, NE))
        v.wait_ge(self.product, self.P_R2 + 1)
        done(v.tensor_tensor(self.p[:, :, :], PS[:, 0, 0:TILES * NE].rearrange("p (t e) -> p t e", e=NE),
                             self.r2_b[:, :].unsqueeze(1).to_broadcast((P, TILES, NE)), ALU.add))
        own()
        done(v.tensor_reduce(self.row[:, :], self.p[:, :, :], AX.X, ALU.max, negate=True))
        own()
        done(v.tensor_tensor(self.p[:, :, :], self.p[:, :, :], by_e(self.row[:, :]), ALU.add))
        v.wait_ge(self.by_a, 7)
        done(v.tensor_reduce(self.row[:, :], self.p[:, :, :], AX.X, ALU.add))
        own()
        done(v.reciprocal(self.row[:, :], self.row[:, :]))
        own()
        done(v.tensor_tensor(self.p[:, :, :], self.p[:, :, :], by_e(self.row[:, :]), ALU.mult))
        own()
        for t in range(TILES):
            done(v.max(self.top[:, t, :], self.p[:, t, :]))
        own()
        for t in range(TILES):
            done(v.max_index(self.at[:, t, :], self.top[:, t, :], self.p[:, t, :]))
        own()
        done(v.tensor_copy(self.atf[:, :, :], self.at[:, :, 0:2]))
        done(v.tensor_tensor(self.row[:, :], self.top[:, :, 0], self.top[:, :, 1], ALU.add))
        own()
        done(v.reciprocal(self.row[:, :], self.row[:, :]))
        own()
        done(v.tensor_tensor(self.w[:, :, :], self.top[:, :, 0:2], self.row[:, :].unsqueeze(2).to_broadcast((P, TILES, 2)), ALU.mult))
        own()
        for i in range(2):
            done(v.tensor_tensor(self.gates[:, i, :, :], self.k.cst[:, C_IOTA:C_IOTA + NE].unsqueeze(1).to_broadcast((P, TILES, NE)),
                                 by_e(self.atf[:, :, i]), ALU.is_equal))
        own()
        for i in range(2):
            done(v.tensor_tensor(self.gates[:, i, :, :], self.gates[:, i, :, :], by_e(self.w[:, :, i]), ALU.mult))
        own()
        done(v.tensor_tensor(self.gates[:, 0, :, :], self.gates[:, 0, :, :], self.gates[:, 1, :, :], ALU.add))
        own()
        assert n == self.V_E1
        for i in range(1, 16, 2):
            v.wait_ge(self.product, self.P_E1 + i + 1)
            done(v.tensor_scalar(self.hT[:, i // 2, BANK:2 * BANK], PS[:, 1 + i % 4, :], self.e1_b[:, i // 2:i // 2 + 1], 0.0, ALU.add, ALU.max))
        assert n == self.V_E2
        for t in range(TILES):
            v.wait_ge(self.product, self.P_E2 + t + 1)
            done(v.tensor_tensor(self.gated[:, t % 2, :, :], PS[:, 5 + t % 2, :].rearrange("p (e m) -> p e m", e=NE),
                                 self.gates[:, 0, t, :].unsqueeze(2).to_broadcast((P, NE, M)), ALU.mult))
            own()
            done(v.tensor_reduce(self.of[:, t, :], self.gated[:, t % 2, :, :].rearrange("p e m -> p m e"), AX.X, ALU.add))
        for f in range(2):
            v.wait_ge(self.product, self.P_OFT + f + 1)
            done(v.tensor_copy(self.ofT[:, f * BANK:f * BANK + BANK], PS[0:M, 1 + f, :]))

    def vector_add(self, v):
        k = self.k
        tiles = lambda a: a[:, :].unsqueeze(1).to_broadcast((P, TILES, D))
        first = self.V_OFT + 2
        v.wait_ge(k.ln.s_y, TILES * (self.norm + 2))
        v.tensor_tensor(k.y[:, :, :], k.y[:, :, :], tiles(self.ln_g), ALU.mult).then_inc(self.by_v, 1)
        v.wait_ge(self.by_v, first + 1)
        v.tensor_tensor(k.y[:, :, :], k.y[:, :, :], tiles(self.ln_b), ALU.add).then_inc(self.by_v, 1)
        v.wait_ge(self.by_v, first + 2)
        v.tensor_tensor(k.x[:, :, :], k.x[:, :, :], k.y[:, :, :], ALU.add)

class TopOneMoE:

    NE = 8

    def __init__(self, k, norm):
        self.yT_in = 2 * (norm + 1)
        self.k = k
        NE = self.NE
        self.wg, self.bg = k.sb("top_wg", [P, NE]), k.sb("top_bg", [P, NE])
        self.w1, self.b1 = k.sb("top_w1", [P, NE, P]), k.sb("top_b1", [P, NE])
        self.w2, self.b2 = k.sb("top_w2", [P, NE, D]), k.sb("top_b2", [NE, D])
        s = k.sem
        self.loaded = s("top_loaded")
        self.product = s("top_product")
        self.by_v, self.by_a = s("top_vector"), s("top_scalar")

    def place(self):
        k, NE = self.k, self.NE
        self.p = k.lb("top_p", [P, TILES, NE])
        self.row = k.lb("top_row", [P, TILES])
        self.top = k.lb("top_top", [P, TILES, 8])
        self.at = k.lb("top_at", [P, TILES, 8], U32)
        self.atf = k.lb("top_at_float", [P, TILES])
        self.oh = k.lb("top_one_hot", [P, TILES, NE])
        self.ohT = k.lb("top_one_hotT", [NE, B * L])
        self.ohb = k.lb("top_one_hot_bf16", [NE, B * L], BF16)
        self.h = k.lb("top_h", [P, 4, BANK])
        self.hm = k.lb("top_h_gated", [P, NE, B * L])

    def load(self, q, Wg, bg, W1, b1, W2, b2):
        pairs = [(self.wg[:, :], Wg), (self.bg[:, :], bg.unsqueeze(0).to_broadcast((P, self.NE))), (self.w1[:, :, :], W1.rearrange("e h i -> h e i")),
                 (self.b1[:, :], b1.rearrange("e i -> i e")), (self.w2[:, :, :], W2.rearrange("e i h -> i e h")), (self.b2[:, :], b2)]
        for dst, src in pairs:
            q.dma_start(dst, src).then_inc(self.loaded, 16)
        self.n_loads = 16 * len(pairs)

    V_OH = 6 + 2 * TILES + 2
    P_OH = 2

    def tensor(self, pe):
        PS, k, NE = self.k.PS, self.k, self.NE
        pe.wait_ge(self.loaded, self.n_loads)
        pe.wait_ge(k.ln.s_yT, self.yT_in)
        for t in range(TILES):
            mm = pe.matmul(PS[:, 0, t * NE:t * NE + NE], k.yT[:, t * P:t * P + P], self.wg[:, :], start=True, stop=True)
        mm.then_inc(self.product, 1)
        pe.wait_ge(self.by_v, self.V_OH)
        for t in range(TILES):
            mm = pe.transpose(PS[0:NE, 1 + t // 4, (t % 4) * P:(t % 4) * P + P], self.oh[:, t, :], k.ident)
        mm.then_inc(self.product, 1)
        pe.wait_ge(self.by_v, self.V_OH + 2)
        for i in range(16):
            e, f = i // 2, i % 2
            if i >= 2:
                pe.wait_ge(self.by_a, i)
                pe.wait_ge(self.by_v, self.V_OH + 2 + i - 1)
            r = slice(f * BANK, f * BANK + BANK)
            pe.matmul(PS[:, (0, 3)[f], :], self.w1[:, e, :], k.yT[:, r], start=True, stop=True)
            pe.matmul(PS[:, (1, 2)[f], :], k.identb[0:NE, e:e + 1].to_broadcast((NE, P)), self.ohb[:, r], start=True, stop=True).then_inc(self.product, 1)
        for t in range(TILES):
            pe.wait_ge(self.by_v, self.V_OH + 2 + 16)
            out = PS[:, 4 + t // 4, (t % 4) * P:(t % 4) * P + P]
            pe.matmul(out, self.ohT[:, t * P:t * P + P], self.b2[:, :], start=True, stop=False)
            for e in range(NE):
                mm = pe.matmul(out, self.hm[:, e, t * P:t * P + P], self.w2[:, e, :], start=False, stop=(e == NE - 1))
            if t % 4 == 3:
                mm.then_inc(self.product, 1)

    def scalar(self, act):
        PS = self.k.PS
        act.wait_ge(self.loaded, self.n_loads)
        act.wait_ge(self.by_v, 3)
        act.activation(self.p[:, :, :], self.p[:, :, :], ACT.Exp).then_inc(self.by_a, 1)
        for i in range(16):
            act.wait_ge(self.product, 2 + i + 1)
            if i >= 4:
                act.wait_ge(self.by_v, self.V_OH + 2 + i - 3)
            act.activation(self.h[:, i % 4, :], PS[:, (0, 3)[i % 2], :], ACT.Gelu, bias=self.b1[:, i // 2:i // 2 + 1]).then_inc(self.by_a, 1)

    def vector(self, v):
        PS, NE = self.k.PS, self.NE
        n = 0

        def done(ins):
            nonlocal n
            ins.then_inc(self.by_v, 1)
            n += 1

        def own():
            v.wait_ge(self.by_v, n)

        by_e = lambda a: a.unsqueeze(2).to_broadcast((P, TILES, NE))
        v.wait_ge(self.loaded, self.n_loads)
        v.wait_ge(self.product, 1)
        done(v.tensor_tensor(self.p[:, :, :], PS[:, 0, 0:TILES * NE].rearrange("p (t e) -> p t e", e=NE),
                             self.bg[:, :].unsqueeze(1).to_broadcast((P, TILES, NE)), ALU.add))
        own()
        done(v.tensor_reduce(self.row[:, :], self.p[:, :, :], AX.X, ALU.max, negate=True))
        own()
        done(v.tensor_tensor(self.p[:, :, :], self.p[:, :, :], by_e(self.row[:, :]), ALU.add))
        v.wait_ge(self.by_a, 1)
        done(v.tensor_reduce(self.row[:, :], self.p[:, :, :], AX.X, ALU.add))
        own()
        done(v.reciprocal(self.row[:, :], self.row[:, :]))
        own()
        done(v.tensor_tensor(self.p[:, :, :], self.p[:, :, :], by_e(self.row[:, :]), ALU.mult))
        own()
        for t in range(TILES):
            done(v.max(self.top[:, t, :], self.p[:, t, :]))
        own()
        for t in range(TILES):
            done(v.max_index(self.at[:, t, :], self.top[:, t, :], self.p[:, t, :]))
        own()
        done(v.tensor_copy(self.atf[:, :], self.at[:, :, 0]))
        own()
        done(v.tensor_tensor(self.oh[:, :, :], self.k.cst[:, C_IOTA:C_IOTA + NE].unsqueeze(1).to_broadcast((P, TILES, NE)), by_e(self.atf[:, :]),
                             ALU.is_equal))
        assert n == self.V_OH
        v.wait_ge(self.product, 2)
        for dst in (self.ohT, self.ohb):
            done(v.tensor_copy(dst[:, :].rearrange("p (f c) -> p f c", f=2), PS[0:NE, 1:3, :]))
        for i in range(16):
            e, f = i // 2, i % 2
            v.wait_ge(self.by_a, 1 + i + 1)
            done(v.tensor_tensor(self.hm[:, e, f * BANK:f * BANK + BANK], self.h[:, i % 4, :], PS[:, (1, 2)[f], :], ALU.mult))
        x = self.k.x
        for f in range(2):
            v.wait_ge(self.product, 2 + 16 + f + 1)
            r = slice(4 * f, 4 * f + 4)
            v.tensor_tensor(x[:, r, :], x[:, r, :], PS[:, 4 + f, :].rearrange("p (t d) -> p t d", t=4), ALU.add)

def build(nc, a, cst_d, out):
    with ExitStack() as stack:
        k = Kit(nc, stack)
        k.PS = stack.enter_context(nc.psum_tensor("PS", [P, 8, BANK], F32))
        k.cst = k.sb("constants", [P, C_END])
        k.ident = k.cst[:, C_ID:C_ID + P]
        k.x = k.sb("x", [P, TILES, D])
        k.y = k.sb("y", [P, TILES, D])
        k.yT = k.sb("yT", [P, B * L])
        k.ctxT = k.sb("ctxT", [P, B, S2])
        k.ctxP = k.sb("ctx_by_lane", [P, S2 // 32, D])
        k.identb = k.sb("ident_bf16", [P, P], BF16)
        k.trib = k.sb("triangle_bf16", [P, P], BF16)
        k.classb = k.sb("classes_bf16", [2, P + REG], BF16)
        k.ln = LayerNorm(k)
        warm = k.sb("warm", [P, 1])
        x_in, cst_in, ctx_in, ctxP_in = k.sem("x_in"), k.sem("constants_in"), k.sem("ctx_in"), k.sem("ctx_by_lane_in")
        ctx_turned, ctx_sb, cast_done, out_done = k.sem("ctx_turned"), k.sem("ctxT_ready"), k.sem("bf16_constants_ready"), k.sem("out_done")
        l1f = NarrowAttention(k, "l1f", 3, by_class=True)
        l2f = SpikingMoE(k, 5)
        l3x = NarrowAttention(k, "l3x", 6, by_class=False)
        l3f = TopOneMoE(k, 7)
        with ExitStack() as k.local:
            l0x = WideAttention(k, "l0x", 0, causal=True, wo_by_head=False)
            l1x = WideAttention(k, "l1x", 2, causal=False, wo_by_head=True)
            group = k.local
            with ExitStack() as k.local:
                ctx_nat = k.lb("ctx_natural", [P, B * S2 // P, D])
                l0f = ShiftMix(k, 1)
            k.local = group
            l1f.place()
        with ExitStack() as k.local:
            l2x = Warping(k, 4)
        with ExitStack() as k.local:
            l3x.place()
            group = k.local
            with ExitStack() as k.local:
                l2f.place()
            k.local = group
            l3f.place()
        stack.enter_context(nc.allow_non_contiguous_dma(reason="biases of at most 1024 elements, one to a partition"))
        block = stack.enter_context(nc.Block())

        @block.sync
        def _(sp):
            sp.dma_start(k.x[:, :, :], a["x"].rearrange("b (t p) d -> p (b t) d", p=P)).then_inc(x_in, 16)
            sp.dma_start(k.cst[:, :], cst_d).then_inc(cst_in, 16)
            ctx = a["ctx_1024"]
            sp.dma_start(ctx_nat[:, :, :], ctx.rearrange("b (t p) d -> p (b t) d", p=P)).then_inc(ctx_in, 16)
            wq, wk, bq, bk = (a["L0_xattn_" + n] for n in ("Wq", "Wk", "bq", "bk"))
            l0x.load_once(sp, a["L0_xattn_Wv"], a["L0_xattn_bv"], a["L0_xattn_bo"], a["L0_xattn_Wo"], wq, wk, bq, bk)
            l0f.load(sp, *(a["L0_ffn_" + n] for n in ("W_r", "W_k", "W_v", "mu_r", "mu_k")))
            wide = lambda n: a["L1_xattn_" + n].rearrange("d n h -> d (n h)")
            bias = lambda n: a["L1_xattn_" + n].rearrange("n o h -> (n o h)")
            wq1, wk1, bq1, bk1 = wide("w_query"), wide("w_key"), bias("b_query"), bias("b_key")
            l1x.load_once(sp, wide("w_value"), bias("b_value"), a["L1_xattn_b_projection"].rearrange("o d -> (o d)"), a["L1_xattn_w_projection"],
                          wq1, wk1, bq1, bk1)
            l0x.load_rounds(sp, wq, wk, bq, bk)
            for b in range(B):
                sp.dma_start(k.ctxP[32 * b:32 * b + 32, :, :], ctx[b].rearrange("(p e) d -> e p d", e=32)).then_inc(ctxP_in, 16)
            qkv = a["L1_ffn_W_qkv"]
            l1f.load(sp, qkv[:, 0:D], qkv[:, D:2 * D], qkv[:, 2 * D:3 * D], a["L1_ffn_W_proj"], a["L1_ffn_b_proj"], g=a["L1_ffn_g_info"][0, 0])
            l3x.load(sp, *(a["L3_xattn_" + n] for n in ("Wq", "Wk", "Wv", "Wo", "bo", "bq", "bk", "bv")), mask=a["mask_BxS2_bf0"])
            l2f.load(sp, *(a["L2_ffn_" + n] for n in ("enc_W", "enc_b", "s2c_W", "s2c_b", "rW1", "rb1", "rW2", "rb2", "We1", "be1", "We2", "be2",
                                                     "c2s_W", "c2s_b", "dec_W", "dec_b", "ln_g", "ln_b")))
            l3f.load(sp, *(a["L3_ffn_" + n] for n in ("Wg", "bg", "W1", "b1", "W2", "b2")))
            l1x.load_rounds(sp, wq1, wk1, bq1, bk1)
            sp.wait_ge(k.stage_done, 4 * 12)
            sp.dma_start(out.rearrange("b (t p) d -> p (b t) d", p=P), k.x[:, :, :]).then_inc(out_done, 16)
            sp.wait_ge(out_done, 16)

        @block.gpsimd
        def _(pool):
            ln = k.ln
            pool.memset(ln.half[:, :], -0.5).then_inc(ln.s_half, 1)
            l1f.pool_zero(pool)
            l3x.pool_zero(pool)
            pool.wait_ge(cst_in, 16)
            pool.tensor_copy(k.identb[:, :], k.ident).then_inc(cast_done, 1)
            pool.tensor_copy(k.trib[:, :], k.cst[:, C_TRI:C_TRI + P]).then_inc(cast_done, 1)
            pool.tensor_copy(k.classb[:, :], k.cst[0:2, C_CLASS:C_CLASS + P + REG]).then_inc(cast_done, 1)
            pool.wait_ge(ln.s_half, 1)
            ln.pool_rstd(pool, 0)
            k.meet(pool, 0)
            ln.pool_rstd(pool, 1)
            k.meet(pool, 1)
            ln.pool_rstd(pool, 2)
            l1f.pool_pad(pool)
            k.meet(pool, 2)
            ln.pool_rstd(pool, 3)
            l1f.pool_find(pool)
            l1f.pool_batches(pool)
            k.meet(pool, 3)
            ln.pool_rstd(pool, 4)
            l2x.pool_before(pool)
            k.meet(pool, 4)
            l2x.pool_forward(pool)
            k.meet(pool, 5)
            k.meet(pool, 6)
            k.meet(pool, 7)
            ln.pool_rstd(pool, 5)
            l2f.pool_ones(pool)
            l3x.pool_pad(pool)
            ln.pool_rstd(pool, 6)
            k.meet(pool, 8)
            ln.pool_rstd(pool, 7)
            l3x.pool_batches(pool)
            k.meet(pool, 9)
            ln.pool_rstd(pool, 8)
            k.meet(pool, 10)
            k.meet(pool, 11)

        @block.tensor
        def _(pe):
            ln = k.ln
            pe.wait_ge(cst_in, 16)
            pe.wait_ge(ctx_in, 16)
            for t in range(B * S2 // P):
                mm = pe.transpose(k.PS[:, t // 4, (t % 4) * P:(t % 4) * P + P], ctx_nat[:, t, :], k.ident)
                if t % 4 == 3:
                    mm.then_inc(ctx_turned, 1)
            ln.tensor_transpose(pe, 0, 0)
            pe.wait_ge(cast_done, 3)
            pe.wait_ge(ctx_sb, B)
            l0x.tensor(pe)
            k.meet(pe, 0)
            ln.tensor_transpose(pe, 1, 1)
            l0f.tensor(pe)
            k.meet(pe, 1)
            ln.tensor_transpose(pe, 2, 2)
            l1x.tensor(pe)
            k.meet(pe, 2)
            ln.tensor_transpose(pe, 3, 3)
            l1f.tensor_find(pe)
            l1f.tensor(pe)
            k.meet(pe, 3)
            ln.tensor_transpose(pe, 4, 4)
            l2x.tensor_distances(pe)
            k.meet(pe, 4)
            k.meet(pe, 5)
            k.meet(pe, 6)
            pe.wait_ge(ctxP_in, 64)
            l2x.tensor_expand(pe)
            k.meet(pe, 7)
            ln.tensor_transpose(pe, 5, 5)
            l2f.tensor(pe)
            k.meet(pe, 8)
            ln.tensor_transpose(pe, 7, 6)
            l3x.tensor(pe)
            k.meet(pe, 9)
            ln.tensor_transpose(pe, 8, 7)
            l3f.tensor(pe)
            k.meet(pe, 10)
            k.meet(pe, 11)

        @block.scalar
        def _(act):
            ln = k.ln
            prime = ln.half[:, 0:1]
            act.wait_ge(ln.s_half, 1)
            for b in range(B):
                act.wait_ge(ctx_turned, b + 1)
                act.copy(k.ctxT[:, b, :], k.PS[:, b, :]).then_inc(ctx_sb, 1)
            ln.scalar_yT(act, 0)
            act.activation(warm[:, :], prime, ACT.Exp)
            l0x.scalar(act)
            k.meet(act, 0)
            ln.scalar_yT(act, 1)
            l0f.scalar(act)
            k.meet(act, 1)
            ln.scalar_yT(act, 2)
            act.activation(warm[:, :], prime, ACT.Exp)
            l1x.scalar(act)
            k.meet(act, 2)
            ln.scalar_yT(act, 3)
            act.activation(warm[:, :], prime, ACT.Exp)
            l1f.scalar(act)
            k.meet(act, 3)
            ln.scalar_yT(act, 4)
            l2x.scalar_distances(act)
            k.meet(act, 4)
            l2x.scalar_forward(act)
            k.meet(act, 5)
            l2x.scalar_backward(act)
            k.meet(act, 6)
            l2x.scalar_expand(act)
            k.meet(act, 7)
            ln.scalar_yT(act, 5)
            l2f.scalar(act)
            k.meet(act, 8)
            ln.scalar_yT(act, 6)
            act.activation(warm[:, :], prime, ACT.Exp)
            l3x.scalar(act)
            k.meet(act, 9)
            ln.scalar_yT(act, 7)
            l3f.scalar(act)
            k.meet(act, 10)
            k.meet(act, 11)

        @block.vector
        def _(v):
            ln, x, y = k.ln, k.x, k.y
            v.wait_ge(x_in, 16)

            def norm(n, src=x):
                ln.vector_stats(v, n, src)
                ln.vector_norm(v, n, src, y)
                v.wait_ge(ln.s_y, TILES * (n + 1))

            norm(0)
            l0x.vector(v)
            k.meet(v, 0)
            norm(1)
            l0f.vector(v)
            k.meet(v, 1)
            norm(2)
            l1x.vector(v)
            k.meet(v, 2)
            norm(3)
            v.wait_ge(cst_in, 16)
            l1f.vector_find(v)
            l1f.vector(v)
            k.meet(v, 3)
            norm(4)
            v.wait_ge(ctxP_in, 64)
            l2x.vector_distances(v)
            k.meet(v, 4)
            l2x.vector_forward(v)
            k.meet(v, 5)
            l2x.vector_backward(v)
            k.meet(v, 6)
            l2x.vector_expand(v)
            k.meet(v, 7)
            norm(5)
            l2f.vector(v)
            v.wait_ge(l2f.by_a, 21)
            norm(6, y)
            l2f.vector_add(v)
            k.meet(v, 8)
            norm(7)
            l3x.vector_padding(v)
            l3x.vector(v)
            k.meet(v, 9)
            norm(8)
            l3f.vector(v)
            k.meet(v, 10)
            k.meet(v, 11)



def constants():
    import numpy as np
    c = np.zeros((P, C_END), dtype=np.float32)
    p = np.arange(P)
    c[:, C_ID:C_ID + P] = np.eye(P)
    c[:, C_TRI:C_TRI + P] = np.where(p[None, :] <= p[:, None], 0.0, -BIG)
    c[:, C_HALO] = np.where(p % 32 == 0, 0.0, BIG)
    c[:, C_START] = p % 32 == S2 // 32 - 1
    for t in range(0, TILES, QT):
        c[0:REG, C_REG + t] = 1.0
    c[:, C_IOTA:C_IOTA + 8] = np.arange(8)
    for row in range(2):
        c[row, C_CLASS + D8 + row:C_CLASS + P:32] = 1.0
    c[1, C_NEG:C_NEG + REG] = 1.0
    for h in range(HEADS8):
        own = (p // 32 == h % 4) & (p % 32 < D8 + 2)
        c[own, C_OWN + (h // 4) * HEADS8 + h] = SCALE8
        for i in range(REG):
            c[h * REG + i, C_DIAG + 32 * h:C_DIAG + 32 * h + D8] = 1.0
            c[h * REG + i, C_SUM + i] = 0.5
    c[0:2, C_ONE:C_ONE + P] = 1.0
    return c


def kernel(**inputs):
    import numpy as np
    import concourse.bacc as bacc
    from concourse.bass_utils import run_bass_kernel_spmd

    nc = bacc.Bacc("TRN2", target_bir_lowering=False, num_devices=1)
    arrays, args = {}, {}
    for name, value in inputs.items():
        a = np.ascontiguousarray(value)
        if a.dtype == np.bool_:
            a = a.view(np.uint32)
        arrays[name + "_dram"] = a
        args[name] = nc.dram_tensor(name + "_dram", a.shape, mybir.dt.from_np(a.dtype), kind="ExternalInput").ap()
    arrays["constants_dram"] = constants()
    cst = nc.dram_tensor("constants_dram", arrays["constants_dram"].shape, F32, kind="ExternalInput").ap()
    out = nc.dram_tensor("out_dram", (B, L, D), F32, kind="ExternalOutput").ap()
    build(nc, args, cst, out)
    r = run_bass_kernel_spmd(nc, [arrays], core_ids=[0])
    return r.results[0]["out_dram"]
```

```python
from contextlib import ExitStack

import concourse.bass as bass
from concourse import mybir

F32 = mybir.dt.float32
BF16 = mybir.dt.bfloat16
U8 = mybir.dt.uint8
U32 = mybir.dt.uint32
ALU = mybir.AluOpType
ACT = mybir.ActivationFunctionType
AX = mybir.AxisListType
ds = bass.ds

P = 128
D = 128
B, L, S2 = 4, 256, 512
TILES = B * L // P
QT = L // P
BIG = 1e30
HALFBANK, BANK = 256, 512
EPS = 1e-5

C_ID = 0
C_TRI = 128
C_HALO = 256
C_START = 257
C_REG = 258
C_IOTA = 266
C_CLASS = 274
C_NEG = 402
C_OWN = 407
C_DIAG = 471
C_SUM = 983
C_ONE = 988
C_END = 1116
REG = 5
HEADS8, D8 = 16, 8
SCALE8 = float(D8) ** -0.5


class Kit:

    def __init__(self, nc, stack):
        self.nc, self.stack = nc, stack
        self.local = None
        self.stage_done = self.sem("stage_done")

    def sb(self, name, shape, dt=F32):
        return self.stack.enter_context(self.nc.sbuf_tensor(name, shape, dt))

    def lb(self, name, shape, dt=F32):
        return self.local.enter_context(self.nc.sbuf_tensor(name, shape, dt))

    def sem(self, name):
        return self.stack.enter_context(self.nc.semaphore(name))

    def meet(self, eng, stage):
        eng.drain().then_inc(self.stage_done, 1)
        eng.wait_ge(self.stage_done, 4 * (stage + 1))

class LayerNorm:

    TPS = (6, 7)

    def __init__(self, k):
        self.k = k
        self.stats = k.sb("ln_stats", [P, TILES, 6])
        self.mv = k.sb("ln_mv", [P, TILES, 2])
        self.rstd = k.sb("ln_rstd", [P, TILES])
        self.half = k.sb("ln_minus_half", [P, P])
        self.s_half = k.sem("minus_half_set")
        self.s_stats = k.sem("ln_stats_done")
        self.s_mv = k.sem("ln_mean_var_done")
        self.s_var = k.sem("ln_var_eps_done")
        self.s_rstd = k.sem("ln_rstd_done")
        self.s_y = k.sem("ln_y_done")
        self.s_tps = k.sem("ln_transposed")
        self.s_yT = k.sem("ln_yT_done")

    def pool_rstd(self, pool, n):
        pool.wait_ge(self.s_mv, TILES * (n + 1))
        pool.tensor_scalar(self.rstd[:, :], self.mv[:, :, 1], EPS, None, ALU.add).then_inc(self.s_var, 1)
        pool.wait_ge(self.s_var, n + 1)
        pool.tensor_tensor(self.rstd[:, :], self.rstd[:, :], self.half[:, 0:TILES], ALU.pow).then_inc(self.s_rstd, 1)

    def vector_stats(self, v, n, src):
        for t in range(TILES):
            v.bn_stats(self.stats[:, t, :], src[:, t, :]).then_inc(self.s_stats, 1)
        for t in range(TILES):
            v.wait_ge(self.s_stats, TILES * n + t + 1)
            v.bn_aggr(self.mv[:, t, :], self.stats[:, t, :]).then_inc(self.s_mv, 1)

    def vector_norm(self, v, n, src, dst):
        v.wait_ge(self.s_rstd, n + 1)
        v.wait_ge(self.s_mv, TILES * (n + 1))
        for t in range(TILES):
            v.tensor_scalar(dst[:, t, :], src[:, t, :], self.mv[:, t, 0:1], self.rstd[:, t:t + 1],
                            ALU.subtract, ALU.mult).then_inc(self.s_y, 1)

    def tensor_transpose(self, pe, n, m):
        for t in range(TILES):
            pe.wait_ge(self.s_y, TILES * n + t + 1)
            mm = pe.transpose(self.k.PS[:, self.TPS[t // 4], (t % 4) * P:(t % 4) * P + P], self.k.y[:, t, :], self.k.ident)
            if t % 4 == 3:
                mm.then_inc(self.s_tps, 1)

    def scalar_yT(self, act, m):
        for h in range(2):
            act.wait_ge(self.s_tps, 2 * m + h + 1)
            act.copy(self.k.yT[:, h * BANK:h * BANK + BANK], self.k.PS[:, self.TPS[h], :]).then_inc(self.s_yT, 1)

class WideAttention:

    ROUNDS, UNITS, STEPS, HD = 8, B, 16, 64
    S, T, O, G = (0, 1), (2, 3), (4, 5), (6, 7)

    def __init__(self, k, name, norm, causal, wo_by_head):
        self.yT_in = 2 * (norm + 1)
        self.k, self.name, self.causal, self.wo_by_head = k, name, causal, wo_by_head
        n = name + "_"
        most = L if causal else S2
        self.wq = k.lb(n + "wq", [P, P])
        self.wk = k.lb(n + "wk", [P, P])
        self.bq = k.lb(n + "bq", [P, 1])
        self.bk = k.lb(n + "bk", [P, 1])
        self.wv = k.lb(n + "wv", [P, 8 * P])
        self.bv = k.lb(n + "bv", [P, 8 * P])
        self.wo = k.lb(n + "wo", [P, 8, P])
        self.wo_in = k.lb(n + "wo_in", [P, 8, P]) if wo_by_head else None
        self.bo = k.lb(n + "bo", [P, P])
        self.qT = k.lb(n + "qT", [P, 2, L])
        self.kT = k.lb(n + "kT", [P, 2, most])
        self.v = k.lb(n + "v", [P, 2, most // P, P])
        self.probs = k.lb(n + "probs", [P, 2, most])
        self.pT = k.lb(n + "pT", [P, 2, most])
        self.nmax = k.lb(n + "nmax", [P, 4])
        self.sums = k.lb(n + "sums", [P, 8])
        self.inv = k.lb(n + "inv", [P, 2, QT, P])
        self.inv_few = k.lb(n + "inv_few", [P, QT, 2])
        self.spread = k.lb(n + "inverse_spread", [P, 2, L])
        self.attT = k.lb(n + "attT", [P, 2, L])
        s = k.sem
        self.w_once = s(n + "weights_loaded")
        self.w_in = s(n + "round_weights_loaded")
        self.q_ps, self.k_ps, self.v_ps = s(n + "q_product"), s(n + "k_product"), s(n + "v_product")
        self.q_sb, self.k_sb, self.v_sb = s(n + "q_ready"), s(n + "k_ready"), s(n + "v_ready")
        self.sc, self.mx, self.ex, self.tr = s(n + "scores"), s(n + "max"), s(n + "probs"), s(n + "turned")
        self.pt_v, self.pt_a = s(n + "pT_even"), s(n + "pT_odd")
        self.av, self.iv_few, self.iv, self.nm = s(n + "pv"), s(n + "inverse"), s(n + "inverse_repeated"), s(n + "attT_normed")
        self.sp_ps, self.sp_sb = s(n + "inverse_spread_product"), s(n + "inverse_spread_ready")
        self.wo_ps, self.x_add = s(n + "out_product"), s(n + "x_added")
        self.first = [("q", 0), ("k", 0), ("v", 0)]
        self.order = []
        for b in range(B):
            self.order += [("q", b + 1), ("k", b + 1), ("v", b + 1)]
            if b >= 1:
                self.order += [("t", b - 1), ("o", b - 1)]
        self.order += [("t", B - 1), ("o", B - 1)]
        self.order_last = [u for u in self.order if u[1] < B]
        assert len(self.order) % 2 == 0

    def uses(self, last):
        return self.order_last if last else self.order

    def bank(self, u, last):
        if u in self.first:
            return self.G[self.first.index(u) % 2]
        return self.G[(len(self.first) + self.uses(last).index(u)) % 2]

    def keys(self, n):
        return P * (n % QT + 1) if self.causal else S2

    def where(self, n):
        return n // 4, (n % 4) // 2, n % 2

    def load_once(self, sp, wv, bv, bo, wo, wq, wk, bq, bk):
        sp.dma_start(self.wq[:, :], wq[:, 0:P]).then_inc(self.w_in, 16)
        sp.dma_start(self.wk[:, :], wk[:, 0:P]).then_inc(self.w_in, 16)
        sp.dma_start(self.bq[:, :], bq[0:P].unsqueeze(1)).then_inc(self.w_in, 16)
        sp.dma_start(self.bk[:, :], bk[0:P].unsqueeze(1)).then_inc(self.w_in, 16)
        sp.dma_start(self.wv[:, :], wv).then_inc(self.w_once, 16)
        sp.dma_start(self.bv[:, :], bv.unsqueeze(0).to_broadcast((P, 8 * P))).then_inc(self.w_once, 16)
        sp.dma_start(self.bo[:, :], bo.unsqueeze(0).to_broadcast((P, P))).then_inc(self.w_once, 16)
        if self.wo_by_head:
            sp.dma_start(self.wo_in[:, :, :].rearrange("p r (u h) -> p (r u) h", u=2), wo.rearrange("n d h -> d n h")).then_inc(self.w_once, 16)
        else:
            sp.dma_start(self.wo[:, :, :], wo.rearrange("(r p) d -> p r d", p=P)).then_inc(self.w_once, 16)

    def load_rounds(self, sp, wq, wk, bq, bk):
        with sp.Fori(0, self.ROUNDS - 1) as it:
            sp.wait_ge(self.q_sb, it * B + B)
            sp.wait_ge(self.k_sb, it * B + B)
            nxt = it * P + P
            sp.dma_start(self.wq[:, :], wq[:, ds(nxt, P)]).then_inc(self.w_in, 16)
            sp.dma_start(self.wk[:, :], wk[:, ds(nxt, P)]).then_inc(self.w_in, 16)
            sp.dma_start(self.bq[:, :], bq[ds(nxt, P)].unsqueeze(1)).then_inc(self.w_in, 16)
            sp.dma_start(self.bk[:, :], bk[ds(nxt, P)].unsqueeze(1)).then_inc(self.w_in, 16)

    def tensor(self, pe):
        PS, ident = self.k.PS, self.k.ident
        pe.wait_ge(self.k.ln.s_yT, self.yT_in)
        pe.wait_ge(self.w_once, 64)
        if self.wo_by_head:
            for r in range(8):
                mm = pe.transpose(PS[:, self.G[r // 4], (r % 4) * P:(r % 4) * P + P], self.wo_in[:, r, :], ident)
            mm.then_inc(self.wo_ps, 1)
            pe.wait_ge(self.x_add, 1)

        def free(u, it, last):
            seq = self.first if u in self.first else self.uses(last)
            n = seq.index(u)
            if u in self.first:
                before = [None, None, ("q", 0)][n]
            elif n < 2:
                pe.wait_ge(self.x_add, it * B + 1)
                before = self.first[n + 1]
            else:
                before = seq[n - 2]
            if before is None:
                return
            kind, b = before
            done, more = {"q": (self.q_sb, 0), "k": (self.k_sb, 0), "v": (self.v_sb, 0), "t": (self.sp_sb, 0),
                          "o": (self.x_add, 1)}[kind]
            pe.wait_ge(done, it * B + b + 1 + more)

        def project(kind, b, it, last=False):
            out = PS[:, self.bank((kind, b), last), :]
            free((kind, b), it, last)
            at = (b % B) * L
            nxt = b // B
            if kind == "q":
                if b % B == 0:
                    pe.wait_ge(self.w_in, it * 64 + 64 + 64 * nxt)
                pe.matmul(out[:, 0:L], self.wq[:, :], self.k.yT[:, at:at + L], start=True, stop=True).then_inc(self.q_ps, 1)
            elif kind == "k":
                n = L if self.causal else S2
                pe.matmul(out[:, 0:n], self.wk[:, :], self.k.ctxT[:, b % B, 0:n], start=True, stop=True).then_inc(self.k_ps, 1)
            elif kind == "v":
                for kt in range(2 if self.causal else 4):
                    mm = pe.matmul(out[:, kt * P:kt * P + P], self.k.ctxT[:, b % B, kt * P:kt * P + P], self.wv[:, ds(it * P + P * nxt, P)],
                                   start=True, stop=True)
                mm.then_inc(self.v_ps, 1)
            elif kind == "t":
                pe.wait_ge(self.iv, it * B + b + 1)
                for qt in range(QT):
                    mm = pe.matmul(out[:, qt * P:qt * P + P], self.inv[:, b % 2, qt, :], ident, start=True, stop=True)
                mm.then_inc(self.sp_ps, 1)
            else:
                pe.wait_ge(self.nm, it * B + b + 1)
                for qt in range(QT):
                    mm = pe.matmul(out[:, qt * P:qt * P + P], self.attT[:, b % 2, qt * P:qt * P + P],
                                   self.wo[:, ds(it, 1), :].rearrange("p a d -> p (a d)"), start=True, stop=True)
                mm.then_inc(self.wo_ps, 1)

        def scores(n, it):
            b, h, qt = self.where(n)
            if n % 4 == 0:
                pe.wait_ge(self.q_sb, it * B + b + 1)
                pe.wait_ge(self.k_sb, it * B + b + 1)
            if n >= 2:
                pe.wait_ge(self.ex, it * self.STEPS + n - 1)
            rows = slice(64 * h, 64 * h + 64)
            mm = pe.matmul(PS[:, self.S[n % 2], 0:self.keys(n)], self.qT[rows, b % 2, qt * P:qt * P + P],
                           self.kT[rows, b % 2, 0:self.keys(n)], start=True, stop=not self.causal)
            if self.causal:
                mm = pe.matmul(PS[:, self.S[n % 2], qt * P:qt * P + P], self.k.identb[:, :], self.k.trib[:, :],
                               start=False, stop=True)
            mm.then_inc(self.sc, 1)

        def turn(n, it):
            pe.wait_ge(self.ex, it * self.STEPS + n + 1)
            if n >= 2:
                pe.wait_ge(self.pt_a if n % 2 else self.pt_v, it * 8 + n // 2)
            for kt in range(self.keys(n) // P):
                mm = pe.transpose(PS[:, self.T[n % 2], kt * P:kt * P + P], self.probs[:, n % 2, kt * P:kt * P + P], ident)
            mm.then_inc(self.tr, 1)

        def times_v(n, it):
            b, h, qt = self.where(n)
            if n % 4 == 0:
                pe.wait_ge(self.v_sb, it * B + b + 1)
            pe.wait_ge(self.pt_a if n % 2 else self.pt_v, it * 8 + n // 2 + 1)
            if n % 4 == 0 and b >= 2:
                pe.wait_ge(self.nm, it * B + b - 1)
            last = self.keys(n) // P - 1
            for kt in range(last + 1):
                mm = pe.matmul(PS[64 * h:64 * h + 64, self.O[b % 2], qt * P:qt * P + P], self.v[:, b % 2, kt, 64 * h:64 * h + 64],
                               self.pT[:, n % 2, kt * P:kt * P + P], start=(kt == 0), stop=(kt == last))
            mm.then_inc(self.av, 1)

        def round_of_steps(it, last):
            for n in range(self.STEPS):
                b, r = n // 4, n % 4
                ahead = b + 1 < B or not last
                turn(n, it)
                if n + 2 < self.STEPS or not last:
                    scores(n + 2, it)
                if n >= 1:
                    times_v(n - 1, it)
                if r == 0 and ahead:
                    project("q", b + 1, it, last)
                    project("k", b + 1, it, last)
                if r == 1 and ahead:
                    project("v", b + 1, it, last)
                if r == 1 and b >= 1:
                    project("t", b - 1, it, last)
                if r == 3 and b >= 1:
                    project("o", b - 1, it, last)
            times_v(self.STEPS - 1, it)
            project("t", B - 1, it, last)
            project("o", B - 1, it, last)

        for kind in "qkv":
            project(kind, 0, 0)
        scores(0, 0)
        scores(1, 0)
        with pe.Fori(0, self.ROUNDS - 1) as it:
            round_of_steps(it, False)
        round_of_steps(self.ROUNDS - 1, True)

    def vector(self, v):
        PS = self.k.PS
        v.wait_ge(self.w_once, 64)
        if self.wo_by_head:
            v.wait_ge(self.wo_ps, 1)
            for i in range(2):
                v.tensor_copy(self.wo[:, 4 * i:4 * i + 4, :], PS[:, self.G[i], :].rearrange("p (r d) -> p r d", r=4))
        v.tensor_tensor(self.k.x[:, :, :], self.k.x[:, :, :], self.bo[:, :].unsqueeze(1).to_broadcast((P, TILES, P)),
                        ALU.add).then_inc(self.x_add, 1)
        v.wait_ge(self.x_add, 1)
        wo_extra = 1 if self.wo_by_head else 0

        def take_q(b, it, last=False):
            v.wait_ge(self.q_ps, it * B + b + 1)
            v.tensor_scalar(self.qT[:, b % 2, :], PS[:, self.bank(("q", b), last), 0:L], self.bq[:, 0:1], 0.125,
                            ALU.add, ALU.mult).then_inc(self.q_sb, 1)

        def take_v(b, it, last=False):
            v.wait_ge(self.v_ps, it * B + b + 1)
            n = 2 if self.causal else 4
            v.tensor_tensor(self.v[:, b % 2, 0:n, :], PS[:, self.bank(("v", b), last), 0:n * P].rearrange("p (t d) -> p t d", t=n),
                            self.bv[:, ds(it * P + P * (b // B), P)].unsqueeze(1).to_broadcast((P, n, P)), ALU.add).then_inc(self.v_sb, 1)

        def invert(b, it):
            v.wait_ge(self.ex, it * self.STEPS + 4 * b + 4)
            sums = self.sums[:, 4 * (b % 2):4 * (b % 2) + 4].rearrange("p (h t) -> p t h", t=QT)
            v.reciprocal(self.inv_few[:, :, :], sums).then_inc(self.iv_few, 1)

        def repeat(b, it):
            v.wait_ge(self.iv_few, it * B + b + 1)
            v.tensor_copy(self.inv[:, b % 2, :, :].rearrange("p t (h f) -> p t h f", h=2),
                          self.inv_few[:, :, :].unsqueeze(3).to_broadcast((P, QT, 2, 64))).then_inc(self.iv, 1)

        def normalise(b, it):
            v.wait_ge(self.sp_sb, it * B + b + 1)
            v.wait_ge(self.av, it * self.STEPS + 4 * b + 4)
            v.tensor_tensor(self.attT[:, b % 2, :], PS[:, self.O[b % 2], 0:L], self.spread[:, b % 2, :], ALU.mult).then_inc(self.nm, 1)

        def add_x(b, it, last):
            v.wait_ge(self.wo_ps, it * B + b + 1 + wo_extra)
            v.tensor_tensor(self.k.x[:, 2 * b:2 * b + 2, :], self.k.x[:, 2 * b:2 * b + 2, :],
                            PS[:, self.bank(("o", b), last), 0:L].rearrange("p (t d) -> p t d", t=QT), ALU.add).then_inc(self.x_add, 1)

        def maximum(n, it):
            v.wait_ge(self.sc, it * self.STEPS + n + 1)
            v.tensor_reduce(self.nmax[:, n % 4:n % 4 + 1], PS[:, self.S[n % 2], 0:self.keys(n)], AX.X, ALU.max,
                            negate=True).then_inc(self.mx, 1)

        def round_of_steps(it, last):
            for n in range(self.STEPS):
                b, r = n // 4, n % 4
                ahead = b + 1 < B or not last
                if n % 2 == 0:
                    v.wait_ge(self.tr, it * self.STEPS + n + 1)
                    w = self.keys(n)
                    v.tensor_copy(self.pT[:, 0, 0:w], PS[:, self.T[0], 0:w]).then_inc(self.pt_v, 1)
                if n + 2 < self.STEPS or not last:
                    maximum(n + 2, it)
                if r == 0 and b >= 1:
                    invert(b - 1, it)
                if r == 0 and ahead:
                    take_q(b + 1, it, last)
                if r == 0 and b >= 1:
                    repeat(b - 1, it)
                if r == 1 and ahead:
                    take_v(b + 1, it, last)
                if r == 2 and b >= 1:
                    normalise(b - 1, it)
                if r == 3 and b >= 1:
                    add_x(b - 1, it, last)
            invert(B - 1, it)
            repeat(B - 1, it)
            normalise(B - 1, it)
            add_x(B - 1, it, last)

        take_q(0, 0)
        take_v(0, 0)
        maximum(0, 0)
        maximum(1, 0)
        with v.Fori(0, self.ROUNDS - 1) as it:
            round_of_steps(it, False)
        round_of_steps(self.ROUNDS - 1, True)

    def scalar(self, act):
        PS = self.k.PS

        def take_k(b, it, last=False):
            act.wait_ge(self.k_ps, it * B + b + 1)
            n = L if self.causal else S2
            act.activation(self.kT[:, b % 2, 0:n], PS[:, self.bank(("k", b), last), 0:n], ACT.Identity, bias=self.bk[:, 0:1]).then_inc(self.k_sb, 1)

        def take_spread(b, it, last):
            act.wait_ge(self.sp_ps, it * B + b + 1)
            act.copy(self.spread[:, b % 2, :], PS[:, self.bank(("t", b), last), 0:L]).then_inc(self.sp_sb, 1)

        def exponent(n, it):
            act.wait_ge(self.mx, it * self.STEPS + n + 1)
            if n >= 2:
                act.wait_ge(self.tr, it * self.STEPS + n - 1)
            w = self.keys(n)
            act.activation(self.probs[:, n % 2, 0:w], PS[:, self.S[n % 2], 0:w], ACT.Exp,
                           bias=self.nmax[:, n % 4:n % 4 + 1], accum_out=self.sums[:, n % 8:n % 8 + 1]).then_inc(self.ex, 1)

        def round_of_steps(it, last):
            for n in range(self.STEPS):
                b, r = n // 4, n % 4
                if n % 2 == 1:
                    act.wait_ge(self.tr, it * self.STEPS + n + 1)
                    w = self.keys(n)
                    act.copy(self.pT[:, 1, 0:w], PS[:, self.T[1], 0:w]).then_inc(self.pt_a, 1)
                if n + 2 < self.STEPS or not last:
                    exponent(n + 2, it)
                if r == 0 and (b + 1 < B or not last):
                    take_k(b + 1, it, last)
                if r == 1 and b >= 1:
                    take_spread(b - 1, it, last)
            take_spread(B - 1, it, last)

        take_k(0, 0)
        exponent(0, 0)
        exponent(1, 0)
        with act.Fori(0, self.ROUNDS - 1) as it:
            round_of_steps(it, False)
        round_of_steps(self.ROUNDS - 1, True)

class ShiftMix:

    def __init__(self, k, norm):
        self.yT_in = 2 * (norm + 1)
        self.k = k
        self.w_in = k.lb("mix_w_in", [P, 3, P])
        self.wT = k.lb("mix_wT", [P, 3, P])
        self.mu = k.lb("mix_mu", [P, 2])
        self.omu = k.lb("mix_one_minus_mu", [P, 2])
        self.xr = k.lb("mix_xr", [P, B, L])
        self.xk = k.lb("mix_xk", [P, B, L])
        self.kr = k.lb("mix_relu", [P, B * L])
        self.ka = k.lb("mix_k_act", [P, B * L])
        self.r = k.lb("mix_r", [P, TILES, P])
        self.t = k.lb("mix_t", [P, TILES, P])
        s = k.sem
        self.loaded, self.w_ps, self.w_sb = s("mix_loaded"), s("mix_w_turned"), s("mix_w_ready")
        self.mixed, self.own = s("mix_mixed"), s("mix_vector")
        self.k_ps, self.kr_sb, self.ka_sb = s("mix_k_product"), s("mix_relu_done"), s("mix_square_done")
        self.r_ps, self.r_sb, self.o_ps = s("mix_r_product"), s("mix_r_done"), s("mix_out_product")

    def load(self, sp, wr, wk, wv, mu_r, mu_k):
        for i, w in enumerate((wr, wk, wv)):
            sp.dma_start(self.w_in[:, i, :], w).then_inc(self.loaded, 16)
        for i, m in enumerate((mu_r, mu_k)):
            sp.dma_start(self.mu[:, i:i + 1], m.unsqueeze(1)).then_inc(self.loaded, 16)

    def tensor(self, pe):
        PS = self.k.PS
        pe.wait_ge(self.loaded, 80)
        for i in range(3):
            mm = pe.transpose(PS[:, 0, i * P:i * P + P], self.w_in[:, i, :], self.k.ident)
        mm.then_inc(self.w_ps, 1)
        pe.wait_ge(self.w_sb, 1)
        pe.wait_ge(self.mixed, 1)
        for f in range(2):
            pe.matmul(PS[:, 1 + f, :], self.wT[:, 1, :], self.xk[:, 2 * f:2 * f + 2, :].rearrange("p b l -> p (b l)"),
                      start=True, stop=True).then_inc(self.k_ps, 1)
        pe.wait_ge(self.mixed, 2)
        for t in range(TILES):
            mm = pe.matmul(PS[:, 3 + t // 4, (t % 4) * P:(t % 4) * P + P],
                           self.xr[:, t // 2, (t % 2) * P:(t % 2) * P + P], self.wT[:, 0, :], start=True, stop=True)
            if t % 4 == 3:
                mm.then_inc(self.r_ps, 1)
        for t in range(TILES):
            if t % 4 == 0:
                pe.wait_ge(self.ka_sb, t // 4 + 1)
            mm = pe.matmul(PS[:, (0, 5)[t // 4], (t % 4) * P:(t % 4) * P + P], self.ka[:, t * P:t * P + P], self.wT[:, 2, :],
                           start=True, stop=True)
            if t % 4 == 3:
                mm.then_inc(self.o_ps, 1)

    def vector(self, v):
        PS = self.k.PS
        v.wait_ge(self.loaded, 80)
        v.wait_ge(self.w_ps, 1)
        v.tensor_copy(self.wT[:, :, :], PS[:, 0, 0:3 * P].rearrange("p (i d) -> p i d", i=3)).then_inc(self.w_sb, 1)
        v.tensor_scalar(self.omu[:, :], self.mu[:, :], -1.0, 1.0, ALU.mult, ALU.add).then_inc(self.own, 1)
        v.wait_ge(self.k.ln.s_yT, self.yT_in)
        yT = self.k.yT[:, :].rearrange("p (b l) -> p b l", b=B)
        for i, dst in ((1, self.xk), (0, self.xr)):
            v.tensor_scalar(dst[:, :, :], yT, self.mu[:, i:i + 1], None, ALU.mult).then_inc(self.own, 1)
        for n, (i, dst) in enumerate(((1, self.xk), (0, self.xr))):
            v.wait_ge(self.own, 2 + n)
            v.scalar_tensor_tensor(dst[:, :, 1:L], yT[:, :, 0:L - 1], self.omu[:, i:i + 1], dst[:, :, 1:L],
                                   ALU.mult, ALU.add).then_inc(self.mixed, 1)
        for f in range(2):
            v.wait_ge(self.kr_sb, f + 1)
            r = slice(f * BANK, f * BANK + BANK)
            v.tensor_tensor(self.ka[:, r], self.kr[:, r], self.kr[:, r], ALU.mult).then_inc(self.ka_sb, 1)
        for f in range(2):
            v.wait_ge(self.o_ps, f + 1)
            v.wait_ge(self.r_sb, f + 1)
            r = slice(4 * f, 4 * f + 4)
            v.tensor_tensor(self.t[:, r, :], self.r[:, r, :], PS[:, (0, 5)[f], :].rearrange("p (t d) -> p t d", t=4),
                            ALU.mult).then_inc(self.own, 1)
            v.wait_ge(self.own, 4 + f)
            v.tensor_tensor(self.k.x[:, r, :], self.k.x[:, r, :], self.t[:, r, :], ALU.add)

    def scalar(self, act):
        PS = self.k.PS
        for f in range(2):
            act.wait_ge(self.k_ps, f + 1)
            act.activation(self.kr[:, f * BANK:f * BANK + BANK], PS[:, 1 + f, :], ACT.Relu).then_inc(self.kr_sb, 1)
        for f in range(2):
            act.wait_ge(self.r_ps, f + 1)
            act.activation(self.r[:, 4 * f:4 * f + 4, :], PS[:, 3 + f, :].rearrange("p (t d) -> p t d", t=4), ACT.Sigmoid).then_inc(self.r_sb, 1)

class NarrowAttention:

    S, T, O, G = (0, 1), (2, 3), (4, 5), (6, 7)
    ROWS = D8 + 2
    QR = HEADS8 * REG

    def __init__(self, k, name, norm, by_class):
        self.yT_in = 2 * (norm + 1)
        self.k, self.name, self.by_class = k, name, by_class
        n = name + "_"
        self.keys = L if by_class else S2
        self.width = L if by_class else S2 // 4
        self.heads = BANK // self.width
        self.steps = QT * HEADS8 // self.heads
        self.kts = self.width // P
        self.w_in = k.sb(n + "w_in", [P, 3, P])
        self.wo = k.sb(n + "wo", [P, 4, P])
        self.bo = k.sb(n + "bo", [P, P])
        if by_class:
            self.g = k.sb(n + "g", [P, P])
        else:
            self.bqp = k.sb(n + "bq", [P, 4])
            self.bkp = k.sb(n + "bk", [P, 4])
            self.bv_in = k.sb(n + "bv_in", [P, P])
            self.mask = k.sb(n + "mask", [1, B * S2 // 4], U32)
        s = k.sem
        self.loaded = s(n + "weights_loaded")
        self.padded = s(n + "weights_padded")
        self.zeroed = s(n + "zeroed")
        self.batch_in = s(n + "batch_in")
        self.product = s(n + "product")
        self.by_v, self.by_a = s(n + "taken_by_vector"), s(n + "taken_by_scalar")
        self.sc, self.mx, self.ex, self.tr = s(n + "scores"), s(n + "max"), s(n + "probs"), s(n + "turned")
        self.pt_v, self.pt_a = s(n + "pT_even"), s(n + "pT_odd")
        self.av, self.iv_few, self.iv, self.nm = s(n + "pv"), s(n + "inverse"), s(n + "inverse_repeated"), s(n + "normed")
        self.cls_sb = s(n + "classes_ready")
        if by_class:
            self.own, self.rooted, self.reduced = s(n + "find_vector"), s(n + "rooted"), s(n + "ends_reduced")
            self.qn_ps, self.c_ps = s(n + "q_natural"), s(n + "classes_turned")
            self.rmx, self.riv = s(n + "r_max_done"), s(n + "r_inverse")
            self.ahead = {6: [("q", 0)], 7: [("q", 1)], 8: [("k", 0)], 10: [("k", 1)], 12: [("v", 0)], 13: [("v", 1)], 14: [("rq", 0)]}
            self.own_uses = {2: [("rs", 0)], 4: [("rt", 0)], 5: [("rp", 0)], 9: [("rm", 0), ("t", 0)], 11: [("o", 0)]}
            self.late = {1: [("t", 1)], 3: [("o", 1)]}
        else:
            self.ahead = {1: [("q", 0)], 2: [("q", 1)], 3: [("k", 0)], 4: [("k", 1), ("k", 2)], 5: [("k", 3)], 7: [("v", 0)]}
            self.own_uses = {5: [("t", 0)], 6: [("o", 0)]}
            self.late = {1: [("t", 1)], 2: [("o", 1)]}
        self.first = [u + (0,) for n in sorted(self.ahead) for u in self.ahead[n]]
        self.at = {}
        for n in range(2 * self.steps):
            par, r = n // self.steps, n % self.steps
            self.at[n] = ([u + (0,) for u in self.late.get(r, [])] if par else []) + [u + (par,) for u in self.own_uses.get(r, [])] \
                + [u + (1 - par,) for u in self.ahead.get(r, [])]
        self.last = [("t", 1, 1), ("o", 1, 1)]
        self.uses = [u for n in range(2 * self.steps) for u in self.at[n]] + self.last
        by_scalar = ("k", "rs", "rt", "t")
        self.is_a = lambda u: u[0] in by_scalar
        self.first_a, self.first_v = sum(map(self.is_a, self.first)), sum(not self.is_a(u) for u in self.first)
        self.a_uses = [u for u in self.uses if self.is_a(u)]
        self.v_uses = [u for u in self.uses if not self.is_a(u)]

    def bank(self, u, ahead):
        return self.G[(self.first.index(u) if ahead else len(self.first) + self.uses.index(u)) % 2]

    def wait_product(self, eng, u, it, ahead=False):
        if ahead:
            eng.wait_ge(self.product, self.first.index(u) + 1)
        else:
            eng.wait_ge(self.product, it * len(self.uses) + len(self.first) + self.uses.index(u) + 1)

    def wait_taken(self, eng, u, it, ahead=False):
        seq = self.first if ahead else self.uses
        same = [w for w in seq if self.is_a(w) == self.is_a(u)]
        n = same.index(u) + 1
        if self.is_a(u):
            eng.wait_ge(self.by_a, n if ahead else it * len(same) + self.first_a + n)
        else:
            eng.wait_ge(self.by_v, n + 1 if ahead else it * len(same) + self.first_v + n + 1)

    def place(self):
        k, by_class, n = self.k, self.by_class, self.name + "_"
        self.wq = k.lb(n + "wq", [P, 4 * P])
        self.wk = k.lb(n + "wk", [P, 4 * P])
        self.qp = k.lb(n + "q", [P, 2, 4, L])
        self.kp = k.lb(n + "k", [P, 2, 4, self.keys])
        self.wv = k.lb(n + "wv", [P, 4 * P])
        self.v = k.lb(n + "v", [P, 2, self.kts * 4 * P])
        self.yb = k.lb(n + "y_of_batch", [P, L])
        self.cqb = k.lb(n + "cq_of_batch", [2, L], BF16)
        self.ckb = k.lb(n + "ck_of_batch", [2, self.keys], BF16)
        self.ck = k.lb(n + "ck", [2, B * self.keys], BF16)
        self.probs = k.lb(n + "probs", [P, 2, BANK])
        self.pT = k.lb(n + "pT", [P, 2, BANK])
        self.nmax = k.lb(n + "nmax", [P, 2, self.heads])
        self.sums = k.lb(n + "sums", [P, QT, HEADS8])
        self.inv = k.lb(n + "inv", [P, QT, 4 * P])
        self.inv_few = k.lb(n + "inv_few", [P, HEADS8])
        self.spread = k.lb(n + "inverse_spread", [P, QT, 4 * P])
        self.attT = k.lb(n + "attT", [P, QT, 4, P])
        if by_class:
            self.cq = k.lb(n + "cq", [2, B * L], BF16)
            self.prod = self.probs[:, :, :].rearrange("p a (t d) -> p (a t) d", d=P)
            self.ss = k.lb(n + "ss", [P, TILES * HEADS8 + HEADS8])
            self.dots = k.lb(n + "dots", [P, TILES * HEADS8])
            self.sim = k.lb(n + "sim", [P, TILES])
            self.ends = k.lb(n + "ends", [P, 2, TILES])
            self.ends_p = k.lb(n + "ends_of_partition", [P, 2])
            self.ends_2 = k.lb(n + "ends_diagonal", [2, 2])
            self.ends_1 = k.lb(n + "ends_row", [2, 1])
            self.ends_all = k.lb(n + "ends_all", [P, 2])
            self.span = k.lb(n + "span", [P, 1])
            self.cls = k.lb(n + "cls", [P, TILES, 4])
            self.qbd = k.lb(n + "q_registers", [P, 4, HEADS8, REG])
            self.rmax = k.lb(n + "r_max", [P, 1])
            self.rsum = k.lb(n + "r_sum", [P, 1])
            self.rinv = k.lb(n + "r_inv", [P, 1])
            self.rprobs = k.lb(n + "r_probs", [P, L])
            self.rpT = k.lb(n + "r_pT", [P, 2 * self.QR])
            self.ratt = k.lb(n + "r_att", [P, 4 * P])
        else:
            self.bv = k.lb(n + "bv", [P, 4 * P])
            self.cb = k.lb(n + "ctx_of_batch", [P, S2])

    def where(self, n):
        per = self.steps // QT
        qt, r = n % self.steps // per, n % per
        return qt, r % 4, range(self.heads * (r // 4), self.heads * (r // 4) + self.heads)

    def load(self, sp, wq, wk, wv, wo, bo, bq=None, bk=None, bv=None, mask=None, g=None):
        sp.wait_ge(self.zeroed, 1)
        for g4 in range(4):
            sp.dma_start(self.wo[32 * g4:32 * g4 + D8, :, :], wo.rearrange("(t g e) d -> g e t d", t=4, g=4)[g4]).then_inc(self.loaded, 16)
        for i, w in enumerate((wq, wk, wv)):
            sp.dma_start(self.w_in[:, i, :], w).then_inc(self.loaded, 16)
        sp.dma_start(self.bo[:, :], bo.unsqueeze(0).to_broadcast((P, P))).then_inc(self.loaded, 16)
        if self.by_class:
            sp.dma_start(self.g[:, :], g.unsqueeze(0).to_broadcast((P, P))).then_inc(self.loaded, 16)
            self.n_loads = 9 * 16
        else:
            sp.dma_start(self.bv_in[:, :], bv.unsqueeze(0).to_broadcast((P, P))).then_inc(self.loaded, 16)
            sp.dma_start(self.mask[:, :], mask.rearrange("(o b) s -> o (b s)", o=1)).then_inc(self.loaded, 16)
            sp.wait_ge(self.zeroed, 3)
            for dst, b in ((self.bqp, bq), (self.bkp, bk)):
                for gr in range(4):
                    sp.dma_start(dst[32 * gr:32 * gr + D8, :], b.rearrange("(t g e) -> g e t", t=4, g=4)[gr]).then_inc(self.loaded, 16)
            self.n_loads = 18 * 16

    def pool_zero(self, pool):
        pool.memset(self.wo[:, :, :], 0.0).then_inc(self.zeroed, 1)
        if not self.by_class:
            pool.memset(self.bqp[:, :], 0.0).then_inc(self.zeroed, 1)
            pool.memset(self.bkp[:, :], 0.0).then_inc(self.zeroed, 1)

    def pool_pad(self, pool):
        pool.memset(self.wq[:, :], 0.0).then_inc(self.zeroed, 1)
        pool.memset(self.wk[:, :], 0.0).then_inc(self.zeroed, 1)
        pool.memset(self.wv[:, :], 0.0).then_inc(self.zeroed, 1)
        if not self.by_class:
            pool.memset(self.cqb[:, :], 1.0)
            pool.memset(self.bv[:, :], 0.0)
            pool.memset(self.ck[:, :], 0.0).then_inc(self.zeroed, 1)
        pool.wait_ge(self.loaded, self.n_loads)
        pool.wait_ge(self.zeroed, 4 if self.by_class else 7)
        for i, w in ((0, self.wq), (1, self.wk), (2, self.wv)) if self.by_class else ((0, self.wq), (1, self.wk)):
            pool.tensor_copy(w[:, :].rearrange("p (h e) -> p h e", e=32)[:, :, 0:D8],
                             self.w_in[:, i, :].rearrange("p (h e) -> p h e", e=D8)).then_inc(self.padded, 1)
        if not self.by_class:
            for dst, src in ((self.wv, self.w_in[:, 2, :]), (self.bv, self.bv_in[:, :])):
                pool.tensor_copy(dst[:, :].rearrange("p (g t e) -> p g t e", g=4, t=4)[:, :, :, 0:D8],
                                 src.rearrange("p (t g e) -> p g t e", g=4, t=4)).then_inc(self.padded, 1)

    def pool_batches(self, pool):
        pool.wait_ge(self.cls_sb, 2)
        pool.wait_ge(self.k.ln.s_yT, self.yT_in)

        def bring(at):
            pool.tensor_copy(self.yb[:, :], self.k.yT[:, ds(at * L, L)])
            if self.by_class:
                pool.tensor_copy(self.cqb[:, :], self.cq[:, ds(at * L, L)])
            else:
                pool.tensor_copy(self.cb[:, :], self.k.ctxT[:, ds(at, 1), :].rearrange("p a s -> p (a s)"))
            pool.tensor_copy(self.ckb[:, :], self.ck[:, ds(at * self.keys, self.keys)]).then_inc(self.batch_in, 1)

        bring(0)
        for b in range(1, B):
            kind = "rq" if self.by_class else "v"
            if b == 1:
                self.wait_product(pool, (kind, 0, 0), 0, ahead=True)
            else:
                self.wait_product(pool, (kind, 0, (b - 1) % 2), (b - 2) // 2)
            bring(b)
        pool.drain().then_inc(self.batch_in, 1)

    def vector_find(self, v):
        cst = self.k.cst
        reg = cst[:, C_REG:C_REG + TILES]
        heads = lambda a: a.rearrange("p (h e) -> p h e", e=D8)
        v.wait_ge(self.loaded, self.n_loads)
        flat = self.prod.rearrange("p t (h e) -> p (t h) e", e=D8)
        v.tensor_tensor(self.prod[:, 0, :], self.g[:, :], self.g[:, :], ALU.mult).then_inc(self.own, 1)
        v.wait_ge(self.own, 1)
        v.tensor_reduce(self.ss[:, TILES * HEADS8:], flat[:, 0:HEADS8, :], AX.X, ALU.add).then_inc(self.own, 1)
        v.wait_ge(self.qn_ps, 1)
        v.wait_ge(self.own, 2)
        qn = self.k.PS[:, 0:2, :].rearrange("p f (t d) -> p (f t) d", d=P)
        v.tensor_copy(self.prod, qn).then_inc(self.own, 1)
        v.wait_ge(self.own, 3)
        v.tensor_tensor(self.prod, self.prod, qn, ALU.mult).then_inc(self.own, 1)
        v.wait_ge(self.own, 4)
        v.tensor_reduce(self.ss[:, 0:TILES * HEADS8], flat, AX.X, ALU.add).then_inc(self.own, 1)
        v.wait_ge(self.own, 5)
        v.tensor_tensor(self.prod, qn, self.g[:, :].unsqueeze(1).to_broadcast((P, TILES, P)), ALU.mult).then_inc(self.own, 1)
        v.wait_ge(self.own, 6)
        v.tensor_reduce(self.dots[:, :], flat, AX.X, ALU.add).then_inc(self.own, 1)
        v.wait_ge(self.rooted, 1)
        v.reciprocal(self.ss[:, :], self.ss[:, :]).then_inc(self.own, 1)
        v.wait_ge(self.own, 8)
        v.tensor_tensor(self.dots[:, :], self.dots[:, :], self.ss[:, 0:TILES * HEADS8], ALU.mult).then_inc(self.own, 1)
        v.wait_ge(self.own, 9)
        dots = self.dots[:, :].rearrange("p (t h) -> p t h", h=HEADS8)
        v.tensor_tensor(dots, dots, self.ss[:, TILES * HEADS8:].unsqueeze(1).to_broadcast((P, TILES, HEADS8)), ALU.mult).then_inc(self.own, 1)
        v.wait_ge(self.own, 10)
        v.tensor_reduce(self.sim[:, :], dots, AX.X, ALU.add).then_inc(self.own, 1)
        v.wait_ge(self.own, 11)
        v.scalar_tensor_tensor(self.ends[:, 0, :], reg, -BIG, self.sim[:, :], ALU.mult, ALU.add).then_inc(self.own, 1)
        v.scalar_tensor_tensor(self.ends[:, 1, :], reg, -BIG, self.sim[:, :], ALU.mult, ALU.subtract).then_inc(self.own, 1)
        v.wait_ge(self.own, 13)
        v.tensor_reduce(self.ends_p[:, :], self.ends[:, :, :], AX.X, ALU.max).then_inc(self.own, 1)
        v.wait_ge(self.reduced, 1)
        v.tensor_reduce(self.ends_1[:, :], self.k.PS[0:2, 2, 0:P], AX.X, ALU.max).then_inc(self.own, 1)
        v.wait_ge(self.own, 15)
        v.tensor_scalar(self.ends_2[:, :], cst[0:2, C_ID:C_ID + 2], self.ends_1[:, 0:1], None, ALU.mult).then_inc(self.own, 1)
        v.wait_ge(self.reduced, 2)
        v.tensor_copy(self.ends_all[:, :], self.k.PS[:, 3, 0:2]).then_inc(self.own, 1)
        v.wait_ge(self.own, 17)
        v.tensor_tensor(self.span[:, :], self.ends_all[:, 0:1], self.ends_all[:, 1:2], ALU.add).then_inc(self.own, 1)
        v.wait_ge(self.own, 18)
        v.reciprocal(self.span[:, :], self.span[:, :]).then_inc(self.own, 1)
        v.wait_ge(self.own, 19)
        v.tensor_scalar(self.sim[:, :], self.sim[:, :], self.ends_all[:, 1:2], self.span[:, 0:1], ALU.add, ALU.mult).then_inc(self.own, 1)
        v.wait_ge(self.own, 20)
        c = self.cls
        v.scalar_tensor_tensor(c[:, :, 0], self.sim[:, :], 0.9, reg, ALU.is_gt, ALU.max).then_inc(self.own, 1)
        v.wait_ge(self.own, 21)
        v.tensor_scalar(c[:, :, 1], c[:, :, 0], -1.0, 1.0, ALU.mult, ALU.add).then_inc(self.own, 1)
        v.tensor_tensor(c[:, :, 3], reg, c[:, :, 0], ALU.subtract).then_inc(self.own, 1)
        v.wait_ge(self.own, 23)
        v.tensor_scalar(c[:, :, 2], c[:, :, 1], -BIG, None, ALU.mult).then_inc(self.own, 1)
        v.tensor_scalar(c[:, :, 3], c[:, :, 3], BIG, None, ALU.mult).then_inc(self.own, 1)
        v.wait_ge(self.c_ps, 1)
        for dst, bank in ((self.cq, 2), (self.ck, 4)):
            v.tensor_copy(dst[:, :].rearrange("p (f c) -> p f c", f=2), self.k.PS[0:2, bank:bank + 2, :]).then_inc(self.cls_sb, 1)

    def vector_padding(self, v):
        v.wait_ge(self.loaded, self.n_loads)
        v.wait_ge(self.zeroed, 7)
        v.tensor_scalar(self.ck[0:1, :], self.mask[:, :].bitcast(U8), -BIG, None, ALU.mult).then_inc(self.cls_sb, 2)

    def vector(self, v):
        PS, cst, x = self.k.PS, self.k.cst, self.k.x
        v.wait_ge(self.loaded, self.n_loads)
        v.tensor_tensor(x[:, :, :], x[:, :, :], self.bo[:, :].unsqueeze(1).to_broadcast((P, TILES, P)), ALU.add).then_inc(self.by_v, 1)
        if not self.by_class:
            v.wait_ge(self.padded, 4)

        def take(u, it, ahead=False):
            kind, i, par = u
            bank = PS[:, self.bank(u, ahead), :]
            self.wait_product(v, u, it, ahead)
            if kind == "q":
                if self.by_class:
                    v.tensor_scalar(self.qp[:, par, 2 * i:2 * i + 2, :], bank.rearrange("p (t l) -> p t l", t=2), SCALE8, None,
                                    ALU.mult).then_inc(self.by_v, 1)
                else:
                    for t in (2 * i, 2 * i + 1):
                        ins = v.tensor_scalar(self.qp[:, par, t, :], bank[:, (t % 2) * L:(t % 2) * L + L], self.bqp[:, t:t + 1], SCALE8,
                                              ALU.add, ALU.mult)
                    ins.then_inc(self.by_v, 1)
            elif kind == "v":
                if self.by_class:
                    v.tensor_copy(self.v[:, par, i * BANK:i * BANK + BANK], bank).then_inc(self.by_v, 1)
                else:
                    v.tensor_tensor(self.v[:, par, :], bank, self.bv[:, :], ALU.add).then_inc(self.by_v, 1)
            elif kind == "rq":
                v.tensor_tensor(self.qbd[:, :, :, :],
                                bank[:, 0:4 * REG].rearrange("p (t i) -> p t i", t=4).unsqueeze(2).to_broadcast((P, 4, HEADS8, REG)),
                                cst[:, C_OWN:C_OWN + 64].rearrange("p (t h) -> p t h", t=4).unsqueeze(3).to_broadcast((P, 4, HEADS8, REG)),
                                ALU.mult).then_inc(self.by_v, 1)
            elif kind == "rp":
                v.reciprocal(self.rinv[0:self.QR, :], self.rsum[0:self.QR, :]).then_inc(self.riv, 1)
                v.wait_ge(self.riv, it * 2 + par + 1)
                v.scalar_tensor_tensor(self.ratt[0:self.QR, :], bank[0:self.QR, :], self.rinv[0:self.QR, 0:1],
                                       cst[0:self.QR, C_DIAG:C_DIAG + 4 * P], ALU.mult, ALU.mult).then_inc(self.by_v, 1)
            elif kind == "rm":
                v.wait_ge(self.nm, it * 2 * QT + par * QT + 1)
                first = self.attT[:, 0, :, 0:REG]
                v.scalar_tensor_tensor(first, first, 0.5, bank[:, 0:4 * REG].rearrange("p (t i) -> p t i", t=4), ALU.mult, ALU.add).then_inc(self.by_v, 1)
            else:
                row = x[:, ds(it * 2 * QT + par * QT + i, 1), :].rearrange("p a d -> p (a d)")
                v.tensor_tensor(row, row, bank[:, 0:P], ALU.add).then_inc(self.by_v, 1)

        def normalise(u, it):
            _, qt, par = u
            self.wait_taken(v, u, it)
            v.wait_ge(self.av, it * 2 * self.steps + par * self.steps + (qt + 1) * per)
            v.tensor_tensor(self.attT[:, qt, :, :].rearrange("p t l -> p (t l)"), PS[:, self.O[qt], :], self.spread[:, qt, :],
                            ALU.mult).then_inc(self.nm, 1)

        def maximum(n, it):
            v.wait_ge(self.sc, it * 2 * self.steps + n + 1)
            v.tensor_reduce(self.nmax[:, n % 2, :], PS[:, self.S[n % 2], :].rearrange("p (j s) -> p j s", j=self.heads), AX.X, ALU.max,
                            negate=True).then_inc(self.mx, 1)

        per = self.steps // QT
        def invert(n, it):
            qt = self.where(n)[0]
            v.wait_ge(self.ex, it * 2 * self.steps + n + 1)
            v.reciprocal(self.inv_few[:, :], self.sums[:, qt, :]).then_inc(self.iv_few, 1)
            v.wait_ge(self.iv_few, it * 2 * QT + (n + 1) // per)
            v.tensor_copy(self.inv[:, qt, :].rearrange("p (h f) -> p h f", f=32),
                          self.inv_few[:, :].unsqueeze(2).to_broadcast((P, HEADS8, 32))).then_inc(self.iv, 1)

        for u in self.first:
            if not self.is_a(u):
                take(u, 0, ahead=True)
        with v.Fori(0, B // 2) as it:
            for n in range(-2, 2 * self.steps + 1):
                if 0 <= n < 2 * self.steps and n % 2 == 0:
                    v.wait_ge(self.tr, it * 2 * self.steps + n + 1)
                    v.tensor_copy(self.pT[:, 0, :], PS[:, self.T[0], :]).then_inc(self.pt_v, 1)
                if n + 2 < 2 * self.steps:
                    maximum(n + 2, it)
                if n >= per and n % per == 0:
                    invert(n - 1, it)
                for u in sorted(self.at.get(n, []), key=lambda u: u[0] != "t"):
                    if u[0] == "t":
                        normalise(u, it)
                    elif u[0] == "rs":
                        self.wait_product(v, u, it)
                        v.tensor_reduce(self.rmax[0:self.QR, :], PS[0:self.QR, self.bank(u, False), 0:L], AX.X, ALU.max, negate=True).then_inc(self.rmx, 1)
                    elif not self.is_a(u):
                        take(u, it)
            normalise(self.last[0], it)
            take(self.last[1], it)

    def scalar_find(self, act):
        act.wait_ge(self.own, 5)
        act.activation(self.ss[:, :], self.ss[:, :], ACT.Sqrt).then_inc(self.rooted, 1)

    def scalar(self, act):
        PS = self.k.PS

        def take(u, it, ahead=False):
            kind, i, par = u
            bank = PS[:, self.bank(u, ahead), :]
            self.wait_product(act, u, it, ahead)
            if kind == "k":
                if self.by_class:
                    act.copy(self.kp[:, par, 2 * i:2 * i + 2, :], bank.rearrange("p (t l) -> p t l", t=2)).then_inc(self.by_a, 1)
                else:
                    act.activation(self.kp[:, par, i, :], bank, ACT.Identity, bias=self.bkp[:, i:i + 1]).then_inc(self.by_a, 1)
            elif kind == "rs":
                act.wait_ge(self.rmx, it * 2 + par + 1)
                act.activation(self.rprobs[0:self.QR, :], bank[0:self.QR, 0:L], ACT.Exp, bias=self.rmax[0:self.QR, 0:1],
                               accum_out=self.rsum[0:self.QR, :]).then_inc(self.by_a, 1)
            elif kind == "rt":
                act.copy(self.rpT[:, :], bank[:, 0:2 * self.QR]).then_inc(self.by_a, 1)
            else:
                act.copy(self.spread[:, i, :], bank).then_inc(self.by_a, 1)

        def exponent(n, it):
            act.wait_ge(self.mx, it * 2 * self.steps + n + 1)
            if n >= 2:
                act.wait_ge(self.tr, it * 2 * self.steps + n - 1)
            qt, g, quads = self.where(n)
            for j, t in enumerate(quads):
                h = 4 * t + g
                cols = slice(j * self.width, j * self.width + self.width)
                ins = act.activation(self.probs[:, n % 2, cols], PS[:, self.S[n % 2], cols], ACT.Exp, bias=self.nmax[:, n % 2, j:j + 1],
                                     accum_out=self.sums[:, qt, h:h + 1])
            ins.then_inc(self.ex, 1)

        for u in self.first:
            if self.is_a(u):
                take(u, 0, ahead=True)
        with act.Fori(0, B // 2) as it:
            for n in range(-2, 2 * self.steps):
                if n >= 0 and n % 2 == 1:
                    act.wait_ge(self.tr, it * 2 * self.steps + n + 1)
                    act.copy(self.pT[:, 1, :], PS[:, self.T[1], :]).then_inc(self.pt_a, 1)
                if n + 2 < 2 * self.steps:
                    exponent(n + 2, it)
                for u in self.at.get(n, []):
                    if self.is_a(u):
                        take(u, it)
            take(self.last[0], it)

    def tensor_find(self, pe):
        PS = self.k.PS
        pe.wait_ge(self.loaded, self.n_loads)
        pe.wait_ge(self.k.ln.s_yT, self.yT_in)
        for t in range(TILES):
            mm = pe.matmul(PS[:, t // 4, (t % 4) * P:(t % 4) * P + P], self.k.yT[:, t * P:t * P + P], self.w_in[:, 0, :], start=True, stop=True)
        mm.then_inc(self.qn_ps, 1)
        pe.wait_ge(self.own, 14)
        pe.transpose(PS[0:2, 2, 0:P], self.ends_p[:, :], self.k.ident).then_inc(self.reduced, 1)
        pe.wait_ge(self.own, 16)
        pe.matmul(PS[:, 3, 0:2], self.k.cst[0:2, C_ONE:C_ONE + P], self.ends_2[:, :], start=True, stop=True).then_inc(self.reduced, 1)
        pe.wait_ge(self.own, 25)
        for side, bank in ((0, 2), (2, 4)):
            for t in range(TILES):
                mm = pe.transpose(PS[0:2, bank + t // 4, (t % 4) * P:(t % 4) * P + P], self.cls[:, t, side:side + 2], self.k.ident)
        mm.then_inc(self.c_ps, 1)

    def tensor(self, pe):
        PS, cst, ident = self.k.PS, self.k.cst, self.k.ident
        pe.wait_ge(self.padded, 3 if self.by_class else 4)
        pe.wait_ge(self.cls_sb, 2)
        src = self.yb if self.by_class else self.cb
        classes, negative = self.k.classb[:, 0:P], self.k.classb[:, P:P + REG]

        def product(u, it, ahead=False):
            kind, i, par = u
            bank = PS[:, self.bank(u, ahead), :]
            seq = self.first if ahead else self.uses
            if seq.index(u) >= 2:
                self.wait_taken(pe, seq[seq.index(u) - 2], it, ahead)
            if u[0:2] == ("q", 0):
                pe.wait_ge(self.batch_in, 1 if ahead else it * 2 + (2 if par else 3))
            if kind == "q":
                for t in (2 * i, 2 * i + 1):
                    out = bank[:, (t % 2) * L:(t % 2) * L + L]
                    pe.matmul(out, self.wq[:, t * P:t * P + P], self.yb[:, :], start=True, stop=False)
                    mm = pe.matmul(out, classes, self.cqb[:, :], start=False, stop=True)
            elif kind == "k":
                for t in ((2 * i, 2 * i + 1) if self.by_class else (i,)):
                    out = bank[:, (t % 2) * L:(t % 2) * L + L] if self.by_class else bank
                    pe.matmul(out, self.wk[:, t * P:t * P + P], src[:, :], start=True, stop=False)
                    mm = pe.matmul(out, classes, self.ckb[:, :], start=False, stop=True)
            elif kind == "v":
                if self.by_class:
                    mm = pe.matmul(bank, src[:, i * P:i * P + P], self.wv[:, :], start=True, stop=True)
                else:
                    for j in range(4):
                        mm = pe.matmul(bank[:, j * P:j * P + P], src[:, j::4], self.wv[:, j * P:j * P + P], start=True, stop=True)
            elif kind == "rq":
                for t in range(4):
                    pe.matmul(bank[:, t * REG:t * REG + REG], self.wq[:, t * P:t * P + P], self.yb[:, 0:REG], start=True, stop=False)
                    mm = pe.matmul(bank[:, t * REG:t * REG + REG], classes, negative, start=False, stop=True)
            elif kind == "rs":
                if par:
                    self.wait_taken(pe, ("rq", 0, 1), it)
                for t in range(4):
                    mm = pe.matmul(bank[0:self.QR, 0:L], self.qbd[:, t, :, :].rearrange("p h i -> p (h i)"), self.kp[:, par, t, :],
                                   start=(t == 0), stop=(t == 3))
            elif kind == "rt":
                self.wait_taken(pe, ("rs", 0, par), it)
                for kt in range(2):
                    mm = pe.transpose(bank[:, kt * self.QR:kt * self.QR + self.QR], self.rprobs[0:self.QR, kt * P:kt * P + P],
                                      ident[0:self.QR, 0:self.QR])
            elif kind == "rp":
                self.wait_taken(pe, ("rt", 0, par), it)
                for kt in range(2):
                    mm = pe.matmul(bank[0:self.QR, :], self.rpT[:, kt * self.QR:kt * self.QR + self.QR], self.v[:, par, kt * BANK:kt * BANK + BANK],
                                   start=(kt == 0), stop=(kt == 1))
            elif kind == "rm":
                self.wait_taken(pe, ("rp", 0, par), it)
                for t in range(4):
                    mm = pe.matmul(bank[:, t * REG:t * REG + REG], self.ratt[0:self.QR, t * P:t * P + P], cst[0:self.QR, C_SUM:C_SUM + REG],
                                   start=True, stop=True)
            elif kind == "t":
                pe.wait_ge(self.iv, it * 2 * QT + par * QT + i + 1)
                for t in range(4):
                    mm = pe.matmul(bank[:, t * P:t * P + P], self.inv[:, i, t * P:t * P + P], ident,
                                   start=True, stop=True)
            else:
                pe.wait_ge(self.nm, it * 2 * QT + par * QT + i + 1)
                if self.by_class and i == 0:
                    self.wait_taken(pe, ("rm", 0, par), it)
                for t in range(4):
                    mm = pe.matmul(bank[:, 0:P], self.attT[:, i, t, :], self.wo[:, t, :], start=(t == 0), stop=(t == 3))
            mm.then_inc(self.product, 1)

        def scores(n, it):
            par = n // self.steps
            if n == self.steps:
                self.wait_taken(pe, ("k", 1 if self.by_class else 3, 1), it)
                self.wait_taken(pe, ("q", 1, 1), it)
            if n >= 2:
                pe.wait_ge(self.ex, it * 2 * self.steps + n - 1)
            qt, g, quads = self.where(n)
            rows = slice(32 * g, 32 * g + self.ROWS)
            for j, t in enumerate(quads):
                keys = self.kp[rows, par, t, :] if self.by_class else self.kp[rows, par, t, g::4]
                mm = pe.matmul(PS[:, self.S[n % 2], j * self.width:j * self.width + self.width], self.qp[rows, par, t, qt * P:qt * P + P], keys,
                               start=True, stop=True)
            mm.then_inc(self.sc, 1)

        def turn(n, it):
            pe.wait_ge(self.ex, it * 2 * self.steps + n + 1)
            if n >= 2:
                pe.wait_ge(self.pt_a if n % 2 else self.pt_v, it * self.steps + n // 2)
            for j in range(BANK // P):
                mm = pe.transpose(PS[:, self.T[n % 2], j * P:j * P + P], self.probs[:, n % 2, j * P:j * P + P], ident)
            mm.then_inc(self.tr, 1)

        def times_v(n, it):
            par = n // self.steps
            if n == self.steps:
                self.wait_taken(pe, ("v", 1 if self.by_class else 0, 1), it)
            pe.wait_ge(self.pt_a if n % 2 else self.pt_v, it * self.steps + n // 2 + 1)
            qt, g, quads = self.where(n)
            for j, t in enumerate(quads):
                h = 4 * t + g
                for kt in range(self.kts):
                    at = kt * BANK + 32 * h if self.by_class else 32 * (4 * g + t)
                    mm = pe.matmul(PS[32 * g:32 * g + 32, self.O[qt], t * P:t * P + P], self.v[:, par, at:at + 32],
                                   self.pT[:, n % 2, (j * self.kts + kt) * P:(j * self.kts + kt) * P + P],
                                   start=(kt == 0), stop=(kt == self.kts - 1))
            mm.then_inc(self.av, 1)

        for u in self.first:
            product(u, 0, ahead=True)
        with pe.Fori(0, B // 2) as it:
            pe.wait_ge(self.by_v, it * len(self.v_uses) + self.first_v + 1)
            pe.wait_ge(self.by_a, it * len(self.a_uses) + self.first_a)
            for n in range(-2, 2 * self.steps + 1):
                if 0 <= n < 2 * self.steps:
                    turn(n, it)
                if n + 2 < 2 * self.steps:
                    scores(n + 2, it)
                if n >= 1:
                    times_v(n - 1, it)
                for u in self.at.get(n, []):
                    product(u, it)
            for u in self.last:
                product(u, it)

class Warping:

    LANES, E = S2 // 32, 32
    HAND = 2
    COLS = 32
    HALF = COLS // 2
    SLOTS = L + LANES * HAND
    ROUNDS = SLOTS // COLS
    ROW = 2 * (E + 1) + 2 * E + 1

    def __init__(self, k, norm):
        self.yT_in = 2 * (norm + 1)
        self.k = k
        E, SLOTS, COLS, LANES = self.E, self.SLOTS, self.COLS, self.LANES
        self.DL = k.lb("w_distances", [P, SLOTS + self.HALF, E])
        self.CUT = k.lb("w_up_table", [P, SLOTS, 66], BF16)
        self.MH = k.lb("w_path", [P, SLOTS, E], BF16)
        self.aa = k.lb("w_aa", [P, LANES])
        self.tick = k.lb("w_tick", [P, 1])
        self.bb = k.lb("w_bb", [P, L])
        self.parts = k.lb("w_context_parts", [P, 3, LANES, D], BF16)
        self.rest = k.lb("w_context_rest", [P, LANES, D])

        def phase(*buffers):
            with ExitStack() as place:
                return [place.enter_context(k.nc.sbuf_tensor("w_" + n, s, d)) for n, s, d in buffers]

        self.sq, self.d2, self.ones = phase(("squares", [P, 2048], F32), ("d2", [P, 2, 2, L], F32), ("ones", [P, 32], F32))
        self.DLr, self.Dr, self.R, self.Mn, self.An, self.Gr, self.Lr, self.Ur, self.Tr = phase(
            ("d_ring_in", [P, COLS, E], F32), ("d_ring", [P, COLS, E], F32), ("R", [P, COLS + 1, E + 1], F32), ("min", [P, E], F32),
            ("min2", [P, 2, E], F32), ("diag_over_up", [P, COLS, E], BF16), ("left", [P, COLS, E], BF16), ("up", [P, COLS, E], BF16),
            ("left_or_up", [P, COLS, E], BF16))
        self.CB, self.CTr, self.CUr = phase(("flags", [P, COLS, self.ROW], F32), ("table_ring", [P, COLS, E, 2], BF16),
                                            ("up_ring", [P, COLS, 2 * E], BF16))
        self.CT = self.DL[:, 0:SLOTS, :].bitcast(BF16).rearrange("p s (e k) -> p s e k", k=2)
        self.MT = self.DL[:, 0:SLOTS // 2, :].bitcast(BF16).rearrange("p s (h e) -> p (s h) e", h=2)
        s = k.sem
        self.zeroed, self.sq_done = s("w_zeroed"), s("w_squares_done")
        self.bb_ps, self.bb_sb = s("w_bb_product"), s("w_bb_ready")
        self.ab_ps, self.d2_done, self.dist_done, self.root_done = s("w_ab_product"), s("w_d2_done"), s("w_clamped"), s("w_root_done")
        self.dve = s("w_column_chain")
        self.dl_in, self.dl_used, self.choices, self.sums, self.tables = (
            s("w_d_ring_in"), s("w_d_ring_used"), s("w_choices"), s("w_left_or_up"), s("w_tables_saved"))
        self.fwd0, self.tab_in, self.half_done = s("w_path_started"), s("w_tables_in"), s("w_half_done")
        self.mt_done, self.split, self.ex_ps = s("w_mask_turned"), s("w_context_split"), s("w_expanded")

    def pool_before(self, pool):
        pool.memset(self.ones[:, :], 1.0).then_inc(self.zeroed, 1)
        n = self.LANES
        pool.memset(self.DL[:, 0:self.HAND * (n + 1), 0:n], 0.0).then_inc(self.zeroed, 1)
        pool.memset(self.DL[:, L + self.HAND:, 0:n], 0.0).then_inc(self.zeroed, 1)
        pool.wait_ge(self.zeroed, 2)
        pool.memset(self.DL[:, self.HAND - 1, 0:1], BIG).then_inc(self.zeroed, 1)
        pool.memset(self.DL[:, :, n:], 0.0)
        pool.memset(self.CUT[:, :, :], 1.0)

    def pool_forward(self, pool):
        with pool.Fori(0, self.ROUNDS) as it:
            for h in range(2):
                pool.wait_ge(self.choices, it * 2 + h + 1)
                r = slice(self.HALF * h, self.HALF * h + self.HALF)
                left, up, over = self.Lr[:, r, :], self.Ur[:, r, :], self.Gr[:, r, :]
                pool.tensor_tensor(up, over, left, ALU.mult).then_inc(self.sums, 1)
                pool.wait_ge(self.sums, it * 6 + 3 * h + 1)
                pool.tensor_tensor(up, over, up, ALU.subtract).then_inc(self.sums, 1)
                pool.wait_ge(self.sums, it * 6 + 3 * h + 2)
                pool.tensor_tensor(self.Tr[:, r, :], left, up, ALU.add).then_inc(self.sums, 1)

    def pool_split(self, pool):
        left = self.k.ctxP
        for i in range(3):
            pool.tensor_copy(self.parts[:, i, :, :], left[:, :, :]).then_inc(self.split, 1)
            if i < 2:
                pool.wait_ge(self.split, 2 * i + 1)
                pool.tensor_tensor(self.rest[:, :, :], left[:, :, :], self.parts[:, i, :, :], ALU.subtract).then_inc(self.split, 1)
                pool.wait_ge(self.split, 2 * i + 2)
                left = self.rest

    def tensor_distances(self, pe):
        PS, k, E = self.k.PS, self.k, self.E
        pe.wait_ge(self.sq_done, 1)
        pe.wait_ge(self.zeroed, 1)
        for b in range(B):
            mm = pe.matmul(PS[32 * b:32 * b + 32, 7, 0:L], self.ones[:, :], self.sq[:, b * L:b * L + L], start=True, stop=True)
        mm.then_inc(self.bb_ps, 1)
        for h in range(self.LANES // 2):
            if h >= 2:
                pe.wait_ge(self.d2_done, h - 1)
            for p in (2 * h, 2 * h + 1):
                for b in range(B):
                    mm = pe.matmul(PS[32 * b:32 * b + 32, h % 2, (p % 2) * L:(p % 2) * L + L],
                                   k.ctxT[:, b, E * p:E * p + E], k.yT[:, b * L:b * L + L], start=True, stop=True)
            mm.then_inc(self.ab_ps, 1)

    def tensor_expand(self, pe):
        PS = self.k.PS
        pe.wait_ge(self.split, 5)
        for jt in range(QT):
            for p in range(self.LANES):
                first = self.HAND * (p + 1) + jt * P
                pe.wait_ge(self.mt_done, (first + P - 1) // (self.SLOTS // 4) + 1)
                for b in range(B):
                    for i in range(3):
                        mm = pe.matmul(PS[:, b, jt * D:jt * D + D], self.MT[32 * b:32 * b + 32, first:first + P, p],
                                       self.parts[32 * b:32 * b + 32, i, p, :], start=(p == 0 and i == 0),
                                       stop=(p == self.LANES - 1 and i == 2))
        mm.then_inc(self.ex_ps, 1)

    def scalar_distances(self, act):
        act.wait_ge(self.k.ln.s_yT, self.yT_in)
        act.activation(self.sq[:, 0:B * L], self.k.yT[:, :], ACT.Square).then_inc(self.sq_done, 1)
        act.wait_ge(self.zeroed, 4)
        for h in range(self.LANES // 2):
            for p in (2 * h, 2 * h + 1):
                act.wait_ge(self.dist_done, p + 1)
                act.activation(self.DL[:, self.HAND * (p + 1):self.HAND * (p + 1) + L, p], self.d2[:, h % 2, p % 2, :],
                               ACT.Sqrt).then_inc(self.root_done, 1)

    def scalar_forward(self, act):
        HALF, COLS = self.HALF, self.COLS

        def bring(it):
            act.wait_ge(self.dl_used, it * 2 + 1)
            act.copy(self.DLr[:, HALF:COLS, :], self.DL[:, ds(it * COLS + HALF, HALF), :]).then_inc(self.dl_in, 1)
            act.copy(self.DLr[:, 0:HALF, :], self.DL[:, ds(it * COLS + COLS, HALF), :]).then_inc(self.dl_in, 1)

        def save(n, r):
            act.wait_ge(self.sums, 3 * n + 3)
            slots = ds(n * HALF, HALF)
            act.activation(self.CT[:, slots, :, 0], self.Tr[:, r, :], ACT.Copy, bias=1.0, scale=-1.0)
            act.activation(self.CT[:, slots, :, 1], self.Lr[:, r, :], ACT.Copy)
            act.activation(self.CUT[:, slots, 1:65:2], self.Ur[:, r, :], ACT.Copy).then_inc(self.tables, 1)

        first, second = slice(0, HALF), slice(HALF, COLS)
        act.copy(self.DLr[:, first, :], self.DL[:, 0:HALF, :]).then_inc(self.dl_in, 1)
        bring(0)
        save(0, first)
        with act.Fori(1, self.ROUNDS) as it:
            bring(it)
            save(it * 2 - 1, second)
            save(it * 2, first)
        save(2 * self.ROUNDS - 1, second)

    def scalar_backward(self, act):
        HALF, COLS, SLOTS = self.HALF, self.COLS, self.SLOTS
        act.wait_ge(self.fwd0, 1)

        def load_tables(slot, half):
            r = slice(HALF * half, HALF * half + HALF)
            act.copy(self.CTr[:, r, :, :], self.CT[:, ds(slot, HALF), :, :])
            act.copy(self.CUr[:, r, :], self.CUT[:, ds(slot, HALF), 2:66]).then_inc(self.tab_in, 1)

        def backward_round(it, last):
            for half in (1, 0):
                slot = SLOTS - COLS + HALF * half - it * COLS
                act.wait_ge(self.half_done, it * 2 + 2 - half)
                act.copy(self.MH[:, ds(slot, HALF), :], self.CB[:, HALF * half:HALF * half + HALF, 66:130:2])
                if not last:
                    load_tables(slot - COLS, half)

        load_tables(SLOTS - HALF, 1)
        load_tables(SLOTS - COLS, 0)
        with act.Fori(0, self.ROUNDS - 1) as it:
            backward_round(it, False)
        backward_round(self.ROUNDS - 1, True)

    def vector_distances(self, v):
        PS, k, ctxP = self.k.PS, self.k, self.k.ctxP[:, :, :].rearrange("p a d -> p (a d)")
        v.wait_ge(self.bb_ps, 1)
        v.tensor_copy(self.bb[:, :], PS[:, 7, 0:L]).then_inc(self.bb_sb, 1)
        v.wait_ge(self.bb_sb, 1)
        v.tensor_tensor(self.sq[:, :], ctxP, ctxP, ALU.mult).then_inc(self.bb_sb, 1)
        v.wait_ge(self.bb_sb, 2)
        v.tensor_reduce(self.aa[:, :], self.sq[:, :].rearrange("p (a d) -> p a d", d=D), AX.X, ALU.add).then_inc(self.bb_sb, 1)
        v.wait_ge(self.bb_sb, 3)
        for h in range(self.LANES // 2):
            v.wait_ge(self.ab_ps, h + 1)
            if h >= 2:
                v.wait_ge(self.root_done, 2 * h - 2)
            v.scalar_tensor_tensor(self.d2[:, h % 2, :, :], PS[:, h % 2, :].rearrange("p (a l) -> p a l", a=2), -2.0,
                                   self.bb[:, :].unsqueeze(1).to_broadcast((P, 2, L)), ALU.mult, ALU.add).then_inc(self.d2_done, 1)
            v.wait_ge(self.d2_done, h + 1)
            for p in (2 * h, 2 * h + 1):
                v.tensor_scalar(self.d2[:, h % 2, p % 2, :], self.d2[:, h % 2, p % 2, :], self.aa[:, p:p + 1], 0.0,
                                ALU.add, ALU.max).then_inc(self.dist_done, 1)

    def vector_forward(self, v):
        E, COLS, HALF, HAND, LANES, R = self.E, self.COLS, self.HALF, self.HAND, self.LANES, self.R
        Lr, An, Gr, Mn, dve = self.Lr, self.An, self.Gr, self.Mn, self.dve
        v.memset(R[:, :, :], BIG).then_inc(dve, 1)
        v.memset(Lr[:, :, :], 0.0).then_inc(self.tables, 2)
        v.wait_ge(self.dl_in, 1)

        def to_lanes(half):
            r = slice(HALF * half, HALF * half + HALF)
            v.transpose(self.Dr[:, r, :].rearrange("p c e -> p (c e)"), self.DLr[:, r, :].rearrange("p c e -> p (c e)")).then_inc(self.dl_used, 1)

        to_lanes(0)
        v.wait_ge(dve, 1)
        v.tensor_copy(R[:, HAND, 0:1], self.k.cst[:, C_HALO:C_HALO + 1]).then_inc(dve, 1)
        v.wait_ge(dve, 2)
        v.sem_clear(dve)
        above = [31] + list(range(LANES - 1)) + [31] * (32 - LANES)
        with v.Fori(0, self.ROUNDS) as it:
            k = 0
            chain = 0
            pair = None

            def choice(c, q):
                nonlocal k
                diag, left, up = R[:, c:c + 2, 0:E], R[:, c:c + 2, 1:E + 1], R[:, c + 1:c + 3, 0:E]
                if q == 0:
                    v.tensor_tensor(An[:, :, :], diag, up, ALU.min).then_inc(dve, 1)
                elif q == 1:
                    if c % HALF == 0:
                        v.wait_ge(self.tables, it * 2 + 1 + c // HALF)
                    v.tensor_tensor(Gr[:, c:c + 2, :], diag, up, ALU.is_gt).then_inc(dve, 1)
                else:
                    done = self.choices if c % HALF == HALF - 2 else dve
                    v.tensor_tensor(Lr[:, c:c + 2, :], An[:, :, :], left, ALU.is_gt).then_inc(done, 1)
                    if done is self.choices:
                        return
                k += 1

            for c in range(COLS):
                if chain:
                    v.wait_ge(dve, chain)
                v.tensor_tensor(Mn[:, :], R[:, c, 0:E], R[:, c, 1:E + 1], ALU.min).then_inc(dve, 1)
                k += 1
                chain = k
                if pair is not None:
                    choice(pair, 0 if c % 2 == 0 else 2)
                if c == 0:
                    v.wait_ge(self.dl_in, it * 2 + 2)
                    to_lanes(1)
                    v.wait_ge(self.dl_used, it * 2 + 1)
                if c == HALF:
                    v.wait_ge(self.dl_in, it * 2 + 3)
                    to_lanes(0)
                    v.wait_ge(self.dl_used, it * 2 + 2)
                v.wait_ge(dve, chain)
                v.tensor_tensor_scan(R[:, c + 1, 1:E + 1], Mn[:, :], self.Dr[:, c, :], R[:, c + 1, 0:1], ALU.min, ALU.add).then_inc(dve, 1)
                k += 1
                chain = k
                if pair is not None and c % 2 == 0:
                    choice(pair, 1)
                if c % 2 == 1:
                    pair = c - 1
                if c % HAND == HAND - 1:
                    n = (c + 1) % COLS + 1
                    v.wait_ge(dve, chain)
                    v.stream_shuffle(R[:, n:n + HAND, 0], R[:, c + 2 - HAND:c + 2, E], mask=above).then_inc(dve, 1)
                    k += 1
            for q in range(3):
                v.wait_ge(dve, k)
                choice(COLS - 2, q)
            v.tensor_copy(R[:, 0, :], R[:, COLS, :]).then_inc(dve, 1)
            k += 1
            v.wait_ge(dve, k)
            v.sem_clear(dve)

    def vector_backward(self, v):
        E, COLS, HALF, HAND, LANES, ROW, CB, dve = self.E, self.COLS, self.HALF, self.HAND, self.LANES, self.ROW, self.CB, self.dve
        below = list(range(1, LANES)) + [31] * (32 - LANES + 1)
        v.memset(CB[:, :, :], 0.0).then_inc(dve, 1)
        v.stream_shuffle(self.CUT[:, 0:self.SLOTS - HAND, 65], self.CUT[:, HAND:self.SLOTS, 1], mask=below).then_inc(dve, 1)
        v.wait_ge(dve, 2)
        v.tensor_copy(CB[:, COLS - 1, 65:66], self.k.cst[:, C_START:C_START + 1]).then_inc(self.fwd0, 1)
        v.wait_ge(self.fwd0, 1)
        v.sem_clear(dve)
        with v.Fori(0, self.ROUNDS) as it:
            k = 0
            for c in reversed(range(COLS)):
                if c % HALF == HALF - 1:
                    v.wait_ge(self.tab_in, it * 2 + (1 if c > HALF else 2))
                if k:
                    v.wait_ge(dve, k)
                v.tensor_tensor_scan(CB[:, c, 129:65:-1], self.CUr[:, c, 63::-1], CB[:, c, 65:1:-1], CB[:, c, 130:131],
                                     ALU.mult, ALU.add).then_inc(dve, 1)
                k += 1
                v.wait_ge(dve, k)
                if c % HAND == 0:
                    n = (c - HAND) % COLS
                    v.stream_shuffle(CB[:, n:n + HAND, 64:131:66], CB[:, c:c + HAND, 0:67:66], mask=below).then_inc(dve, 1)
                    k += 1
                sent = bass.AP(tensor=CB, offset=((c - 1) % COLS) * ROW, ap=[[COLS * ROW, P], [2, E], [3, 2]])
                v.tensor_tensor(sent, CB[:, c, 66:130:2].unsqueeze(2).to_broadcast((P, E, 2)), self.CTr[:, c, :, :],
                                ALU.mult).then_inc(self.half_done if c == HALF else dve, 1)
                if c == HALF:
                    v.wait_ge(self.half_done, it * 2 + 1)
                else:
                    k += 1
            v.wait_ge(dve, k)
            v.sem_clear(dve)
            v.memset(self.tick[:, :], 0.0).then_inc(self.half_done, 1)

    def vector_expand(self, v):
        n = self.SLOTS // 4 * self.E
        MT, MH = (a[:, :, :].rearrange("p s e -> p (s e)") for a in (self.MT, self.MH))
        for q in range(4):
            v.transpose(MT[:, q * n:q * n + n], MH[:, q * n:q * n + n]).then_inc(self.mt_done, 1)
        v.wait_ge(self.ex_ps, 1)
        x = self.k.x
        for b in range(B):
            v.tensor_tensor(x[:, 2 * b:2 * b + 2, :], x[:, 2 * b:2 * b + 2, :], self.k.PS[:, b, 0:L].rearrange("p (t d) -> p t d", t=QT), ALU.add)

class SpikingMoE:

    NE, M, H = 8, 64, 256

    def __init__(self, k, norm):
        self.norm = norm
        self.k = k
        NE, M, H = self.NE, self.M, self.H
        self.enc_w, self.enc_b = k.sb("moe_enc_w", [P, H]), k.sb("moe_enc_b", [P, 2])
        self.s2c_w, self.s2c_b = k.sb("moe_s2c_w", [P, 2, M]), k.sb("moe_s2c_b", [M, 1])
        self.r1_w, self.r1_b = k.sb("moe_router1_w", [M, 64]), k.sb("moe_router1_b", [64, 1])
        self.r2_w, self.r2_b = k.sb("moe_router2_w", [64, NE]), k.sb("moe_router2_b", [P, NE])
        self.e1_w, self.e1_b = k.sb("moe_e1_w", [M, NE, P]), k.sb("moe_e1_b", [P, NE])
        self.e2_w, self.e2_b = k.sb("moe_e2_w", [P, NE, M]), k.sb("moe_e2_b", [NE, M])
        self.c2s_w, self.c2s_b = k.sb("moe_c2s_w", [M, H]), k.sb("moe_c2s_b", [P, 2])
        self.dec_w, self.dec_b = k.sb("moe_dec_w", [P, 2, D]), k.sb("moe_dec_b", [1, D])
        self.ln_g, self.ln_b = k.sb("moe_ln_g", [P, D]), k.sb("moe_ln_b", [P, D])
        s = k.sem
        self.loaded = s("moe_loaded")
        self.product = s("moe_product")
        self.by_v, self.by_a = s("moe_vector"), s("moe_scalar")
        self.ones_set = s("moe_ones_set")
        self.P_ENC, self.P_CONT, self.P_R1, self.P_R2 = 0, 4, 6, 8
        self.P_E1 = self.P_R2 + 1
        self.P_GT = self.P_E1 + 16
        self.P_B2 = self.P_GT + 1
        self.P_E2 = self.P_B2 + 1
        self.P_OFT = self.P_E2 + TILES
        self.P_C2S = self.P_OFT + 2
        self.P_DEC = self.P_C2S + 4

    def place(self):
        k, NE, M = self.k, self.NE, self.M
        self.ones = k.lb("moe_ones", [1, P])
        self.encT = k.lb("moe_encT", [P, 2, B * L])
        self.contT = k.lb("moe_contT", [M, B * L])
        self.tanhT = k.lb("moe_tanhT", [64, B * L])
        self.p = k.lb("moe_p", [P, TILES, NE])
        self.row = k.lb("moe_row", [P, TILES])
        self.top = k.lb("moe_top", [P, TILES, 8])
        self.at = k.lb("moe_top_at", [P, TILES, 8], U32)
        self.atf = k.lb("moe_top_at_float", [P, TILES, 2])
        self.w = k.lb("moe_w", [P, TILES, 2])
        self.gates = k.lb("moe_gates", [P, 2, TILES, NE])
        self.gT = k.lb("moe_gatesT", [NE, B * L])
        self.hT = k.lb("moe_hT", [P, NE, B * L])
        self.gated = k.lb("moe_gated", [P, 2, NE, M])
        self.of = k.lb("moe_of", [P, TILES, M])
        self.ofT = k.lb("moe_ofT", [M, B * L])
        self.spT = k.lb("moe_spT", [P, 2, B * L])

    def load(self, q, enc_W, enc_b, s2c_W, s2c_b, rW1, rb1, rW2, rb2, We1, be1, We2, be2, c2s_W, c2s_b, dec_W, dec_b, ln_g, ln_b):
        halves = lambda b: b.rearrange("(c p) -> p c", p=P)
        pairs = [(self.enc_w[:, :], enc_W), (self.enc_b[:, :], halves(enc_b)), (self.s2c_w[:, :, :], s2c_W.rearrange("(c p) m -> p c m", p=P)),
                 (self.s2c_b[:, :], s2c_b.unsqueeze(1)), (self.r1_w[:, :], rW1), (self.r1_b[:, :], rb1.unsqueeze(1)), (self.r2_w[:, :], rW2),
                 (self.r2_b[:, :], rb2.unsqueeze(0).to_broadcast((P, self.NE))), (self.e1_w[:, :, :], We1.rearrange("e m h -> m e h")),
                 (self.e1_b[:, :], be1.rearrange("e h -> h e")), (self.e2_w[:, :, :], We2.rearrange("e h m -> h e m")),
                 (self.e2_b[:, :], be2), (self.c2s_w[:, :], c2s_W), (self.c2s_b[:, :], halves(c2s_b)),
                 (self.dec_w[:, :, :], dec_W.rearrange("(c p) d -> p c d", p=P)), (self.dec_b[:, :], dec_b.unsqueeze(0)),
                 (self.ln_g[:, :], ln_g.unsqueeze(0).to_broadcast((P, D))), (self.ln_b[:, :], ln_b.unsqueeze(0).to_broadcast((P, D)))]
        for dst, src in pairs:
            q.dma_start(dst, src).then_inc(self.loaded, 16)
        self.n_loads = 16 * len(pairs)

    def pool_ones(self, pool):
        pool.memset(self.ones[:, :], 1.0).then_inc(self.ones_set, 1)

    def tensor(self, pe):
        PS, k, NE, M = self.k.PS, self.k, self.NE, self.M
        pe.wait_ge(self.loaded, self.n_loads)
        for f in range(2):
            pe.wait_ge(k.ln.s_yT, 2 * self.norm + f + 1)
            for c in range(2):
                pe.matmul(PS[:, 2 * f + c, :], self.enc_w[:, c * P:c * P + P], k.yT[:, f * BANK:f * BANK + BANK],
                          start=True, stop=True).then_inc(self.product, 1)
        for f in range(2):
            pe.wait_ge(self.by_a, 2 * f + 2)
            for c in range(2):
                mm = pe.matmul(PS[0:M, 4 + f, :], self.s2c_w[:, c, :], self.encT[:, c, f * BANK:f * BANK + BANK], start=(c == 0), stop=(c == 1))
            mm.then_inc(self.product, 1)
        for f in range(2):
            pe.wait_ge(self.by_v, f + 1)
            pe.matmul(PS[0:64, 6 + f, :], self.r1_w[:, :], self.contT[:, f * BANK:f * BANK + BANK], start=True, stop=True).then_inc(self.product, 1)
        pe.wait_ge(self.by_a, 6)
        for t in range(TILES):
            mm = pe.matmul(PS[:, 0, t * NE:t * NE + NE], self.tanhT[:, t * P:t * P + P], self.r2_w[:, :], start=True, stop=True)
        mm.then_inc(self.product, 1)
        for i in range(16):
            e, f = i // 2, i % 2
            if i >= 4:
                if f:
                    pe.wait_ge(self.by_v, self.V_E1 + (i - 4) // 2 + 1)
                else:
                    pe.wait_ge(self.by_a, 7 + (i - 4) // 2 + 1)
            pe.matmul(PS[:, 1 + i % 4, :], self.e1_w[:, e, :], self.contT[:, f * BANK:f * BANK + BANK], start=True, stop=True).then_inc(self.product, 1)
        for t in range(TILES):
            mm = pe.transpose(PS[0:NE, 6 + t // 4, (t % 4) * P:(t % 4) * P + P], self.gates[:, 0, t, :], k.ident)
        mm.then_inc(self.product, 1)
        pe.wait_ge(self.by_a, 16)
        for t in range(TILES):
            mm = pe.matmul(PS[:, 7, t * M:t * M + M], self.gT[:, t * P:t * P + P], self.e2_b[:, :], start=True, stop=True)
        mm.then_inc(self.product, 1)
        pe.wait_ge(self.by_v, self.V_E1 + 8)
        pe.wait_ge(self.ones_set, 1)
        for t in range(TILES):
            if t >= 2:
                pe.wait_ge(self.by_v, self.V_E2 + 2 * (t - 2) + (t - 2) // 4 + 1)
            bank = PS[:, 5 + t % 2, :]
            for e in range(NE):
                mm = pe.matmul(bank[:, e * M:e * M + M], self.hT[:, e, t * P:t * P + P], self.e2_w[:, e, :], start=True, stop=True)
            mm.then_inc(self.product, 1)
        for f in range(2):
            pe.wait_ge(self.by_v, self.V_E2 + 9 * (f + 1))
            for t in range(4 * f, 4 * f + 4):
                mm = pe.transpose(PS[0:M, 1 + f, (t % 4) * P:(t % 4) * P + P], self.of[:, t, :], k.ident)
            mm.then_inc(self.product, 1)
        for f in range(2):
            pe.wait_ge(self.by_v, self.V_OFT + f + 1)
            for c in range(2):
                pe.matmul(PS[:, (3, 4, 5, 6)[2 * f + c], :], self.c2s_w[:, c * P:c * P + P], self.ofT[:, f * BANK:f * BANK + BANK],
                          start=True, stop=True).then_inc(self.product, 1)
        for f in range(2):
            pe.wait_ge(self.by_a, 16 + 2 * f + 2)
            for t in range(4 * f, 4 * f + 4):
                out = PS[:, (7, 0)[f], (t % 4) * P:(t % 4) * P + P]
                pe.matmul(out, self.ones[:, :], self.dec_b[:, :], start=True, stop=False)
                for c in range(2):
                    mm = pe.matmul(out, self.spT[:, c, t * P:t * P + P], self.dec_w[:, c, :], start=False, stop=(c == 1))
            mm.then_inc(self.product, 1)

    V_E1 = 2 + 15 + 2 * TILES
    V_E2 = V_E1 + 8
    V_OFT = V_E2 + 2 * TILES + 2

    def scalar(self, act):
        PS, k = self.k.PS, self.k
        halves = lambda f: slice(f * BANK, f * BANK + BANK)
        act.wait_ge(self.loaded, self.n_loads)
        for f in range(2):
            for c in range(2):
                act.wait_ge(self.product, 2 * f + c + 1)
                act.activation(self.encT[:, c, halves(f)], PS[:, 2 * f + c, :], ACT.Sigmoid, bias=self.enc_b[:, c:c + 1]).then_inc(self.by_a, 1)
        for f in range(2):
            act.wait_ge(self.product, self.P_R1 + f + 1)
            act.activation(self.tanhT[:, halves(f)], PS[0:64, 6 + f, :], ACT.Tanh, bias=self.r1_b[:, 0:1]).then_inc(self.by_a, 1)
        act.wait_ge(self.by_v, 5)
        act.activation(self.p[:, :, :], self.p[:, :, :], ACT.Exp).then_inc(self.by_a, 1)
        for i in range(0, 16, 2):
            act.wait_ge(self.product, self.P_E1 + i + 1)
            act.activation(self.hT[:, i // 2, halves(0)], PS[:, 1 + i % 4, :], ACT.Relu, bias=self.e1_b[:, i // 2:i // 2 + 1]).then_inc(self.by_a, 1)
        act.wait_ge(self.product, self.P_GT + 1)
        act.copy(self.gT[:, :].rearrange("p (f c) -> p f c", f=2), PS[0:self.NE, 6:8, :]).then_inc(self.by_a, 1)
        for f in range(2):
            for c in range(2):
                act.wait_ge(self.product, self.P_C2S + 2 * f + c + 1)
                act.activation(self.spT[:, c, halves(f)], PS[:, (3, 4, 5, 6)[2 * f + c], :], ACT.Sigmoid, bias=self.c2s_b[:, c:c + 1]).then_inc(self.by_a, 1)
        for f in range(2):
            act.wait_ge(self.product, self.P_DEC + f + 1)
            act.activation(k.y[:, 4 * f:4 * f + 4, :], PS[:, (7, 0)[f], :].rearrange("p (t d) -> p t d", t=4), ACT.Sigmoid).then_inc(self.by_a, 1)

    def vector(self, v):
        PS, NE, M = self.k.PS, self.NE, self.M
        n = 0

        def done(ins):
            nonlocal n
            ins.then_inc(self.by_v, 1)
            n += 1

        def own():
            v.wait_ge(self.by_v, n)

        v.wait_ge(self.loaded, self.n_loads)
        for f in range(2):
            v.wait_ge(self.product, self.P_CONT + f + 1)
            done(v.tensor_scalar(self.contT[:, f * BANK:f * BANK + BANK], PS[0:M, 4 + f, :], self.s2c_b[:, 0:1], None, ALU.add))
        by_e = lambda a: a.unsqueeze(2).to_broadcast((P, TILES, NE))
        v.wait_ge(self.product, self.P_R2 + 1)
        done(v.tensor_tensor(self.p[:, :, :], PS[:, 0, 0:TILES * NE].rearrange("p (t e) -> p t e", e=NE),
                             self.r2_b[:, :].unsqueeze(1).to_broadcast((P, TILES, NE)), ALU.add))
        own()
        done(v.tensor_reduce(self.row[:, :], self.p[:, :, :], AX.X, ALU.max, negate=True))
        own()
        done(v.tensor_tensor(self.p[:, :, :], self.p[:, :, :], by_e(self.row[:, :]), ALU.add))
        v.wait_ge(self.by_a, 7)
        done(v.tensor_reduce(self.row[:, :], self.p[:, :, :], AX.X, ALU.add))
        own()
        done(v.reciprocal(self.row[:, :], self.row[:, :]))
        own()
        done(v.tensor_tensor(self.p[:, :, :], self.p[:, :, :], by_e(self.row[:, :]), ALU.mult))
        own()
        for t in range(TILES):
            done(v.max(self.top[:, t, :], self.p[:, t, :]))
        own()
        for t in range(TILES):
            done(v.max_index(self.at[:, t, :], self.top[:, t, :], self.p[:, t, :]))
        own()
        done(v.tensor_copy(self.atf[:, :, :], self.at[:, :, 0:2]))
        done(v.tensor_tensor(self.row[:, :], self.top[:, :, 0], self.top[:, :, 1], ALU.add))
        own()
        done(v.reciprocal(self.row[:, :], self.row[:, :]))
        own()
        done(v.tensor_tensor(self.w[:, :, :], self.top[:, :, 0:2], self.row[:, :].unsqueeze(2).to_broadcast((P, TILES, 2)), ALU.mult))
        own()
        for i in range(2):
            done(v.tensor_tensor(self.gates[:, i, :, :], self.k.cst[:, C_IOTA:C_IOTA + NE].unsqueeze(1).to_broadcast((P, TILES, NE)),
                                 by_e(self.atf[:, :, i]), ALU.is_equal))
        own()
        for i in range(2):
            done(v.tensor_tensor(self.gates[:, i, :, :], self.gates[:, i, :, :], by_e(self.w[:, :, i]), ALU.mult))
        own()
        done(v.tensor_tensor(self.gates[:, 0, :, :], self.gates[:, 0, :, :], self.gates[:, 1, :, :], ALU.add))
        own()
        assert n == self.V_E1
        for i in range(1, 16, 2):
            v.wait_ge(self.product, self.P_E1 + i + 1)
            done(v.tensor_scalar(self.hT[:, i // 2, BANK:2 * BANK], PS[:, 1 + i % 4, :], self.e1_b[:, i // 2:i // 2 + 1], 0.0, ALU.add, ALU.max))
        assert n == self.V_E2
        for t in range(TILES):
            v.wait_ge(self.product, self.P_E2 + t + 1)
            done(v.tensor_tensor(self.gated[:, t % 2, :, :], PS[:, 5 + t % 2, :].rearrange("p (e m) -> p e m", e=NE),
                                 self.gates[:, 0, t, :].unsqueeze(2).to_broadcast((P, NE, M)), ALU.mult))
            own()
            done(v.tensor_reduce(self.of[:, t, :], self.gated[:, t % 2, :, :].rearrange("p e m -> p m e"), AX.X, ALU.add))
            if t % 4 == 3:
                own()
                half = self.of[:, t - 3:t + 1, :]
                done(v.tensor_tensor(half, half, PS[:, 7, (t - 3) * M:(t + 1) * M].rearrange("p (t m) -> p t m", t=4), ALU.add))
        for f in range(2):
            v.wait_ge(self.product, self.P_OFT + f + 1)
            done(v.tensor_copy(self.ofT[:, f * BANK:f * BANK + BANK], PS[0:M, 1 + f, :]))

    def vector_add(self, v):
        k = self.k
        tiles = lambda a: a[:, :].unsqueeze(1).to_broadcast((P, TILES, D))
        first = self.V_OFT + 2
        v.wait_ge(k.ln.s_y, TILES * (self.norm + 2))
        v.tensor_tensor(k.y[:, :, :], k.y[:, :, :], tiles(self.ln_g), ALU.mult).then_inc(self.by_v, 1)
        v.wait_ge(self.by_v, first + 1)
        v.tensor_tensor(k.y[:, :, :], k.y[:, :, :], tiles(self.ln_b), ALU.add).then_inc(self.by_v, 1)
        v.wait_ge(self.by_v, first + 2)
        v.tensor_tensor(k.x[:, :, :], k.x[:, :, :], k.y[:, :, :], ALU.add)

class TopOneMoE:

    NE = 8

    def __init__(self, k, norm):
        self.yT_in = 2 * (norm + 1)
        self.k = k
        NE = self.NE
        self.wg, self.bg = k.sb("top_wg", [P, NE]), k.sb("top_bg", [P, NE])
        self.w1, self.b1 = k.sb("top_w1", [P, NE, P]), k.sb("top_b1", [P, NE])
        self.w2, self.b2 = k.sb("top_w2", [P, NE, D]), k.sb("top_b2", [NE, D])
        s = k.sem
        self.loaded = s("top_loaded")
        self.product = s("top_product")
        self.by_v, self.by_a = s("top_vector"), s("top_scalar")

    def place(self):
        k, NE = self.k, self.NE
        self.p = k.lb("top_p", [P, TILES, NE])
        self.row = k.lb("top_row", [P, TILES])
        self.top = k.lb("top_top", [P, TILES, 8])
        self.at = k.lb("top_at", [P, TILES, 8], U32)
        self.atf = k.lb("top_at_float", [P, TILES])
        self.oh = k.lb("top_one_hot", [P, TILES, NE])
        self.ohT = k.lb("top_one_hotT", [NE, B * L])
        self.ohb = k.lb("top_one_hot_bf16", [NE, B * L], BF16)
        self.h = k.lb("top_h", [P, NE, B * L])

    def load(self, q, Wg, bg, W1, b1, W2, b2):
        pairs = [(self.wg[:, :], Wg), (self.bg[:, :], bg.unsqueeze(0).to_broadcast((P, self.NE))), (self.w1[:, :, :], W1.rearrange("e h i -> h e i")),
                 (self.b1[:, :], b1.rearrange("e i -> i e")), (self.w2[:, :, :], W2.rearrange("e i h -> i e h")), (self.b2[:, :], b2)]
        for dst, src in pairs:
            q.dma_start(dst, src).then_inc(self.loaded, 16)
        self.n_loads = 16 * len(pairs)

    V_OH = 6 + 2 * TILES + 2
    STEPS = 16
    P_OH = 10

    def p_hidden(self, i):
        return 2 + i if i < 8 else 3 + i

    def p_spread(self, i):
        return 19 + i

    def p_out(self, f):
        return 35 + f

    def tensor(self, pe):
        PS, k, NE = self.k.PS, self.k, self.NE
        pe.wait_ge(self.loaded, self.n_loads)
        pe.wait_ge(k.ln.s_yT, self.yT_in)
        for t in range(TILES):
            mm = pe.matmul(PS[:, 0, t * NE:t * NE + NE], k.yT[:, t * P:t * P + P], self.wg[:, :], start=True, stop=True)
        mm.then_inc(self.product, 1)
        half = lambda f: slice(f * BANK, f * BANK + BANK)

        def output(t):
            out = PS[:, 4 + t // 4, (t % 4) * P:(t % 4) * P + P]
            pe.matmul(out, self.ohT[:, t * P:t * P + P], self.b2[:, :], start=True, stop=False)
            for e in range(NE):
                mm = pe.matmul(out, self.h[:, e, t * P:t * P + P], self.w2[:, e, :], start=False, stop=(e == NE - 1))
            if t % 4 == 3:
                mm.then_inc(self.product, 1)

        for i in range(self.STEPS):
            if i == 8:
                pe.wait_ge(self.by_v, self.V_OH)
                for t in range(TILES):
                    mm = pe.transpose(PS[0:NE, 1 + t // 4, (t % 4) * P:(t % 4) * P + P], self.oh[:, t, :], k.ident)
                mm.then_inc(self.product, 1)
            if i >= 2:
                pe.wait_ge(self.by_a, i)
            pe.matmul(PS[:, (3, 6)[i % 2], :], self.w1[:, i % 8, :], k.yT[:, half(i // 8)], start=True, stop=True).then_inc(self.product, 1)
        pe.wait_ge(self.by_v, self.V_OH + 2)
        for i in range(self.STEPS):
            if i >= 2:
                pe.wait_ge(self.by_v, self.V_OH + 2 + i - 1)
            pe.matmul(PS[:, 1 + i % 2, :], k.identb[0:NE, i % 8:i % 8 + 1].to_broadcast((NE, P)), self.ohb[:, half(i // 8)],
                      start=True, stop=True).then_inc(self.product, 1)
            if i >= 8 and i % 2 == 1:
                if i == 9:
                    pe.wait_ge(self.by_v, self.V_OH + 2 + 8)
                output((i - 9) // 2)
        pe.wait_ge(self.by_v, self.V_OH + 2 + self.STEPS)
        for t in range(4, TILES):
            output(t)

    def scalar(self, act):
        PS = self.k.PS
        act.wait_ge(self.loaded, self.n_loads)
        act.wait_ge(self.by_v, 3)
        act.activation(self.p[:, :, :], self.p[:, :, :], ACT.Exp).then_inc(self.by_a, 1)
        for i in range(self.STEPS):
            act.wait_ge(self.product, self.p_hidden(i))
            act.activation(self.h[:, i % 8, (i // 8) * BANK:(i // 8) * BANK + BANK], PS[:, (3, 6)[i % 2], :], ACT.Gelu,
                           bias=self.b1[:, i % 8:i % 8 + 1]).then_inc(self.by_a, 1)

    def vector(self, v):
        PS, NE = self.k.PS, self.NE
        n = 0

        def done(ins):
            nonlocal n
            ins.then_inc(self.by_v, 1)
            n += 1

        def own():
            v.wait_ge(self.by_v, n)

        by_e = lambda a: a.unsqueeze(2).to_broadcast((P, TILES, NE))
        v.wait_ge(self.loaded, self.n_loads)
        v.wait_ge(self.product, 1)
        done(v.tensor_tensor(self.p[:, :, :], PS[:, 0, 0:TILES * NE].rearrange("p (t e) -> p t e", e=NE),
                             self.bg[:, :].unsqueeze(1).to_broadcast((P, TILES, NE)), ALU.add))
        own()
        done(v.tensor_reduce(self.row[:, :], self.p[:, :, :], AX.X, ALU.max, negate=True))
        own()
        done(v.tensor_tensor(self.p[:, :, :], self.p[:, :, :], by_e(self.row[:, :]), ALU.add))
        v.wait_ge(self.by_a, 1)
        done(v.tensor_reduce(self.row[:, :], self.p[:, :, :], AX.X, ALU.add))
        own()
        done(v.reciprocal(self.row[:, :], self.row[:, :]))
        own()
        done(v.tensor_tensor(self.p[:, :, :], self.p[:, :, :], by_e(self.row[:, :]), ALU.mult))
        own()
        for t in range(TILES):
            done(v.max(self.top[:, t, :], self.p[:, t, :]))
        own()
        for t in range(TILES):
            done(v.max_index(self.at[:, t, :], self.top[:, t, :], self.p[:, t, :]))
        own()
        done(v.tensor_copy(self.atf[:, :], self.at[:, :, 0]))
        own()
        done(v.tensor_tensor(self.oh[:, :, :], self.k.cst[:, C_IOTA:C_IOTA + NE].unsqueeze(1).to_broadcast((P, TILES, NE)), by_e(self.atf[:, :]),
                             ALU.is_equal))
        assert n == self.V_OH
        v.wait_ge(self.product, self.P_OH)
        for dst in (self.ohT, self.ohb):
            done(v.tensor_copy(dst[:, :].rearrange("p (f c) -> p f c", f=2), PS[0:NE, 1:3, :]))
        for i in range(self.STEPS):
            v.wait_ge(self.product, self.p_spread(i))
            v.wait_ge(self.by_a, i + 2)
            h = self.h[:, i % 8, (i // 8) * BANK:(i // 8) * BANK + BANK]
            done(v.tensor_tensor(h, h, PS[:, 1 + i % 2, :], ALU.mult))
        x = self.k.x
        for f in range(2):
            v.wait_ge(self.product, self.p_out(f))
            r = slice(4 * f, 4 * f + 4)
            v.tensor_tensor(x[:, r, :], x[:, r, :], PS[:, 4 + f, :].rearrange("p (t d) -> p t d", t=4), ALU.add)

def build(nc, a, cst_d, out):
    with ExitStack() as stack:
        k = Kit(nc, stack)
        k.PS = stack.enter_context(nc.psum_tensor("PS", [P, 8, BANK], F32))
        k.cst = k.sb("constants", [P, C_END])
        k.ident = k.cst[:, C_ID:C_ID + P]
        k.x = k.sb("x", [P, TILES, D])
        k.y = k.sb("y", [P, TILES, D])
        k.yT = k.sb("yT", [P, B * L])
        k.ctxT = k.sb("ctxT", [P, B, S2])
        k.ctxP = k.sb("ctx_by_lane", [P, S2 // 32, D])
        k.identb = k.sb("ident_bf16", [P, P], BF16)
        k.trib = k.sb("triangle_bf16", [P, P], BF16)
        k.classb = k.sb("classes_bf16", [2, P + REG], BF16)
        k.ln = LayerNorm(k)
        warm = k.sb("warm", [P, 1])
        x_in, cst_in, ctx_in, ctxP_in = k.sem("x_in"), k.sem("constants_in"), k.sem("ctx_in"), k.sem("ctx_by_lane_in")
        ctx_turned, ctx_sb, cast_done, out_done = k.sem("ctx_turned"), k.sem("ctxT_ready"), k.sem("bf16_constants_ready"), k.sem("out_done")
        l1f = NarrowAttention(k, "l1f", 3, by_class=True)
        l2f = SpikingMoE(k, 5)
        l3x = NarrowAttention(k, "l3x", 6, by_class=False)
        l3f = TopOneMoE(k, 7)
        with ExitStack() as k.local:
            l0x = WideAttention(k, "l0x", 0, causal=True, wo_by_head=False)
            l1x = WideAttention(k, "l1x", 2, causal=False, wo_by_head=True)
            group = k.local
            with ExitStack() as k.local:
                ctx_nat = k.lb("ctx_natural", [P, B * S2 // P, D])
                l0f = ShiftMix(k, 1)
            k.local = group
            l1f.place()
        with ExitStack() as k.local:
            l2x = Warping(k, 4)
        with ExitStack() as k.local:
            l3x.place()
            group = k.local
            with ExitStack() as k.local:
                l2f.place()
            k.local = group
            l3f.place()
        stack.enter_context(nc.allow_non_contiguous_dma(reason="biases of at most 1024 elements, one to a partition"))
        block = stack.enter_context(nc.Block())

        @block.sync
        def _(sp):
            sp.dma_start(k.x[:, :, :], a["x"].rearrange("b (t p) d -> p (b t) d", p=P)).then_inc(x_in, 16)
            sp.dma_start(k.cst[:, :], cst_d).then_inc(cst_in, 16)
            ctx = a["ctx_1024"]
            sp.dma_start(ctx_nat[:, :, :], ctx.rearrange("b (t p) d -> p (b t) d", p=P)).then_inc(ctx_in, 16)
            wq, wk, bq, bk = (a["L0_xattn_" + n] for n in ("Wq", "Wk", "bq", "bk"))
            l0x.load_once(sp, a["L0_xattn_Wv"], a["L0_xattn_bv"], a["L0_xattn_bo"], a["L0_xattn_Wo"], wq, wk, bq, bk)
            l0f.load(sp, *(a["L0_ffn_" + n] for n in ("W_r", "W_k", "W_v", "mu_r", "mu_k")))
            wide = lambda n: a["L1_xattn_" + n].rearrange("d n h -> d (n h)")
            bias = lambda n: a["L1_xattn_" + n].rearrange("n o h -> (n o h)")
            wq1, wk1, bq1, bk1 = wide("w_query"), wide("w_key"), bias("b_query"), bias("b_key")
            l1x.load_once(sp, wide("w_value"), bias("b_value"), a["L1_xattn_b_projection"].rearrange("o d -> (o d)"), a["L1_xattn_w_projection"],
                          wq1, wk1, bq1, bk1)
            l0x.load_rounds(sp, wq, wk, bq, bk)
            for b in range(B):
                sp.dma_start(k.ctxP[32 * b:32 * b + 32, :, :], ctx[b].rearrange("(p e) d -> e p d", e=32)).then_inc(ctxP_in, 16)
            qkv = a["L1_ffn_W_qkv"]
            l1f.load(sp, qkv[:, 0:D], qkv[:, D:2 * D], qkv[:, 2 * D:3 * D], a["L1_ffn_W_proj"], a["L1_ffn_b_proj"], g=a["L1_ffn_g_info"][0, 0])
            l3x.load(sp, *(a["L3_xattn_" + n] for n in ("Wq", "Wk", "Wv", "Wo", "bo", "bq", "bk", "bv")), mask=a["mask_BxS2_bf0"])
            l2f.load(sp, *(a["L2_ffn_" + n] for n in ("enc_W", "enc_b", "s2c_W", "s2c_b", "rW1", "rb1", "rW2", "rb2", "We1", "be1", "We2", "be2",
                                                     "c2s_W", "c2s_b", "dec_W", "dec_b", "ln_g", "ln_b")))
            l3f.load(sp, *(a["L3_ffn_" + n] for n in ("Wg", "bg", "W1", "b1", "W2", "b2")))
            l1x.load_rounds(sp, wq1, wk1, bq1, bk1)
            sp.wait_ge(k.stage_done, 4 * 12)
            sp.dma_start(out.rearrange("b (t p) d -> p (b t) d", p=P), k.x[:, :, :]).then_inc(out_done, 16)
            sp.wait_ge(out_done, 16)

        @block.gpsimd
        def _(pool):
            ln = k.ln
            pool.memset(ln.half[:, :], -0.5).then_inc(ln.s_half, 1)
            l1f.pool_zero(pool)
            l3x.pool_zero(pool)
            pool.wait_ge(cst_in, 16)
            pool.tensor_copy(k.identb[:, :], k.ident).then_inc(cast_done, 1)
            pool.tensor_copy(k.trib[:, :], k.cst[:, C_TRI:C_TRI + P]).then_inc(cast_done, 1)
            pool.tensor_copy(k.classb[:, :], k.cst[0:2, C_CLASS:C_CLASS + P + REG]).then_inc(cast_done, 1)
            pool.wait_ge(ln.s_half, 1)
            ln.pool_rstd(pool, 0)
            k.meet(pool, 0)
            ln.pool_rstd(pool, 1)
            k.meet(pool, 1)
            ln.pool_rstd(pool, 2)
            l1f.pool_pad(pool)
            k.meet(pool, 2)
            ln.pool_rstd(pool, 3)
            l1f.pool_batches(pool)
            k.meet(pool, 3)
            ln.pool_rstd(pool, 4)
            l2x.pool_before(pool)
            k.meet(pool, 4)
            l2x.pool_forward(pool)
            k.meet(pool, 5)
            pool.wait_ge(ctxP_in, 64)
            l2x.pool_split(pool)
            k.meet(pool, 6)
            k.meet(pool, 7)
            ln.pool_rstd(pool, 5)
            l2f.pool_ones(pool)
            l3x.pool_pad(pool)
            ln.pool_rstd(pool, 6)
            k.meet(pool, 8)
            ln.pool_rstd(pool, 7)
            l3x.pool_batches(pool)
            k.meet(pool, 9)
            ln.pool_rstd(pool, 8)
            k.meet(pool, 10)
            k.meet(pool, 11)

        @block.tensor
        def _(pe):
            ln = k.ln
            pe.wait_ge(cst_in, 16)
            pe.wait_ge(ctx_in, 16)
            for t in range(B * S2 // P):
                mm = pe.transpose(k.PS[:, t // 4, (t % 4) * P:(t % 4) * P + P], ctx_nat[:, t, :], k.ident)
                if t % 4 == 3:
                    mm.then_inc(ctx_turned, 1)
            ln.tensor_transpose(pe, 0, 0)
            pe.wait_ge(cast_done, 3)
            pe.wait_ge(ctx_sb, B)
            l0x.tensor(pe)
            k.meet(pe, 0)
            ln.tensor_transpose(pe, 1, 1)
            l0f.tensor(pe)
            k.meet(pe, 1)
            ln.tensor_transpose(pe, 2, 2)
            l1x.tensor(pe)
            k.meet(pe, 2)
            ln.tensor_transpose(pe, 3, 3)
            l1f.tensor_find(pe)
            l1f.tensor(pe)
            k.meet(pe, 3)
            ln.tensor_transpose(pe, 4, 4)
            l2x.tensor_distances(pe)
            k.meet(pe, 4)
            k.meet(pe, 5)
            k.meet(pe, 6)
            l2x.tensor_expand(pe)
            k.meet(pe, 7)
            ln.tensor_transpose(pe, 5, 5)
            l2f.tensor(pe)
            k.meet(pe, 8)
            ln.tensor_transpose(pe, 7, 6)
            l3x.tensor(pe)
            k.meet(pe, 9)
            ln.tensor_transpose(pe, 8, 7)
            l3f.tensor(pe)
            k.meet(pe, 10)
            k.meet(pe, 11)

        @block.scalar
        def _(act):
            ln = k.ln
            prime = ln.half[:, 0:1]
            act.wait_ge(ln.s_half, 1)
            for b in range(B):
                act.wait_ge(ctx_turned, b + 1)
                act.copy(k.ctxT[:, b, :], k.PS[:, b, :]).then_inc(ctx_sb, 1)
            ln.scalar_yT(act, 0)
            act.activation(warm[:, :], prime, ACT.Exp)
            l0x.scalar(act)
            k.meet(act, 0)
            ln.scalar_yT(act, 1)
            l0f.scalar(act)
            k.meet(act, 1)
            ln.scalar_yT(act, 2)
            act.activation(warm[:, :], prime, ACT.Exp)
            l1x.scalar(act)
            k.meet(act, 2)
            ln.scalar_yT(act, 3)
            l1f.scalar_find(act)
            act.activation(warm[:, :], prime, ACT.Exp)
            l1f.scalar(act)
            k.meet(act, 3)
            ln.scalar_yT(act, 4)
            l2x.scalar_distances(act)
            k.meet(act, 4)
            l2x.scalar_forward(act)
            k.meet(act, 5)
            l2x.scalar_backward(act)
            k.meet(act, 6)
            k.meet(act, 7)
            ln.scalar_yT(act, 5)
            l2f.scalar(act)
            k.meet(act, 8)
            ln.scalar_yT(act, 6)
            act.activation(warm[:, :], prime, ACT.Exp)
            l3x.scalar(act)
            k.meet(act, 9)
            ln.scalar_yT(act, 7)
            l3f.scalar(act)
            k.meet(act, 10)
            k.meet(act, 11)

        @block.vector
        def _(v):
            ln, x, y = k.ln, k.x, k.y
            v.wait_ge(x_in, 16)

            def norm(n, src=x):
                ln.vector_stats(v, n, src)
                ln.vector_norm(v, n, src, y)
                v.wait_ge(ln.s_y, TILES * (n + 1))

            norm(0)
            l0x.vector(v)
            k.meet(v, 0)
            norm(1)
            l0f.vector(v)
            k.meet(v, 1)
            norm(2)
            l1x.vector(v)
            k.meet(v, 2)
            norm(3)
            v.wait_ge(cst_in, 16)
            l1f.vector_find(v)
            l1f.vector(v)
            k.meet(v, 3)
            norm(4)
            v.wait_ge(ctxP_in, 64)
            l2x.vector_distances(v)
            k.meet(v, 4)
            l2x.vector_forward(v)
            k.meet(v, 5)
            l2x.vector_backward(v)
            k.meet(v, 6)
            l2x.vector_expand(v)
            k.meet(v, 7)
            norm(5)
            l2f.vector(v)
            v.wait_ge(l2f.by_a, 22)
            norm(6, y)
            l2f.vector_add(v)
            k.meet(v, 8)
            norm(7)
            l3x.vector_padding(v)
            l3x.vector(v)
            k.meet(v, 9)
            norm(8)
            l3f.vector(v)
            k.meet(v, 10)
            k.meet(v, 11)



def constants():
    import numpy as np
    c = np.zeros((P, C_END), dtype=np.float32)
    p = np.arange(P)
    c[:, C_ID:C_ID + P] = np.eye(P)
    c[:, C_TRI:C_TRI + P] = np.where(p[None, :] <= p[:, None], 0.0, -BIG)
    c[:, C_HALO] = np.where(p % 32 == 0, 0.0, BIG)
    c[:, C_START] = p % 32 == S2 // 32 - 1
    for t in range(0, TILES, QT):
        c[0:REG, C_REG + t] = 1.0
    c[:, C_IOTA:C_IOTA + 8] = np.arange(8)
    for row in range(2):
        c[row, C_CLASS + D8 + row:C_CLASS + P:32] = 1.0
    c[1, C_NEG:C_NEG + REG] = 1.0
    for h in range(HEADS8):
        own = (p // 32 == h % 4) & (p % 32 < D8 + 2)
        c[own, C_OWN + (h // 4) * HEADS8 + h] = SCALE8
        for i in range(REG):
            c[h * REG + i, C_DIAG + 32 * h:C_DIAG + 32 * h + D8] = 1.0
            c[h * REG + i, C_SUM + i] = 0.5
    c[0:2, C_ONE:C_ONE + P] = 1.0
    return c


def kernel(**inputs):
    import numpy as np
    import concourse.bacc as bacc
    from concourse.bass_utils import run_bass_kernel_spmd

    nc = bacc.Bacc("TRN2", target_bir_lowering=False, num_devices=1)
    arrays, args = {}, {}
    for name, value in inputs.items():
        a = np.ascontiguousarray(value)
        if a.dtype == np.bool_:
            a = a.view(np.uint32)
        arrays[name + "_dram"] = a
        args[name] = nc.dram_tensor(name + "_dram", a.shape, mybir.dt.from_np(a.dtype), kind="ExternalInput").ap()
    arrays["constants_dram"] = constants()
    cst = nc.dram_tensor("constants_dram", arrays["constants_dram"].shape, F32, kind="ExternalInput").ap()
    out = nc.dram_tensor("out_dram", (B, L, D), F32, kind="ExternalOutput").ap()
    build(nc, args, cst, out)
    r = run_bass_kernel_spmd(nc, [arrays], core_ids=[0])
    return r.results[0]["out_dram"]
```
